# Optimizing a Trainium2 kernel written in Bass

```python
import numpy as np
import jax
import jax.numpy as jnp

def _softmax(x, axis=-1):
    return jax.nn.softmax(x, axis=axis)

def _gelu(x):
    return jax.nn.gelu(x, approximate=True)

def _silu(x):
    return jax.nn.silu(x)

def _sigmoid(x):
    return jax.nn.sigmoid(x)

def _layernorm(x, axis=-1, eps=1e-05):
    m = jnp.mean(x, axis=axis, keepdims=True)
    v = jnp.var(x, axis=axis, keepdims=True)
    return (x - m) / jnp.sqrt(v + eps)

def _scatter_add(tgt, idx, src, axis=0):
    return tgt.at[idx].add(src)

def _segment_sum(src, seg, n):
    return jax.ops.segment_sum(src, seg, n)
kernel_name = 'mk_seq_postln_d2_jaxref_r8_80314f'

def setup_inputs(seed: int=0):
    np.random.seed(seed)
    _w = jnp.asarray

    def _L0_attn_setup():
        import jax, jax.numpy as jnp
        import numpy as np
        D_MODEL = 128
        N_HEADS = 16
        D_K = D_MODEL // N_HEADS
        MAX_POS = 64
        ATT_SPAN = MAX_POS
        B, T = (4, 128)
        SCALE_FACTOR = 3

        def _heads(y):
            b, t, _ = y.shape
            return y.reshape(b, t, N_HEADS, D_K).transpose(0, 2, 1, 3)
        key = jax.random.key(seed)
        ks = jax.random.split(key, 16)
        init = lambda k, shape: jax.random.normal(k, shape, dtype=jnp.float32) * 0.02
        inp = {'x': jax.random.normal(ks[0], (B, T, D_MODEL), dtype=jnp.float32), 'Wq': init(ks[1], (D_MODEL, D_MODEL)), 'bq': jnp.zeros((D_MODEL,), jnp.float32), 'Wk': init(ks[2], (D_MODEL, D_MODEL)), 'bk': jnp.zeros((D_MODEL,), jnp.float32), 'Wv': init(ks[3], (D_MODEL, D_MODEL)), 'bv': jnp.zeros((D_MODEL,), jnp.float32), 'Wo': init(ks[4], (D_MODEL, D_MODEL)), 'bo': jnp.zeros((D_MODEL,), jnp.float32), 'Wpk': init(ks[5], (D_MODEL, D_MODEL)), 'bpk': jnp.zeros((D_MODEL,), jnp.float32), 'Wpq': init(ks[6], (D_MODEL, D_MODEL)), 'bpq': jnp.zeros((D_MODEL,), jnp.float32), 'rel_emb': init(ks[7], (2 * ATT_SPAN, D_MODEL))}
        return inp
    _L0_attn_in = _L0_attn_setup()

    def _L0_ffn_setup():
        import jax, jax.numpy as jnp
        import numpy as np
        DIM = 128

        def _reference_tuple_inner(x, W_r, W_k, W_v, mu_r, mu_k):
            B, T, C = x.shape
            x_prev = jnp.concatenate([jnp.zeros((B, 1, C), x.dtype), x[:, :-1, :]], axis=1)
            xr = mu_r * x + (1.0 - mu_r) * x_prev
            xk = mu_k * x + (1.0 - mu_k) * x_prev
            r = jax.nn.sigmoid(jnp.einsum('btc,dc->btd', xr, W_r))
            k = jnp.einsum('btc,dc->btd', xk, W_k)
            k_act = jnp.square(jax.nn.relu(k))
            out = r * jnp.einsum('btc,dc->btd', k_act, W_v)
            new_state = x[:, -1, :]
            return (out, new_state)
        key = jax.random.key(seed)
        ks = jax.random.split(key, 6)
        B, T, C = (8, 256, DIM)
        x = jax.random.normal(ks[0], (B, T, C), dtype=jnp.float32)
        s = 1.0 / np.sqrt(C)
        W_r = jax.random.uniform(ks[1], (C, C), jnp.float32, -s, s)
        W_k = jax.random.uniform(ks[2], (C, C), jnp.float32, -s, s)
        W_v = jax.random.uniform(ks[3], (C, C), jnp.float32, -s, s)
        mu_r = jax.random.uniform(ks[4], (C,), jnp.float32)
        mu_k = jax.random.uniform(ks[5], (C,), jnp.float32)
        return {'x': x, 'W_r': W_r, 'W_k': W_k, 'W_v': W_v, 'mu_r': mu_r, 'mu_k': mu_k}
    _L0_ffn_in = _L0_ffn_setup()

    def _L1_attn_setup():
        import jax, jax.numpy as jnp
        import numpy as np
        NUM_HEADS = 16

        def _sinusoid_rel_pos(seq_len, dim):
            pos = jnp.arange(seq_len - 1, -1, -1, dtype=jnp.float32)
            inv_freq = 1.0 / 10000.0 ** (jnp.arange(0, dim, 2, dtype=jnp.float32) / dim)
            ang = pos[:, None] * inv_freq[None, :]
            return jnp.concatenate([jnp.sin(ang), jnp.cos(ang)], axis=-1)

        def _rel_shift(x):
            B, H, S, L = x.shape
            x = jnp.pad(x, ((0, 0), (0, 0), (0, 0), (1, 0)))
            x = x.reshape(B, H, L + 1, S)
            return x[:, :, 1:S + 1, :]
        key = jax.random.key(seed)
        ks = jax.random.split(key, 8)
        B, S, C = (2, 256, 128)
        Dk, Dv, H = (128, 128, NUM_HEADS)
        dk = Dk // H
        scale = 0.02
        return {'x': jax.random.normal(ks[0], (B, S, C), dtype=jnp.float32), 'Wq': jax.random.normal(ks[1], (C, Dk), dtype=jnp.float32) * scale, 'Wk': jax.random.normal(ks[2], (C, Dk), dtype=jnp.float32) * scale, 'Wv': jax.random.normal(ks[3], (C, Dv), dtype=jnp.float32) * scale, 'u': jax.random.normal(ks[4], (H, dk), dtype=jnp.float32) * scale, 'v': jax.random.normal(ks[5], (H, dk), dtype=jnp.float32) * scale, 'Wo': jax.random.normal(ks[6], (Dv, C), dtype=jnp.float32) * scale, 'bo': jnp.zeros((C,), dtype=jnp.float32)}
    _L1_attn_in = _L1_attn_setup()

    def _L1_ffn_setup():
        import jax, jax.numpy as jnp
        import numpy as np
        D_IN, D_HID = (128, 512)

        def _ternary(key, shape):
            return jax.random.randint(key, shape, -1, 2).astype(jnp.float32)

        def _tlin(x, w, s):
            return jnp.einsum('bsi,oi->bso', x, w) * s
        key = jax.random.key(seed)
        ks = jax.random.split(key, 12)
        inv = lambda fan: 1.0 / np.sqrt(fan).astype(np.float32)
        return {'x': jax.random.normal(ks[0], (4, 256, D_IN), dtype=jnp.float32), 'w1_w': _ternary(ks[1], (D_HID, D_IN)), 'w1_s': jax.random.uniform(ks[2], (D_HID,), dtype=jnp.float32) * inv(D_IN), 'w2_w': _ternary(ks[3], (D_HID, D_IN)), 'w2_s': jax.random.uniform(ks[4], (D_HID,), dtype=jnp.float32) * inv(D_IN), 'h1_w': _ternary(ks[5], (D_HID, D_HID)), 'h1_s': jax.random.uniform(ks[6], (D_HID,), dtype=jnp.float32) * inv(D_HID), 'h2_w': _ternary(ks[7], (D_HID, D_HID)), 'h2_s': jax.random.uniform(ks[8], (D_HID,), dtype=jnp.float32) * inv(D_HID), 'w3_w': _ternary(ks[9], (D_IN, D_HID)), 'w3_s': jax.random.uniform(ks[10], (D_IN,), dtype=jnp.float32) * inv(D_HID)}
    _L1_ffn_in = _L1_ffn_setup()
    _d = {'L0_attn_x': _L0_attn_in['x'], 'L0_attn_Wq': _L0_attn_in['Wq'], 'L0_attn_bq': _L0_attn_in['bq'], 'L0_attn_Wk': _L0_attn_in['Wk'], 'L0_attn_bk': _L0_attn_in['bk'], 'L0_attn_Wv': _L0_attn_in['Wv'], 'L0_attn_bv': _L0_attn_in['bv'], 'L0_attn_Wo': _L0_attn_in['Wo'], 'L0_attn_bo': _L0_attn_in['bo'], 'L0_attn_Wpk': _L0_attn_in['Wpk'], 'L0_attn_bpk': _L0_attn_in['bpk'], 'L0_attn_Wpq': _L0_attn_in['Wpq'], 'L0_attn_bpq': _L0_attn_in['bpq'], 'L0_attn_rel_emb': _L0_attn_in['rel_emb'], 'L0_ffn_W_r': _L0_ffn_in['W_r'], 'L0_ffn_W_k': _L0_ffn_in['W_k'], 'L0_ffn_W_v': _L0_ffn_in['W_v'], 'L0_ffn_mu_r': _L0_ffn_in['mu_r'], 'L0_ffn_mu_k': _L0_ffn_in['mu_k'], 'L1_attn_Wq': _L1_attn_in['Wq'], 'L1_attn_Wk': _L1_attn_in['Wk'], 'L1_attn_Wv': _L1_attn_in['Wv'], 'L1_attn_u': _L1_attn_in['u'], 'L1_attn_v': _L1_attn_in['v'], 'L1_attn_Wo': _L1_attn_in['Wo'], 'L1_attn_bo': _L1_attn_in['bo'], 'L1_ffn_w1_w': _L1_ffn_in['w1_w'], 'L1_ffn_w1_s': _L1_ffn_in['w1_s'], 'L1_ffn_w2_w': _L1_ffn_in['w2_w'], 'L1_ffn_w2_s': _L1_ffn_in['w2_s'], 'L1_ffn_h1_w': _L1_ffn_in['h1_w'], 'L1_ffn_h1_s': _L1_ffn_in['h1_s'], 'L1_ffn_h2_w': _L1_ffn_in['h2_w'], 'L1_ffn_h2_s': _L1_ffn_in['h2_s'], 'L1_ffn_w3_w': _L1_ffn_in['w3_w'], 'L1_ffn_w3_s': _L1_ffn_in['w3_s']}
    _x0 = _d['L0_attn_x']
    _d['L0_attn_x'] = jax.random.normal(jax.random.fold_in(jax.random.key(seed), 1), (8, 512, 128), dtype=_x0.dtype)
    del _x0
    return _d

def reference(L0_attn_x, L0_attn_Wq, L0_attn_bq, L0_attn_Wk, L0_attn_bk, L0_attn_Wv, L0_attn_bv, L0_attn_Wo, L0_attn_bo, L0_attn_Wpk, L0_attn_bpk, L0_attn_Wpq, L0_attn_bpq, L0_attn_rel_emb, L0_ffn_W_r, L0_ffn_W_k, L0_ffn_W_v, L0_ffn_mu_r, L0_ffn_mu_k, L1_attn_Wq, L1_attn_Wk, L1_attn_Wv, L1_attn_u, L1_attn_v, L1_attn_Wo, L1_attn_bo, L1_ffn_w1_w, L1_ffn_w1_s, L1_ffn_w2_w, L1_ffn_w2_s, L1_ffn_h1_w, L1_ffn_h1_s, L1_ffn_h2_w, L1_ffn_h2_s, L1_ffn_w3_w, L1_ffn_w3_s):

    def _L0_attn_ref(x, Wq, bq, Wk, bk, Wv, bv, Wo, bo, Wpk, bpk, Wpq, bpq, rel_emb):
        import jax, jax.numpy as jnp
        import numpy as np
        D_MODEL = 128
        N_HEADS = 16
        D_K = D_MODEL // N_HEADS
        MAX_POS = 64
        ATT_SPAN = MAX_POS
        B, T = (4, 128)
        SCALE_FACTOR = 3

        def _heads(y):
            b, t, _ = y.shape
            return y.reshape(b, t, N_HEADS, D_K).transpose(0, 2, 1, 3)
        b, t, c = x.shape
        scale = 1.0 / jnp.sqrt(jnp.asarray(D_K * SCALE_FACTOR, x.dtype))
        Q = _heads(x @ Wq.T + bq)
        K = _heads(x @ Wk.T + bk)
        V = _heads(x @ Wv.T + bv)
        rel = jnp.arange(t)[None, :] - jnp.arange(t)[:, None]
        rel_pos = jnp.clip(rel + ATT_SPAN, 0, 2 * ATT_SPAN - 1)
        p2c_pos = jnp.clip(-rel + ATT_SPAN, 0, 2 * ATT_SPAN - 1)
        scores = jnp.einsum('bhqd,bhkd->bhqk', Q, K) * scale
        pos_key = (rel_emb @ Wpk.T + bpk).reshape(2 * ATT_SPAN, N_HEADS, D_K)
        c2p = jnp.einsum('bhqd,shd->bhqs', Q, pos_key) * scale
        c2p = jnp.take_along_axis(c2p, rel_pos[None, None, :, :], axis=-1)
        pos_query = (rel_emb @ Wpq.T + bpq).reshape(2 * ATT_SPAN, N_HEADS, D_K)
        p2c = jnp.einsum('bhkd,shd->bhks', K, pos_query) * scale
        p2c = jnp.take_along_axis(p2c, p2c_pos[None, None, :, :], axis=-1)
        p2c = jnp.swapaxes(p2c, -1, -2)
        scores = scores + c2p + p2c
        probs = jax.nn.softmax(scores, axis=-1)
        ctx = jnp.einsum('bhqk,bhkd->bhqd', probs, V)
        ctx = ctx.transpose(0, 2, 1, 3).reshape(b, t, c)
        return ctx @ Wo.T + bo

    def _L0_ffn_ref(x, W_r, W_k, W_v, mu_r, mu_k):
        import jax, jax.numpy as jnp
        import numpy as np
        DIM = 128

        def _reference_tuple_inner(x, W_r, W_k, W_v, mu_r, mu_k):
            B, T, C = x.shape
            x_prev = jnp.concatenate([jnp.zeros((B, 1, C), x.dtype), x[:, :-1, :]], axis=1)
            xr = mu_r * x + (1.0 - mu_r) * x_prev
            xk = mu_k * x + (1.0 - mu_k) * x_prev
            r = jax.nn.sigmoid(jnp.einsum('btc,dc->btd', xr, W_r))
            k = jnp.einsum('btc,dc->btd', xk, W_k)
            k_act = jnp.square(jax.nn.relu(k))
            out = r * jnp.einsum('btc,dc->btd', k_act, W_v)
            new_state = x[:, -1, :]
            return (out, new_state)
        return _reference_tuple_inner(x, W_r, W_k, W_v, mu_r, mu_k)[0]

    def _L1_attn_ref(x, Wq, Wk, Wv, u, v, Wo, bo):
        import jax, jax.numpy as jnp
        import numpy as np
        NUM_HEADS = 16

        def _sinusoid_rel_pos(seq_len, dim):
            pos = jnp.arange(seq_len - 1, -1, -1, dtype=jnp.float32)
            inv_freq = 1.0 / 10000.0 ** (jnp.arange(0, dim, 2, dtype=jnp.float32) / dim)
            ang = pos[:, None] * inv_freq[None, :]
            return jnp.concatenate([jnp.sin(ang), jnp.cos(ang)], axis=-1)

        def _rel_shift(x):
            B, H, S, L = x.shape
            x = jnp.pad(x, ((0, 0), (0, 0), (0, 0), (1, 0)))
            x = x.reshape(B, H, L + 1, S)
            return x[:, :, 1:S + 1, :]
        B, S, C = x.shape
        H = NUM_HEADS
        dk = Wq.shape[1] // H
        dv = Wv.shape[1] // H
        Q = (x @ Wq).reshape(B, S, H, dk).transpose(0, 2, 1, 3)
        K = (x @ Wk).reshape(B, S, H, dk).transpose(0, 2, 1, 3)
        V = (x @ Wv).reshape(B, S, H, dv).transpose(0, 2, 1, 3)
        r = _sinusoid_rel_pos(S, dk)
        term1 = jnp.einsum('bhqd,bhkd->bhqk', Q, K)
        term2 = jnp.einsum('bhqd,kd->bhqk', Q, r)
        term3 = jnp.einsum('hd,bhkd->bhk', u, K)[:, :, None, :]
        term4 = jnp.einsum('hd,kd->hk', v, r)[None, :, None, :]
        scores = (term1 + term3 + _rel_shift(term2 + term4)) / jnp.sqrt(jnp.asarray(dk, dtype=x.dtype))
        attn = jax.nn.softmax(scores, axis=-1)
        out = jnp.einsum('bhqk,bhkd->bqhd', attn, V).reshape(B, S, H * dv)
        return out @ Wo + bo

    def _L1_ffn_ref(x, w1_w, w1_s, w2_w, w2_s, h1_w, h1_s, h2_w, h2_s, w3_w, w3_s):
        import jax, jax.numpy as jnp
        import numpy as np
        D_IN, D_HID = (128, 512)

        def _ternary(key, shape):
            return jax.random.randint(key, shape, -1, 2).astype(jnp.float32)

        def _tlin(x, w, s):
            return jnp.einsum('bsi,oi->bso', x, w) * s
        h = jax.nn.silu(_tlin(x, w1_w, w1_s)) * _tlin(x, w2_w, w2_s)
        h = jax.nn.gelu(_tlin(h, h1_w, h1_s), approximate=False)
        h = jax.nn.gelu(_tlin(h, h2_w, h2_s), approximate=False)
        return _tlin(h, w3_w, w3_s)
    x = L0_attn_x
    x = _layernorm(x + _L0_attn_ref(x, L0_attn_Wq, L0_attn_bq, L0_attn_Wk, L0_attn_bk, L0_attn_Wv, L0_attn_bv, L0_attn_Wo, L0_attn_bo, L0_attn_Wpk, L0_attn_bpk, L0_attn_Wpq, L0_attn_bpq, L0_attn_rel_emb), axis=-1)
    x = _layernorm(x + _L0_ffn_ref(x, L0_ffn_W_r, L0_ffn_W_k, L0_ffn_W_v, L0_ffn_mu_r, L0_ffn_mu_k), axis=-1)
    x = _layernorm(x + _L1_attn_ref(x, L1_attn_Wq, L1_attn_Wk, L1_attn_Wv, L1_attn_u, L1_attn_v, L1_attn_Wo, L1_attn_bo), axis=-1)
    x = _layernorm(x + _L1_ffn_ref(x, L1_ffn_w1_w, L1_ffn_w1_s, L1_ffn_w2_w, L1_ffn_w2_s, L1_ffn_h1_w, L1_ffn_h1_s, L1_ffn_h2_w, L1_ffn_h2_s, L1_ffn_w3_w, L1_ffn_w3_s), axis=-1)
    return x

_drawn_inputs = setup_inputs


def setup_inputs(seed=0):
    import zlib

    import numpy as np

    out = dict(_drawn_inputs(seed))
    spreads = {'L0_attn_bq': (0.0, 0.8),
     'L0_attn_bk': (0.0, 2.0),
     'L0_attn_bv': (0.0, 0.378),
     'L0_attn_bo': (0.0, 0.1),
     'L0_attn_bpk': (0.0, 2.0),
     'L0_attn_bpq': (0.0, 0.8),
     'L1_attn_bo': (0.0, 0.1)}
    factors = {'L0_attn_Wq': 8.0,
     'L0_attn_Wk': 8.0,
     'L0_attn_Wv': 8.0,
     'L0_attn_Wpk': 8.0,
     'L0_attn_Wpq': 8.0,
     'L0_attn_rel_emb': 8.0,
     'L0_ffn_W_r': 3.216,
     'L0_ffn_mu_r': 6.376,
     'L1_attn_Wq': 8.0,
     'L1_attn_Wk': 8.0,
     'L1_attn_Wv': 8.0,
     'L1_attn_u': 8.0,
     'L1_attn_v': 8.0,
     'L1_attn_Wo': 8.0,
     'L1_ffn_w1_w': 8.0,
     'L1_ffn_w1_s': 8.0,
     'L1_ffn_w2_w': 8.0,
     'L1_ffn_w2_s': 8.0,
     'L1_ffn_h1_w': 8.0,
     'L1_ffn_h1_s': 8.0,
     'L1_ffn_h2_w': 8.0,
     'L1_ffn_h2_s': 8.0,
     'L1_ffn_w3_w': 8.0,
     'L1_ffn_w3_s': 8.0}
    for name, (base, spread) in spreads.items():
        noise = np.random.default_rng([zlib.crc32(name.encode()), seed]).standard_normal(out[name].shape)
        drawn = base * np.exp(spread * noise) if base else spread * noise
        out[name] = jnp.asarray(drawn.astype(out[name].dtype))
    for name, factor in factors.items():
        out[name] = (out[name] * factor).astype(out[name].dtype)
    return out
```

```python
from contextlib import ExitStack

import concourse.bass as bass
from concourse import mybir

F32 = mybir.dt.float32
BF16 = mybir.dt.bfloat16
U32 = mybir.dt.uint32
ALU = mybir.AluOpType
ACT = mybir.ActivationFunctionType
AX = mybir.AxisListType

B, T, C = 8, 512, 128
H = 16
DH = C // H
NT = T // 128
NHEAD = B * H
SPAN = 64
REL = 2 * SPAN
HID = 512
KH = HID // 128
EPS = 1e-5
Q_PART = [0, 0, 0, 1, 1, 2]
K_PART = [0, 1, 2, 0, 1, 0]
NTERM = len(Q_PART)
SR = NTERM * DH
R0 = SR + 3
R1 = 2 * SR
KHI, KLO, QLO, QHI = range(4)
GROUP = 4
NG = NHEAD // GROUP
PITCH_A = SPAN + T + SPAN
PITCH_B = 3 * REL
WIN = 2 * REL
VC = DH + 1
VW = 32
BASE = 32

SCALE = {0: (3 * DH) ** -0.5, 1: DH ** -0.5}


def build(nc, t):
    top = ExitStack()
    with top:
        sems, held = {}, ExitStack()

        def sem(name):
            if name not in sems:
                sems[name] = held.enter_context(nc.semaphore(name))
            return sems[name]

        def start_phase():
            with nc.Block() as block:
                @block.sync
                def _(sp):
                    for handle in sems.values():
                        sp.sem_inc(handle, BASE)

        def end_phase():
            with nc.Block() as block:
                @block.sync
                def _(sp):
                    for handle in sems.values():
                        sp.sem_clear(handle)
            held.close()
            sems.clear()

        bank = [top.enter_context(nc.psum_tensor(f"bank{i}", [128, 512], F32)) for i in range(8)]

        def dram(name, shape, dt):
            return nc.dram_tensor(name, shape, dt, kind="Internal").ap()

        stack = {0: dram("stack0", [NHEAD, R0, 4, T], BF16), 1: dram("stack1", [NHEAD, R1, 3, T], BF16)}
        values = dram("values", [NHEAD, 128, NT, VC], F32)
        table = dram("table", [H, R0, 2 * REL], BF16)
        heads_out = dram("heads_out", [NHEAD, VW, T], F32)
        resid = dram("resid", [B, T, C], F32)
        shear_a = dram("shear_a", [4, 128, PITCH_A], F32)
        shear_b = dram("shear_b", [4, T, PITCH_B], F32)

        def tables_phase():
            with ExitStack() as ctx:
                def sb(name, shape, dt=F32):
                    return ctx.enter_context(nc.sbuf_tensor(name, shape, dt))

                wpk, wpq, relt = sb("wpk", [C, C]), sb("wpq", [C, C]), sb("relt", [C, REL])
                cols = sb("cols", [C, 4])
                sc = sb("sc", [C, 2])
                negblock = sb("negblock", [C, H])
                pk, pq = sb("pk", [C, REL]), sb("pq", [C, REL])
                d = sb("d", [C, 2, REL])
                e = sb("e", [C, REL + 1])
                e1 = sb("e1", [C, REL + 1])
                kc = sb("kc", [H, REL + T])
                parts = [sb(f"dp{i}", [C, 2, REL], BF16) for i in range(3)]
                kparts = [sb(f"kp{i}", [H, REL + T], BF16) for i in range(3)]
                rest, krest = sb("rest", [C, 2, REL]), sb("krest", [H, REL + T])
                ones, zeros = sb("ones", [SR, T], BF16), sb("zeros", [128, T], BF16)
                zf = sb("zf", [128, 3 * REL])
                bias = sb("bias", [C, 4])
                s_in, s_ps, s_pk, s_col, s_d = (sem(n) for n in ("tab_in", "tab_ps", "tab_pk", "tab_col", "tab_d"))
                s_e, s_kps, s_kc, s_part, s_out = (sem(n) for n in ("tab_e", "tab_kps", "tab_kc", "tab_part", "tab_out"))
                s_fill = sem("tab_fill")

                start_phase()
                with nc.Block() as block:
                    @block.sync
                    def _(sp):
                        for dst, src in ((wpk, t["WpkT"]), (wpq, t["WpqT"]), (relt, t["relT"]), (negblock, t["negblock"])):
                            sp.dma_start(dst[:, :], src).then_inc(s_in, 16)
                        for i, n in enumerate(("bq", "bk", "bpk", "bpq")):
                            sp.dma_start(cols[:, i:i + 1], t[n]).then_inc(s_in, 16)
                        sp.wait_ge(s_fill, BASE + 3)
                        for i in range(4):
                            for at in (0, SPAN + T):
                                sp.dma_start(shear_a[i, :, at:at + SPAN], zf[:, 0:SPAN]).then_inc(s_out, 16)
                            for at in (0, 2 * REL):
                                for n in range(NT):
                                    sp.dma_start(shear_b[i, n * 128:(n + 1) * 128, at:at + REL], zf[:, 0:REL]).then_inc(s_out, 16)
                        sp.wait_ge(s_part, BASE + 1)
                        for j in range(NTERM):
                            rows = slice(DH * j, DH * j + DH)
                            sp.dma_start(table[:, rows, 0:REL], parts[Q_PART[j]][:, 0, :]).then_inc(s_out, 16)
                            sp.dma_start(table[:, rows, REL:2 * REL], parts[K_PART[j]][:, 1, :]).then_inc(s_out, 16)
                        for i in range(3):
                            sp.dma_start(table[:, SR + i, 0:REL], kparts[i][:, 0:REL]).then_inc(s_out, 16)
                            sp.dma_start(table[:, SR + i, REL:2 * REL], zeros[0:H, 0:REL]).then_inc(s_out, 16)
                        for b in range(B):
                            own = slice(b * H, b * H + H)
                            sp.dma_start(stack[0][own, SR:R0, KLO, :], ones[:, :]).then_inc(s_out, 16)
                            sp.dma_start(stack[0][own, SR:R0, KHI, :], ones[:, :]).then_inc(s_out, 16)
                            sp.dma_start(stack[0][own, SR:R0, QLO, :], zeros[0:SR, :]).then_inc(s_out, 16)
                            for i in range(3):
                                sp.dma_start(stack[0][own, SR + i, QHI, :], kparts[i][:, REL:REL + T]).then_inc(s_out, 16)
                        n_out = 4 * (2 + 2 * NT) + 2 * NTERM + 6 + 6 * B
                        sp.wait_ge(s_out, BASE + 16 * n_out)

                    @block.tensor
                    def _(pe):
                        pe.wait_ge(s_in, BASE + 16 * 8)
                        pe.matmul(bank[0][:, 0:REL], wpk[:, :], relt[:, :], start=True, stop=True).then_inc(s_ps, 1)
                        pe.matmul(bank[1][:, 0:REL], wpq[:, :], relt[:, :], start=True, stop=True).then_inc(s_ps, 1)
                        pe.wait_ge(s_e, BASE + 4)
                        pe.matmul(bank[2][0:H, 0:REL + 1], negblock[:, :], e[:, :], start=True, stop=True).then_inc(s_kps, 1)

                    @block.scalar
                    def _(act):
                        act.wait_ge(s_in, BASE + 16 * 8)
                        nc.scalar.activation(sc[:, 0:1], cols[:, 0:1], ACT.Identity, scale=SCALE[0]).then_inc(s_col, 1)
                        nc.scalar.activation(sc[:, 1:2], cols[:, 3:4], ACT.Identity, scale=SCALE[0]).then_inc(s_col, 1)
                        act.wait_ge(s_ps, BASE + 2)
                        nc.scalar.activation(pk[:, :], bank[0][:, 0:REL], ACT.Identity, bias=cols[:, 2:3]).then_inc(s_pk, 1)
                        act.wait_ge(s_col, BASE + 2)
                        nc.scalar.activation(pq[:, :], bank[1][:, 0:REL], ACT.Identity, bias=sc[:, 1:2], scale=SCALE[0]).then_inc(s_pk, 1)

                    @block.vector
                    def _(v):
                        last = REL - 1
                        v.memset(ones[:, :], 1.0).then_inc(s_fill, 1)
                        v.memset(zeros[:, :], 0.0).then_inc(s_fill, 1)
                        v.memset(zf[:, :], 0.0).then_inc(s_fill, 1)
                        v.wait_ge(s_pk, BASE + 2)
                        v.tensor_tensor(bias[:, QLO:QLO + 1], sc[:, 0:1], pq[:, 0:1], ALU.add).then_inc(s_d, 1)
                        v.tensor_tensor(bias[:, QHI:QHI + 1], sc[:, 0:1], pq[:, last:REL], ALU.add).then_inc(s_d, 1)
                        v.tensor_tensor(bias[:, KLO:KLO + 1], cols[:, 1:2], pk[:, 0:1], ALU.add).then_inc(s_d, 1)
                        v.tensor_tensor(bias[:, KHI:KHI + 1], cols[:, 1:2], pk[:, last:REL], ALU.add).then_inc(s_d, 1)
                        v.tensor_scalar(d[:, 0, :], pq[:, :], pq[:, 0:1], None, ALU.subtract).then_inc(s_d, 1)
                        v.tensor_scalar(d[:, 1, :], pk[:, :], pk[:, 0:1], None, ALU.subtract).then_inc(s_d, 1)
                        v.wait_ge(s_d, BASE + 6)
                        v.tensor_scalar(e1[:, 0:REL], d[:, 1, :], pq[:, 0:1], None, ALU.mult).then_inc(s_e, 1)
                        v.tensor_tensor(e1[:, REL:REL + 1], pq[:, 0:1], pk[:, 0:1], ALU.mult).then_inc(s_e, 1)
                        v.wait_ge(s_e, BASE + 2)
                        v.scalar_tensor_tensor(out=e[:, 0:REL], in0=d[:, 0, :], scalar=pk[:, 0:1], in1=e1[:, 0:REL],
                                               op0=ALU.mult, op1=ALU.add).then_inc(s_e, 1)
                        v.scalar_tensor_tensor(out=e[:, REL:REL + 1], in0=pq[:, last:REL], scalar=pk[:, last:REL],
                                               in1=e1[:, REL:REL + 1], op0=ALU.mult, op1=ALU.subtract).then_inc(s_e, 1)
                        v.wait_ge(s_kps, BASE + 1)
                        v.tensor_copy(kc[:, 0:REL], bank[2][0:H, 0:REL]).then_inc(s_kc, 1)
                        v.tensor_scalar(kc[:, REL:REL + T], zeros[0:H, :], bank[2][0:H, REL:REL + 1], None, ALU.add).then_inc(s_kc, 1)
                        v.wait_ge(s_kc, BASE + 2)
                        v.tensor_copy(parts[0][:, :, :], d[:, :, :]).then_inc(s_kc, 1)
                        v.tensor_copy(kparts[0][:, :], kc[:, :]).then_inc(s_kc, 1)
                        v.wait_ge(s_kc, BASE + 4)
                        v.tensor_tensor(rest[:, :, :], d[:, :, :], parts[0][:, :, :], ALU.subtract).then_inc(s_kc, 1)
                        v.tensor_tensor(krest[:, :], kc[:, :], kparts[0][:, :], ALU.subtract).then_inc(s_kc, 1)
                        v.wait_ge(s_kc, BASE + 6)
                        v.tensor_copy(parts[1][:, :, :], rest[:, :, :]).then_inc(s_kc, 1)
                        v.tensor_copy(kparts[1][:, :], krest[:, :]).then_inc(s_kc, 1)
                        v.wait_ge(s_kc, BASE + 8)
                        v.tensor_tensor(parts[2][:, :, :], rest[:, :, :], parts[1][:, :, :], ALU.subtract)
                        v.tensor_tensor(kparts[2][:, :], krest[:, :], kparts[1][:, :], ALU.subtract).then_inc(s_part, 1)

                wq, wk, wv = sb("wq", [C, C]), sb("wk", [C, C]), sb("wv", [C, C])
                bv = sb("bv", [128, C])
                xt = sb("xt", [C, T])
                full = sb("full", [C, 4, T])
                part = [sb(f"part{i}", [C, 4, T], BF16) for i in range(3)]
                left = sb("left", [C, 4, T])
                vt = sb("vt", [128, H, NT, VC])
                n_out = 2 * NTERM + 1
                end_phase()
                w_in, x_in, p_ps, v_ps = sem("p0_w"), sem("p0_x"), sem("p0_ps"), sem("p0_vps")
                p_full, p_hi, p_rest, p_mid, p_lo = (sem(n) for n in ("p0_full", "p0_hi", "p0_rest", "p0_mid", "p0_lo"))
                p_v, p_vone, p_out, held_off = sem("p0_v"), sem("p0_vone"), sem("p0_out"), sem("held_off")
                start_phase()
                with nc.Block() as block:
                    @block.sync
                    def _(sp):
                        for dst, src in ((wq, t["WqT"]), (wk, t["WkT"]), (wv, t["WvT"])):
                            sp.dma_start(dst[:, :], src).then_inc(w_in, 16)
                        sp.dma_start(bv[:, :], t["bv"].partition_broadcast(128)).then_inc(w_in, 16)
                        with sp.Fori(0, B) as b:
                            sp.wait_ge(p_ps, BASE + 2 * b)
                            sp.sem_inc(held_off, 1)
                            sp.wait_ge(v_ps, BASE + b)
                            sp.sem_inc(held_off, 1)
                            sp.dma_start(xt[:, :], t["xT"][b]).then_inc(x_in, 16)
                            sp.wait_ge(p_lo, BASE + b + 1)
                            sp.sem_inc(held_off, 1)
                            own = bass.ts(b, H)
                            for j in range(NTERM):
                                rows = slice(DH * j, DH * j + DH)
                                sp.dma_start(stack[0][own, rows, KHI:KLO + 1, :], part[K_PART[j]][:, KHI:KLO + 1, :]).then_inc(p_out, 16)
                                sp.dma_start(stack[0][own, rows, QLO:QHI + 1, :], part[Q_PART[j]][:, QLO:QHI + 1, :]).then_inc(p_out, 16)
                            sp.wait_ge(p_v, BASE + b + 1)
                            sp.sem_inc(held_off, 1)
                            sp.dma_start(values[own].rearrange("h p n c -> p h n c"), vt[:, :, :, :]).then_inc(p_out, 16)
                        sp.wait_ge(p_out, BASE + 16 * n_out * B)

                    @block.tensor
                    def _(pe):
                        pe.wait_ge(w_in, BASE + 16 * 4)
                        with pe.Fori(0, B) as b:
                            pe.wait_ge(x_in, BASE + 16 * b + 16)
                            pe.wait_ge(p_full, BASE + b)
                            pe.wait_ge(p_v, BASE + b)
                            pe.matmul(bank[0][:, :], wq[:, :], xt[:, :], start=True, stop=True).then_inc(p_ps, 1)
                            pe.matmul(bank[1][:, :], wk[:, :], xt[:, :], start=True, stop=True).then_inc(p_ps, 1)
                            for n in range(NT):
                                last = pe.matmul(bank[2][:, n * 128:(n + 1) * 128], xt[:, n * 128:(n + 1) * 128], wv[:, :],
                                                 start=True, stop=True)
                            last.then_inc(v_ps, 1)

                    @block.scalar
                    def _(act):
                        with act.Fori(0, B) as b:
                            act.wait_ge(p_ps, BASE + 2 * b + 2)
                            act.wait_ge(p_lo, BASE + b)
                            for arr, src, scale in ((QLO, 0, SCALE[0]), (QHI, 0, SCALE[0]), (KLO, 1, 1.0), (KHI, 1, 1.0)):
                                last = nc.scalar.activation(full[:, arr, :], bank[src][:, :], ACT.Identity,
                                                            bias=bias[:, arr:arr + 1], scale=scale)
                            last.then_inc(p_full, 1)
                            act.wait_ge(p_full, BASE + b + 1)
                            act.wait_ge(p_out, BASE + 16 * n_out * b)
                            nc.scalar.copy(part[0][:, :, :], full[:, :, :]).then_inc(p_hi, 1)

                    @block.vector
                    def _(v):
                        v.memset(vt[:, :, :, DH:VC], 1.0).then_inc(p_vone, 1)
                        v.wait_ge(p_vone, BASE + 1)
                        v.wait_ge(w_in, BASE + 16 * 4)
                        with v.Fori(0, B) as b:
                            v.wait_ge(v_ps, BASE + b + 1)
                            v.wait_ge(p_out, BASE + 16 * n_out * b)
                            for n in range(NT):
                                last = v.tensor_tensor(vt[:, :, n, 0:DH],
                                                       bank[2][:, n * 128:(n + 1) * 128].rearrange("p (h d) -> p h d", d=DH),
                                                       bv[:, :].rearrange("p (h d) -> p h d", d=DH), ALU.add)
                            last.then_inc(p_v, 1)
                            v.wait_ge(p_hi, BASE + b + 1)
                            v.tensor_tensor(left[:, :, :], full[:, :, :], part[0][:, :, :], ALU.subtract).then_inc(p_rest, 1)
                            v.wait_ge(p_rest, BASE + b + 1)
                            v.tensor_copy(part[1][:, :, :], left[:, :, :]).then_inc(p_mid, 1)
                            v.wait_ge(p_mid, BASE + b + 1)
                            v.tensor_tensor(part[2][:, :, :], left[:, :, :], part[1][:, :, :], ALU.subtract).then_inc(p_lo, 1)

        def attention_phase(layer):
            rel = layer == 0
            with ExitStack() as ctx:
                def sb(name, shape, dt=F32):
                    return ctx.enter_context(nc.sbuf_tensor(f"a{layer}_{name}", shape, dt))

                def s(name):
                    return sem(f"a{layer}_{name}")

                rows = R0 if rel else R1
                stk = [sb(f"stk{i}", [rows, 4, T], BF16) for i in range(4)]
                vs = [sb(f"vs{i}", [128, NT, VW]) for i in range(4)]
                prob = [sb(f"prob{i}", [128, NT, T]) for i in range(2)]
                probt = [sb(f"probt{i}", [128, T]) for i in range(2)]
                negmax = [sb(f"negmax{i}", [128, NT]) for i in range(2)]
                ident = sb("ident", [128, 128])
                mask = sb("mask", [128, 128], U32)
                outs = sb("outs", [128, T])
                if rel:
                    rst = [sb(f"rst{i}", [R0, 2, T], BF16) for i in range(4)]
                    tab = [sb(f"tab{i}", [R0, 2 * REL], BF16) for i in range(4)]
                    keyside = [sb(f"keyside{i}", [128, T]) for i in range(2)]
                    sheared = [sb(f"sheared{i}", [128, T]) for i in range(2)]
                    corr = [sb(f"corr{i}", [128, NT, REL]) for i in range(2)]
                    band = [sb(f"band{i}", [128, NT, WIN]) for i in range(2)]
                score = bank[0:4]
                other, rbank, tbank, cbank = bank[4:8]

                s_const, s_pad, held_off = s("const"), s("pad"), s("held_off")
                stk_in = [s(f"stk_in{i}") for i in range(4)]
                v_in = [s(f"v_in{i}") for i in range(4)]
                score_mm, fixed, mid_fixed, added, maxed, exped = (s(n) for n in ("score_mm", "fixed", "mid_fixed", "added", "maxed", "exped"))
                turned, copied, pv_mm, out_copied, out_written = (s(n) for n in ("turned", "copied", "pv_mm", "out_copied", "out_written"))
                if rel:
                    rst_in = [s(f"rst_in{i}") for i in range(4)]
                    key_mm, key_copied, a_written, corr_mm, corr_copied, b_written = (
                        s(n) for n in ("key_mm", "key_copied", "a_written", "corr_mm", "corr_copied", "b_written"))
                    sheared_in = [s(f"sheared_in{i}") for i in range(2)]
                    band_in = [s(f"band_in{i}") for i in range(2)]

                poskey_in = s("poskey_in")

                def cut(n):
                    return min(T, 128 * n + (REL + SPAN if rel else 128))

                def fix_cols(n):
                    a = 128 * n + (SPAN if rel else 0)
                    return a, min(T, a + 128)

                def mid_cols(n):
                    return 128 * n + 1, min(T, 128 * n + 129)

                def win_cols(n):
                    a, e = 128 * n - SPAN, 128 * n - SPAN + WIN
                    return max(a, 0), min(e, T), max(a, 0) - a

                def hold(sp, event, value):
                    sp.wait_ge(event, BASE + value)
                    sp.sem_inc(held_off, 1)

                def head_loads(sp, i, j):
                    m = GROUP * i + j
                    if rel:
                        sp.dma_start(stk[j][:, :, :], stack[0][m]).then_inc(stk_in[j], 16)
                    else:
                        sp.dma_start(stk[j][0:SR, KLO:QHI + 1, :], stack[1][m, 0:SR]).then_inc(stk_in[j], 16)
                        sp.dma_start(stk[j][SR:R1, QLO:QHI + 1, :], stack[1][m, SR:R1, 1:3, :]).then_inc(stk_in[j], 16)
                    sp.dma_start(vs[j][:, :, 0:VC], values[m]).then_inc(v_in[j], 16)

                per_stk = 16 if rel else 32

                def rel_loads(sp, i, j):
                    m = GROUP * i + j
                    sp.dma_start(rst[j][:, :, :], stack[0][m, :, KLO:QLO + 1, :]).then_inc(rst_in[j], 16)
                    sp.dma_start(tab[j][:, :], table[m % H]).then_inc(rst_in[j], 16)

                def shear_a_step(sp, r, j):
                    hold(sp, key_copied, r + 1)
                    sp.dma_start(shear_a[j % 2, :, SPAN:SPAN + T], keyside[j % 2][:, :]).then_inc(a_written, 16)
                    hold(sp, a_written, 16 * (r + 1))
                    skew = bass.AP(shear_a.tensor, (j % 2) * 128 * PITCH_A, [[PITCH_A + 1, 128], [1, T]])
                    sp.dma_start(sheared[j % 2][:, :], skew).then_inc(sheared_in[j % 2], 16)

                def shear_b_write(sp, r, j):
                    hold(sp, corr_copied, r + 1)
                    dst = shear_b[j].rearrange("(n p) c -> p n c", p=128)[:, :, REL:2 * REL]
                    sp.dma_start(dst, corr[j % 2][:, :, :]).then_inc(b_written, 16)

                def shear_b_read(sp, r, j):
                    hold(sp, b_written, 16 * (r + 1))
                    skew = bass.AP(shear_b.tensor, j * T * PITCH_B + REL,
                                   [[PITCH_B - 1, 128], [128 * PITCH_B, NT], [1, WIN]])
                    sp.dma_start(band[j % 2][:, :, :], skew).then_inc(band_in[j % 2], 16)

                def out_store(sp, i):
                    hold(sp, out_copied, i + 1)
                    sp.dma_start(heads_out[bass.ts(i, GROUP)],
                                 outs[:, :]).then_inc(out_written, 16)

                def sync_step(sp, i, j, more_rel, more_heads):
                    n = GROUP * i + j
                    if rel and more_rel:
                        hold(sp, corr_mm, n + 1)
                        rel_loads(sp, i + 1, j)
                    if rel and more_heads > 1:
                        shear_b_write(sp, n + 2, (j + 2) % 4)
                    if more_heads > 1:
                        hold(sp, pv_mm, 4 * (n - 1))
                        head_loads(sp, i + (j + 2) // 4, (j + 2) % 4)
                    if rel and more_heads > 1:
                        hold(sp, added, 4 * (n + 1))
                        shear_b_read(sp, n + 2, (j + 2) % 4)
                    if rel and more_rel:
                        shear_a_step(sp, n + 4, j)

                start_phase()
                with nc.Block() as block:
                    @block.sync
                    def _(sp):
                        sp.dma_start(ident[:, :], t["ident"]).then_inc(s_const, 16)
                        sp.dma_start(mask[:, :], t[f"mask{layer}"]).then_inc(s_const, 16)
                        if not rel:
                            for i in range(4):
                                for j in range(NTERM):
                                    sp.dma_start(stk[i][SR + DH * j:SR + DH * j + DH, KLO, :],
                                                 t["poskey"][K_PART[j]]).then_inc(poskey_in, 16)
                        sp.wait_ge(s_pad, BASE + 4)
                        if rel:
                            for j in range(4):
                                rel_loads(sp, 0, j)
                        head_loads(sp, 0, 0)
                        head_loads(sp, 0, 1)
                        if rel:
                            shear_a_step(sp, 0, 0)
                            shear_a_step(sp, 1, 1)
                            shear_b_write(sp, 0, 0)
                            shear_b_read(sp, 0, 0)
                            hold(sp, corr_mm, 1)
                            shear_a_step(sp, 2, 2)
                            shear_b_write(sp, 1, 1)
                            shear_b_read(sp, 1, 1)
                            hold(sp, corr_mm, 2)
                            shear_a_step(sp, 3, 3)
                        with sp.Fori(0, NG - 1) as i:
                            for j in range(GROUP):
                                sync_step(sp, i, j, True, 2)
                                if j == 3:
                                    out_store(sp, i)
                        for j in range(GROUP):
                            sync_step(sp, NG - 1, j, False, 3 - j)
                        out_store(sp, NG - 1)
                        sp.wait_ge(out_written, BASE + 16 * NG)

                    def score_tile(pe, i, j, n):
                        m = GROUP * i + j
                        q = slice(128 * n, 128 * n + 128)
                        c = cut(n)
                        if n == 0:
                            pe.wait_ge(stk_in[j], BASE + per_stk * (i + 1))
                        pe.wait_ge(exped, BASE + 4 * m - 4 + n + 1)
                        lo = SR if rel else R1
                        pe.matmul(score[n][:, 0:c], stk[j][0:lo, QLO, q], stk[j][0:lo, KLO, 0:c], start=True, stop=True)
                        khi = KHI if rel else KLO
                        if c < T:
                            pe.matmul(score[n][:, c:T], stk[j][:, QHI, q], stk[j][:, khi, c:T], start=True, stop=True)
                        pe.wait_ge(fixed, BASE + 4 * m + n)
                        if not rel:
                            pe.wait_ge(mid_fixed, BASE + 4 * m + n)
                        a, e = fix_cols(n)
                        last = pe.matmul(other[:, 0:e - a], stk[j][:, QHI, q], stk[j][:, khi, a:e], start=True, stop=True)
                        if not rel:
                            a, e = mid_cols(n)
                            last = pe.matmul(other[:, 128:128 + e - a], stk[j][0:SR, QLO, q], stk[j][0:SR, KLO, a:e],
                                             start=True, stop=True)
                        last.then_inc(score_mm, 1)

                    def turn(pe, i, j, k):
                        m = GROUP * i + j
                        if k == 0:
                            pe.wait_ge(exped, BASE + 4 * m + 4)
                        pe.wait_ge(copied, BASE + 4 * m + k)
                        for n in range(NT):
                            last = pe.transpose(tbank[:, n * 128:(n + 1) * 128], prob[j % 2][:, n, k * 128:(k + 1) * 128], ident[:, :])
                        last.then_inc(turned, 1)

                    def weigh(pe, i, j, k):
                        m = GROUP * i + j
                        if k == 0:
                            pe.wait_ge(v_in[j], BASE + 16 * (i + 1))
                            if j == 0:
                                pe.wait_ge(out_copied, BASE + i)
                        pe.wait_ge(copied, BASE + 4 * m + k + 1)
                        pe.matmul(cbank[32 * j:32 * j + VW, :], vs[j][:, k, :], probt[k % 2][:, :],
                                  start=(k == 0), stop=(k == NT - 1)).then_inc(pv_mm, 1)

                    def key_side(pe, i, j, corrs):
                        pe.wait_ge(rst_in[j], BASE + 32 * (i + 1))
                        pe.wait_ge(key_copied, BASE + GROUP * i + j)
                        pe.wait_ge(corr_copied, BASE + corrs)
                        pe.matmul(rbank[:, :], tab[j][:, 0:REL], rst[j][:, 0, :], start=True, stop=True).then_inc(key_mm, 1)

                    def correction(pe, i, j, keys):
                        m = GROUP * i + j
                        pe.wait_ge(sheared_in[j % 2], BASE + 16 * (2 * i + j // 2 + 1))
                        pe.wait_ge(key_copied, BASE + keys)
                        pe.wait_ge(corr_copied, BASE + m)
                        for n in range(NT):
                            q = slice(128 * n, 128 * n + 128)
                            pe.matmul(rbank[:, q], sheared[j % 2][:, q], ident[:, :], start=True, stop=False)
                            last = pe.matmul(rbank[:, q], rst[j][0:SR, 1, q], tab[j][0:SR, REL:2 * REL], start=False, stop=True)
                        last.then_inc(corr_mm, 1)

                    def tensor_step(pe, i, j, more_rel, more_heads):
                        nxt = (i + (j + 1) // 4, (j + 1) % 4)
                        n = GROUP * i + j
                        for k in range(NT):
                            if more_heads:
                                score_tile(pe, nxt[0], nxt[1], k)
                            turn(pe, i, j, k)
                            if k:
                                weigh(pe, i, j, k - 1)
                            if rel and k == 1 and (more_rel or j == 0):
                                correction(pe, i + (j + 3) // 4, (j + 3) % 4, n + 4)
                            if rel and k == 2 and more_rel:
                                key_side(pe, i + 1, j, n + 4)
                        weigh(pe, i, j, NT - 1)

                    @block.tensor
                    def _(pe):
                        pe.wait_ge(s_pad, BASE + 4)
                        pe.wait_ge(s_const, BASE + 32)
                        if not rel:
                            pe.wait_ge(poskey_in, BASE + 16 * 4 * NTERM)
                        if rel:
                            key_side(pe, 0, 0, 0)
                            key_side(pe, 0, 1, 0)
                            correction(pe, 0, 0, 2)
                            key_side(pe, 0, 2, 1)
                            correction(pe, 0, 1, 3)
                            key_side(pe, 0, 3, 2)
                            correction(pe, 0, 2, 4)
                        for n in range(NT):
                            score_tile(pe, 0, 0, n)
                        with pe.Fori(0, NG - 1) as i:
                            for j in range(GROUP):
                                tensor_step(pe, i, j, True, True)
                        for j in range(GROUP):
                            tensor_step(pe, NG - 1, j, False, j < 3)

                    def fix(v, i, j, n):
                        m = GROUP * i + j
                        v.wait_ge(score_mm, BASE + 4 * m + n + 1)
                        a, e = fix_cols(n)
                        v.sem_inc(held_off, 1)
                        v.copy_predicated(score[n][:, a:e], mask[:, 0:e - a], other[:, 0:e - a]).then_inc(fixed, 1)
                        v.wait_ge(fixed, BASE + 4 * m + n + 1)
                        if rel:
                            if n == 0:
                                v.wait_ge(band_in[j % 2], BASE + 16 * (2 * i + j // 2 + 1))
                            a, e, w = win_cols(n)
                            v.tensor_tensor(score[n][:, a:e], score[n][:, a:e], band[j % 2][:, n, w:w + e - a], ALU.add).then_inc(added, 1)
                            v.wait_ge(added, BASE + 4 * m + n + 1)
                        else:
                            a, e = mid_cols(n)
                            v.sem_inc(held_off, 1)
                            v.copy_predicated(score[n][:, a:e], ident[:, 0:e - a].bitcast(U32), other[:, 128:128 + e - a]).then_inc(mid_fixed, 1)
                            v.wait_ge(mid_fixed, BASE + 4 * m + n + 1)
                        v.tensor_reduce(negmax[j % 2][:, n:n + 1], score[n][:, :], AX.X, ALU.max, negate=True).then_inc(maxed, 1)

                    def key_out(v, i, j):
                        m = GROUP * i + j
                        v.wait_ge(key_mm, BASE + m + 1)
                        v.wait_ge(a_written, BASE + 16 * (m - 1))
                        v.tensor_copy(keyside[j % 2][:, :], rbank[:, :]).then_inc(key_copied, 1)

                    @block.vector
                    def _(v):
                        for i in range(4):
                            v.memset(vs[i][:, :, :], 0.0).then_inc(s_pad, 1)
                        v.wait_ge(s_const, BASE + 32)
                        if rel:
                            for j in range(4):
                                key_out(v, 0, j)
                        for n in range(NT):
                            fix(v, 0, 0, n)

                        def vector_step(i, j, more_rel, more_heads):
                            for k in range(NT):
                                if more_heads:
                                    fix(v, i + (j + 1) // 4, (j + 1) % 4, k)
                                if rel and k == 2 and more_rel:
                                    key_out(v, i + 1, j)

                        with v.Fori(0, NG - 1) as i:
                            for j in range(GROUP):
                                vector_step(i, j, True, True)
                        for j in range(GROUP):
                            vector_step(NG - 1, j, False, j < 3)

                    def exp_tile(act, i, j, n):
                        m = GROUP * i + j
                        act.wait_ge(maxed, BASE + 4 * m + n + 1)
                        if n == 0:
                            act.wait_ge(turned, BASE + 4 * (m - 1))
                        nc.scalar.activation(prob[j % 2][:, n, :], score[n][:, :], ACT.Exp,
                                             bias=negmax[j % 2][:, n:n + 1]).then_inc(exped, 1)

                    def copy_turned(act, i, j, k):
                        m = GROUP * i + j
                        act.wait_ge(turned, BASE + 4 * m + k + 1)
                        act.wait_ge(pv_mm, BASE + 4 * m + k - 1)
                        nc.scalar.copy(probt[k % 2][:, :], tbank[:, :]).then_inc(copied, 1)

                    def corr_out(act, i, j):
                        m = GROUP * i + j
                        act.wait_ge(corr_mm, BASE + m + 1)
                        act.wait_ge(b_written, BASE + 16 * (m - 1))
                        nc.scalar.copy(corr[j % 2][:, :, :], rbank[:, :].rearrange("p (n r) -> p n r", n=NT)).then_inc(corr_copied, 1)

                    @block.scalar
                    def _(act):
                        if rel:
                            for j in range(3):
                                corr_out(act, 0, j)
                        for n in range(NT):
                            exp_tile(act, 0, 0, n)

                        def scalar_step(i, j, more_rel, more_heads):
                            for k in range(NT):
                                copy_turned(act, i, j, k)
                                if more_heads:
                                    exp_tile(act, i + (j + 1) // 4, (j + 1) % 4, k)
                                if rel and k == 1 and (more_rel or j == 0):
                                    corr_out(act, i + (j + 3) // 4, (j + 3) % 4)
                            if j == 3:
                                act.wait_ge(pv_mm, BASE + 4 * GROUP * (i + 1))
                                act.wait_ge(out_written, BASE + 16 * i)
                                nc.scalar.copy(outs[:, :], cbank[:, :]).then_inc(out_copied, 1)

                        with act.Fori(0, NG - 1) as i:
                            for j in range(GROUP):
                                scalar_step(i, j, True, True)
                        for j in range(GROUP):
                            scalar_step(NG - 1, j, False, j < 3)

        def dense_phase(layer):
            first = layer == 0
            with ExitStack() as ctx:
                def sb(name, shape, dt=F32):
                    return ctx.enter_context(nc.sbuf_tensor(f"d{layer}_{name}", shape, dt))

                def s(name):
                    return sem(f"d{layer}_{name}")

                loads = []

                def const(name, shape, src, dt=F32):
                    tile = sb(name, shape, dt)
                    loads.append((tile, src))
                    return tile

                ident = const("ident", [128, 128], t["ident"])
                wo = const("wo", [C, C], t["WoT"] if first else t["Wo"])
                bo = const("bo", [128, C], (t["bo"] if first else t["bo1"]).partition_broadcast(128))
                if first:
                    w_r, w_k, w_v = (const(n, [C, C], t[n]) for n in ("W_rT", "W_kT", "W_vT"))
                    mu = const("mu", [C, 2], t["mu"])
                    wq, wqs, wk, wv = (const(n, [C, C], t[n]) for n in ("Wq", "Wq_swap", "Wk", "Wv"))
                    uv = const("uv", [C, 3], t["uv"])
                    trig = const("trig", [C, 4, T], t["trig"])
                    uvs = sb("uvs", [C, 3])
                    xt1 = sb("xt1", [C, 1 + T])
                    delta, xr, xk = sb("delta", [C, T]), sb("xr", [C, T]), sb("xk", [C, T])
                    kr, kact, gate = sb("kr", [C, T]), sb("kact", [C, T]), sb("gate", [128, NT, C])
                    x2 = sb("x2", [128, NT, C])
                    xt2 = sb("xt2", [C, T])
                    full = sb("full", [C, 4, T])
                    qv = sb("qv", [C, 2, T])
                    rot = sb("rot", [C, 4, T])
                    left = sb("left", [C, 4, T])
                    part = [sb(f"part{i}", [C, 4 * T + 2], BF16) for i in range(3)]
                    vt = sb("vt", [128, H, NT, VC])
                else:
                    w1, w2 = (const(n, [C, HID], t[n]) for n in ("w1T", "w2T"))
                    h1, h2 = (const(n, [128, KH, HID], t[n].rearrange("(k p) o -> p k o", p=128)) for n in ("h1T", "h2T"))
                    w3 = const("w3", [128, KH, C], t["w3T"].rearrange("(k p) o -> p k o", p=128))
                    fs = const("fs", [128, 4, KH], t["hid_s"])
                    s3 = const("s3", [128, C], t["w3_s"].partition_broadcast(128))
                    xt1 = sb("xt1", [C, 1 + T])
                    silu, ha, hb, hc = (sb(n, [128, KH, T]) for n in ("silu", "ha", "hb", "hc"))
                    x2 = sb("x2", [128, NT, C])
                head_t, sums, head_n = sb("head_t", [C, T]), sb("sums", [C, T]), sb("head_n", [C, T])
                xin, xb, pre, x1 = (sb(n, [128, NT, C]) for n in ("xin", "xb", "pre", "x1"))
                stats, mv = sb("stats", [128, NT, 6]), sb("mv", [128, NT, 2])
                veps, rstd, half = sb("veps", [128, NT]), sb("rstd", [128, NT]), sb("half", [128, NT])
                drop = sb("drop", [128, NT, C])

                c_in, ready, held_off = s("c_in"), s("ready"), s("held_off")
                e = {n: s(n) for n in (
                    "x_in", "head_in", "recip", "normed", "out_mm", "biased", "summed",
                    "st1", "mv1", "ve1", "rs1", "x1", "tr1", "xt1", "f_stored",
                    "st2", "mv2", "ve2", "rs2", "x2", "gated", "added")}
                if first:
                    e |= {n: s(n) for n in ("delta", "mixed", "k_mm", "r_mm", "kr", "kact", "sig", "kv_mm", "tr2", "xt2",
                                            "qk_mm", "v_mm", "qk", "r1", "r2", "rot", "hi", "left", "mid", "lo", "vt", "written")}
                else:
                    e |= {n: s(n) for n in ("w1_mm", "w2_mm", "silu", "ha", "h1_mm", "hb", "h2_mm", "hc", "o_mm")}

                def norm_vector(v, b, src, dst, i):
                    for n in range(NT):
                        last = v.bn_stats(stats[:, n, :], src[:, n, :])
                    last.then_inc(e[f"st{i}"], 1)
                    v.wait_ge(e[f"st{i}"], BASE + b + 1)
                    v.sem_inc(held_off, 1)
                    for n in range(NT):
                        last = v.bn_aggr(mv[:, n, :], stats[:, n, :])
                    last.then_inc(e[f"mv{i}"], 1)
                    v.wait_ge(e[f"rs{i}"], BASE + b + 1)
                    for n in range(NT):
                        last = v.tensor_scalar(dst[:, n, :], src[:, n, :], mv[:, n, 0:1], rstd[:, n:n + 1], ALU.subtract, ALU.mult)
                    last.then_inc(e[f"x{i}"], 1)

                def norm_pool(p, b, i):
                    p.wait_ge(e[f"mv{i}"], BASE + b + 1)
                    p.sem_inc(held_off, 1)
                    p.tensor_scalar(veps[:, :], mv[:, :, 1], EPS, None, ALU.add).then_inc(e[f"ve{i}"], 1)
                    p.wait_ge(e[f"ve{i}"], BASE + b + 1)
                    p.tensor_tensor(rstd[:, :], veps[:, :], half[:, :], ALU.pow).then_inc(e[f"rs{i}"], 1)

                def flip(pe, dst, src, event):
                    for n in range(NT):
                        last = pe.transpose(dst[:, n * 128:(n + 1) * 128], src[:, n, :], ident[:, :])
                    last.then_inc(event, 1)

                def by_token(pe, dst, src, w, event):
                    for n in range(NT):
                        last = pe.matmul(dst[:, n * 128:(n + 1) * 128], src[:, n * 128:(n + 1) * 128], w, start=True, stop=True)
                    last.then_inc(event, 1)

                n_written = 5 * NTERM + 1
                uvs_in, fill = s("uvs_in"), s("fill")

                start_phase()
                with nc.Block() as block:
                    @block.sync
                    def _(sp):
                        for tile, src in loads:
                            dst = tile[:, :] if len(tile.shape) == 2 else tile[:, :, :]
                            sp.dma_start(dst, src).then_inc(c_in, 16)
                        with sp.Fori(0, B) as b:
                            sp.wait_ge(e["normed"], BASE + b)
                            sp.sem_inc(held_off, 1)
                            sp.wait_ge(e["biased"], BASE + b)
                            sp.sem_inc(held_off, 1)
                            own = bass.ts(b, H)
                            sp.dma_start(head_t[:, :], heads_out[own, 0:DH, :]).then_inc(e["head_in"], 16)
                            rep = bass.AP(heads_out.tensor, (b * H) * (VW * T) + DH * T, [[VW * T, H], [0, DH], [1, T]])
                            sp.dma_start(sums[:, :], rep).then_inc(e["head_in"], 16)
                            old = t["x"][b] if first else resid[b]
                            sp.dma_start(xin[:, :, :], old.rearrange("(n p) c -> p n c", p=128)).then_inc(e["x_in"], 16)
                            sp.wait_ge(e["x2"], BASE + b + 1)
                            sp.sem_inc(held_off, 1)
                            new = resid[b] if first else t["out"][b]
                            sp.dma_start(new.rearrange("(n p) c -> p n c", p=128), x2[:, :, :]).then_inc(e["f_stored"], 16)
                            if first:
                                sp.wait_ge(e["lo"], BASE + b + 1)
                                sp.sem_inc(held_off, 1)
                                for j in range(NTERM):
                                    content, pos = slice(DH * j, DH * j + DH), slice(SR + DH * j, SR + DH * j + DH)
                                    st, q = stack[1], part[Q_PART[j]]
                                    sp.dma_start(st[own, content, 0, :], part[K_PART[j]][:, 0:T]).then_inc(e["written"], 16)
                                    sp.dma_start(st[own, content, 1, :], q[:, T:2 * T]).then_inc(e["written"], 16)
                                    sp.dma_start(st[own, content, 2, :], q[:, T:2 * T]).then_inc(e["written"], 16)
                                    sp.dma_start(st[own, pos, 1, :], q[:, 2 * T:3 * T]).then_inc(e["written"], 16)
                                    sp.dma_start(st[own, pos, 2, :], q[:, 3 * T + 1:4 * T + 1]).then_inc(e["written"], 16)
                                sp.wait_ge(e["vt"], BASE + b + 1)
                                sp.sem_inc(held_off, 1)
                                sp.dma_start(values[own].rearrange("h p n c -> p h n c"), vt[:, :, :, :]).then_inc(e["written"], 16)
                        sp.wait_ge(e["f_stored"], BASE + 16 * B)
                        if first:
                            sp.wait_ge(e["written"], BASE + 16 * n_written * B)

                    @block.tensor
                    def _(pe):
                        pe.wait_ge(c_in, BASE + 16 * len(loads))
                        with pe.Fori(0, B) as b:
                            pe.wait_ge(e["normed"], BASE + b + 1)
                            if first:
                                pe.wait_ge(e["qk"], BASE + b)
                            else:
                                pe.wait_ge(e["gated"], BASE + b)
                            by_token(pe, bank[0], head_n, wo[:, :], e["out_mm"])
                            pe.wait_ge(e["x1"], BASE + b + 1)
                            if first:
                                flip(pe, bank[1], x1, e["tr1"])
                                pe.wait_ge(e["mixed"], BASE + b + 1)
                                pe.matmul(bank[2][:, :], w_k[:, :], xk[:, :], start=True, stop=True).then_inc(e["k_mm"], 1)
                                pe.wait_ge(e["vt"], BASE + b)
                                by_token(pe, bank[3], xr, w_r[:, :], e["r_mm"])
                                pe.wait_ge(e["kact"], BASE + b + 1)
                                by_token(pe, bank[4], kact, w_v[:, :], e["kv_mm"])
                                pe.wait_ge(e["x2"], BASE + b + 1)
                                flip(pe, bank[5], x2, e["tr2"])
                                pe.wait_ge(e["xt2"], BASE + b + 1)
                                pe.matmul(bank[2][:, :], wk[:, :], xt2[:, :], start=True, stop=True)
                                pe.matmul(bank[0][:, :], wq[:, :], xt2[:, :], start=True, stop=True)
                                pe.matmul(bank[1][:, :], wqs[:, :], xt2[:, :], start=True, stop=True).then_inc(e["qk_mm"], 1)
                                by_token(pe, bank[3], xt2, wv[:, :], e["v_mm"])
                            else:
                                flip(pe, bank[7], x1, e["tr1"])
                                pe.wait_ge(e["xt1"], BASE + b + 1)
                                for m in range(KH):
                                    col = slice(128 * m, 128 * m + 128)
                                    pe.matmul(bank[m][:, :], w1[:, col], xt1[:, 1:1 + T], start=True, stop=True).then_inc(e["w1_mm"], 1)
                                    pe.matmul(bank[4 + m][:, :], w2[:, col], xt1[:, 1:1 + T], start=True, stop=True).then_inc(e["w2_mm"], 1)
                                pe.wait_ge(e["ha"], BASE + KH * b + KH)
                                for m in range(KH):
                                    for k in range(KH):
                                        last = pe.matmul(bank[m][:, :], h1[:, k, 128 * m:128 * m + 128], ha[:, k, :],
                                                         start=(k == 0), stop=(k == KH - 1))
                                    last.then_inc(e["h1_mm"], 1)
                                pe.wait_ge(e["hb"], BASE + KH * b + KH)
                                for m in range(KH):
                                    for k in range(KH):
                                        last = pe.matmul(bank[4 + m][:, :], h2[:, k, 128 * m:128 * m + 128], hb[:, k, :],
                                                         start=(k == 0), stop=(k == KH - 1))
                                    last.then_inc(e["h2_mm"], 1)
                                pe.wait_ge(e["hc"], BASE + KH * b + KH)
                                for n in range(NT):
                                    for k in range(KH):
                                        last = pe.matmul(bank[0][:, n * 128:(n + 1) * 128], hc[:, k, n * 128:(n + 1) * 128], w3[:, k, :],
                                                         start=(k == 0), stop=(k == KH - 1))
                                last.then_inc(e["o_mm"], 1)

                    @block.gpsimd
                    def _(p):
                        p.memset(half[:, :], -0.5).then_inc(ready, 1)
                        p.wait_ge(ready, BASE + 1)
                        with p.Fori(0, B) as b:
                            norm_pool(p, b, 1)
                            norm_pool(p, b, 2)
                            if first:
                                p.wait_ge(e["qk"], BASE + b + 1)
                                p.tensor_tensor(rot[:, 1, :], qv[:, 1, :], trig[:, 1, :], ALU.mult)
                                p.tensor_tensor(rot[:, 3, :], qv[:, 1, :], trig[:, 3, :], ALU.mult).then_inc(e["r1"], 1)

                    @block.scalar
                    def _(act):
                        act.wait_ge(c_in, BASE + 16 * len(loads))
                        if first:
                            nc.scalar.activation(uvs[:, :], uv[:, :], ACT.Identity, scale=SCALE[1]).then_inc(uvs_in, 1)
                            act.wait_ge(uvs_in, BASE + 1)
                        with act.Fori(0, B) as b:
                            act.wait_ge(e["tr1"], BASE + b + 1)
                            nc.scalar.copy(xt1[:, 1:1 + T], bank[1 if first else 7][:, :]).then_inc(e["xt1"], 1)
                            if first:
                                act.wait_ge(e["r_mm"], BASE + b + 1)
                                nc.scalar.activation(gate[:, :, :], bank[3][:, :].rearrange("p (n c) -> p n c", n=NT),
                                                     ACT.Sigmoid).then_inc(e["sig"], 1)
                                act.wait_ge(e["kr"], BASE + b + 1)
                                nc.scalar.activation(kact[:, :], kr[:, :], ACT.Square).then_inc(e["kact"], 1)
                                act.wait_ge(e["tr2"], BASE + b + 1)
                                nc.scalar.copy(xt2[:, :], bank[5][:, :]).then_inc(e["xt2"], 1)
                                act.wait_ge(e["qk_mm"], BASE + b + 1)
                                nc.scalar.copy(full[:, 0, :], bank[2][:, :])
                                nc.scalar.activation(full[:, 1, :], bank[0][:, :], ACT.Identity, bias=uvs[:, 0:1], scale=SCALE[1])
                                nc.scalar.activation(qv[:, 0, :], bank[0][:, :], ACT.Identity, bias=uvs[:, 1:2], scale=SCALE[1])
                                nc.scalar.activation(qv[:, 1, :], bank[1][:, :], ACT.Identity, bias=uvs[:, 2:3],
                                                     scale=SCALE[1]).then_inc(e["qk"], 1)
                                act.wait_ge(e["qk"], BASE + b + 1)
                                act.wait_ge(e["rot"], BASE + b + 1)
                                act.wait_ge(e["written"], BASE + 16 * n_written * b)
                                nc.scalar.copy(part[0][:, 0:4 * T], full[:, :, :].rearrange("p a t -> p (a t)")).then_inc(e["hi"], 1)
                            else:
                                for m in range(KH):
                                    act.wait_ge(e["w1_mm"], BASE + KH * b + m + 1)
                                    nc.scalar.activation(silu[:, m, :], bank[m][:, :], ACT.Silu, scale=fs[:, 0, m:m + 1]).then_inc(e["silu"], 1)
                                for m in range(KH):
                                    act.wait_ge(e["h1_mm"], BASE + KH * b + m + 1)
                                    nc.scalar.activation(hb[:, m, :], bank[m][:, :], ACT.Gelu, scale=fs[:, 2, m:m + 1]).then_inc(e["hb"], 1)
                                for m in range(KH):
                                    act.wait_ge(e["h2_mm"], BASE + KH * b + m + 1)
                                    nc.scalar.activation(hc[:, m, :], bank[4 + m][:, :], ACT.Gelu, scale=fs[:, 3, m:m + 1]).then_inc(e["hc"], 1)

                    @block.vector
                    def _(v):
                        if first:
                            v.memset(xt1[:, 0:1], 0.0).then_inc(fill, 1)
                            v.memset(vt[:, :, :, DH:VC], 1.0).then_inc(fill, 1)
                            for i in range(3):
                                v.memset(part[i][:, 4 * T:4 * T + 2], 0.0).then_inc(fill, 1)
                            v.wait_ge(fill, BASE + 5)
                        v.wait_ge(c_in, BASE + 16 * len(loads))
                        with v.Fori(0, B) as b:
                            v.wait_ge(e["head_in"], BASE + 32 * b + 32)
                            v.reciprocal(sums[:, :], sums[:, :]).then_inc(e["recip"], 1)
                            v.wait_ge(e["recip"], BASE + b + 1)
                            v.tensor_tensor(head_n[:, :], head_t[:, :], sums[:, :], ALU.mult).then_inc(e["normed"], 1)
                            v.wait_ge(e["x_in"], BASE + 16 * b + 16)
                            for n in range(NT):
                                last = v.tensor_tensor(xb[:, n, :], xin[:, n, :], bo[:, :], ALU.add)
                            last.then_inc(e["biased"], 1)
                            v.wait_ge(e["biased"], BASE + b + 1)
                            v.wait_ge(e["out_mm"], BASE + b + 1)
                            v.tensor_tensor(pre[:, :, :], bank[0][:, :].rearrange("p (n c) -> p n c", n=NT), xb[:, :, :],
                                            ALU.add).then_inc(e["summed"], 1)
                            v.wait_ge(e["summed"], BASE + b + 1)
                            norm_vector(v, b, pre, x1, 1)
                            if first:
                                v.wait_ge(e["xt1"], BASE + b + 1)
                                v.tensor_tensor(delta[:, :], xt1[:, 1:1 + T], xt1[:, 0:T], ALU.subtract).then_inc(e["delta"], 1)
                                v.wait_ge(e["delta"], BASE + b + 1)
                                v.scalar_tensor_tensor(out=xk[:, :], in0=delta[:, :], scalar=mu[:, 1:2], in1=xt1[:, 0:T],
                                                       op0=ALU.mult, op1=ALU.add)
                                v.scalar_tensor_tensor(out=xr[:, :], in0=delta[:, :], scalar=mu[:, 0:1], in1=xt1[:, 0:T],
                                                       op0=ALU.mult, op1=ALU.add).then_inc(e["mixed"], 1)
                                v.wait_ge(e["k_mm"], BASE + b + 1)
                                v.tensor_scalar(kr[:, :], bank[2][:, :], 0.0, None, ALU.max).then_inc(e["kr"], 1)
                                v.wait_ge(e["sig"], BASE + b + 1)
                                v.wait_ge(e["kv_mm"], BASE + b + 1)
                                v.tensor_tensor(drop[:, :, :], bank[4][:, :].rearrange("p (n c) -> p n c", n=NT), gate[:, :, :],
                                                ALU.mult).then_inc(e["gated"], 1)
                            else:
                                for m in range(KH):
                                    v.wait_ge(e["w2_mm"], BASE + KH * b + m + 1)
                                    v.wait_ge(e["silu"], BASE + KH * b + m + 1)
                                    v.scalar_tensor_tensor(out=ha[:, m, :], in0=bank[4 + m][:, :], scalar=fs[:, 1, m:m + 1],
                                                           in1=silu[:, m, :], op0=ALU.mult, op1=ALU.mult).then_inc(e["ha"], 1)
                                v.wait_ge(e["o_mm"], BASE + b + 1)
                                for n in range(NT):
                                    last = v.tensor_tensor(drop[:, n, :], bank[0][:, n * 128:(n + 1) * 128], s3[:, :], ALU.mult)
                                last.then_inc(e["gated"], 1)
                            v.wait_ge(e["gated"], BASE + b + 1)
                            v.tensor_tensor(pre[:, :, :], drop[:, :, :], x1[:, :, :], ALU.add).then_inc(e["added"], 1)
                            v.wait_ge(e["added"], BASE + b + 1)
                            v.wait_ge(e["f_stored"], BASE + 16 * b)
                            norm_vector(v, b, pre, x2, 2)
                            if first:
                                v.wait_ge(e["v_mm"], BASE + b + 1)
                                v.wait_ge(e["written"], BASE + 16 * n_written * b)
                                for n in range(NT):
                                    last = v.tensor_copy(vt[:, :, n, 0:DH],
                                                         bank[3][:, n * 128:(n + 1) * 128].rearrange("p (h d) -> p h d", d=DH))
                                last.then_inc(e["vt"], 1)
                                v.wait_ge(e["qk"], BASE + b + 1)
                                v.tensor_tensor(rot[:, 0, :], qv[:, 0, :], trig[:, 0, :], ALU.mult)
                                v.tensor_tensor(rot[:, 2, :], qv[:, 0, :], trig[:, 2, :], ALU.mult).then_inc(e["r2"], 1)
                                v.wait_ge(e["r2"], BASE + b + 1)
                                v.wait_ge(e["r1"], BASE + b + 1)
                                v.tensor_tensor(full[:, 2, :], rot[:, 0, :], rot[:, 1, :], ALU.add)
                                v.tensor_tensor(full[:, 3, :], rot[:, 2, :], rot[:, 3, :], ALU.add).then_inc(e["rot"], 1)
                                v.wait_ge(e["hi"], BASE + b + 1)
                                flat = full[:, :, :].rearrange("p a t -> p (a t)")
                                lf = left[:, :, :].rearrange("p a t -> p (a t)")
                                v.tensor_tensor(lf, flat, part[0][:, 0:4 * T], ALU.subtract).then_inc(e["left"], 1)
                                v.wait_ge(e["left"], BASE + b + 1)
                                v.tensor_copy(part[1][:, 0:4 * T], lf).then_inc(e["mid"], 1)
                                v.wait_ge(e["mid"], BASE + b + 1)
                                v.tensor_tensor(part[2][:, 0:4 * T], lf, part[1][:, 0:4 * T], ALU.subtract).then_inc(e["lo"], 1)

        tables_phase()
        end_phase()
        attention_phase(0)
        end_phase()
        dense_phase(0)
        end_phase()
        attention_phase(1)
        end_phase()
        dense_phase(1)


def _tables(np):
    k = np.arange(T, dtype=np.float64)
    freq = (1.0 / np.float32(10000.0) ** (np.arange(0, DH, 2, dtype=np.float32) / np.float32(DH))).astype(np.float64)
    sin, cos = (lambda p: np.sin(p[None, :] * freq[:, None])), (lambda p: np.cos(p[None, :] * freq[:, None]))
    own = [np.concatenate([sin(p), sin(p)]) for p in (k, k + T)]
    swap = [np.concatenate([cos(p), -cos(p)]) for p in (k, k + T)]
    trig = np.stack([own[0], swap[0], own[1], swap[1]], 1)
    key = np.concatenate([cos(k), sin(k)]).astype(np.float32)
    bits = []
    left = key.copy()
    for _ in range(3):
        u = left.view(np.uint32)
        r = ((u + np.uint32(0x7FFF) + ((u >> 16) & 1)) >> 16).astype(np.uint32)
        bits.append(r.astype(np.uint16))
        left = left - (r << 16).astype(np.uint32).view(np.float32)
    p, c = np.arange(128)[:, None], np.arange(128)[None, :]
    block = -(np.arange(C)[:, None] // DH == np.arange(H)[None, :]).astype(np.float32)
    return {
        "ident": np.eye(128, dtype=np.float32), "mask0": (c >= p).astype(np.uint32), "mask1": (c >= p + 2).astype(np.uint32),
        "negblock": block, "trig": np.ascontiguousarray(np.tile(trig, (H, 1, 1)).astype(np.float32)),
        "poskey": np.stack(bits),
    }


def kernel(**inputs):
    import numpy as np
    import concourse.bacc as bacc
    from concourse.bass_utils import run_bass_kernel_spmd

    a = {n: np.asarray(v) for n, v in inputs.items()}
    L0, F0, L1, F1 = "L0_attn_", "L0_ffn_", "L1_attn_", "L1_ffn_"
    swap = (np.arange(C) // DH) * DH + (np.arange(C) + DH // 2) % DH

    def tr(x):
        return np.ascontiguousarray(x.T)

    def col(x):
        return np.ascontiguousarray(x.reshape(C, 1))

    arrays = {
        "x": a[L0 + "x"], "xT": np.ascontiguousarray(a[L0 + "x"].transpose(0, 2, 1)),
        "WqT": tr(a[L0 + "Wq"]), "WkT": tr(a[L0 + "Wk"]), "WvT": tr(a[L0 + "Wv"]), "WoT": tr(a[L0 + "Wo"]),
        "WpkT": tr(a[L0 + "Wpk"]), "WpqT": tr(a[L0 + "Wpq"]), "relT": tr(a[L0 + "rel_emb"]),
        "bq": col(a[L0 + "bq"]), "bk": col(a[L0 + "bk"]), "bpk": col(a[L0 + "bpk"]), "bpq": col(a[L0 + "bpq"]),
        "bv": a[L0 + "bv"], "bo": a[L0 + "bo"],
        "W_rT": tr(a[F0 + "W_r"]), "W_kT": tr(a[F0 + "W_k"]), "W_vT": tr(a[F0 + "W_v"]),
        "mu": np.ascontiguousarray(np.stack([a[F0 + "mu_r"], a[F0 + "mu_k"]], 1)),
        "Wq": a[L1 + "Wq"], "Wq_swap": np.ascontiguousarray(a[L1 + "Wq"][:, swap]), "Wk": a[L1 + "Wk"], "Wv": a[L1 + "Wv"],
        "Wo": a[L1 + "Wo"], "bo1": a[L1 + "bo"],
        "uv": np.ascontiguousarray(np.stack([a[L1 + "u"].reshape(C), a[L1 + "v"].reshape(C), a[L1 + "v"].reshape(C)[swap]], 1)),
        "w1T": tr(a[F1 + "w1_w"]), "w2T": tr(a[F1 + "w2_w"]), "h1T": tr(a[F1 + "h1_w"]), "h2T": tr(a[F1 + "h2_w"]),
        "w3T": tr(a[F1 + "w3_w"]), "w3_s": a[F1 + "w3_s"],
        "hid_s": np.ascontiguousarray(np.stack([a[F1 + n].reshape(KH, 128) for n in ("w1_s", "w2_s", "h1_s", "h2_s")], 0)
                                      .transpose(2, 0, 1)),
    }
    arrays.update(_tables(np))
    nc = bacc.Bacc("TRN2", target_bir_lowering=False, num_devices=1)
    t = {}
    for n, v in arrays.items():
        dt = BF16 if n == "poskey" else mybir.dt.from_np(v.dtype)
        if n == "poskey":
            t[n] = nc.dram_tensor("in_" + n, v.shape, mybir.dt.uint16, kind="ExternalInput").ap().bitcast(BF16)
        else:
            t[n] = nc.dram_tensor("in_" + n, v.shape, dt, kind="ExternalInput").ap()
    t["out"] = nc.dram_tensor("out_0", (B, T, C), F32, kind="ExternalOutput").ap()
    build(nc, t)
    r = run_bass_kernel_spmd(nc, [{"in_" + n: v for n, v in arrays.items()}], core_ids=[0])
    return r.results[0]["out_0"]
```

```python
from contextlib import ExitStack

import concourse.bass as bass
from concourse import mybir

F32 = mybir.dt.float32
BF16 = mybir.dt.bfloat16
U32 = mybir.dt.uint32
ALU = mybir.AluOpType
ACT = mybir.ActivationFunctionType
AX = mybir.AxisListType

B, T, C = 8, 512, 128
H = 16
DH = C // H
NT = T // 128
NHEAD = B * H
SPAN = 64
REL = 2 * SPAN
HID = 512
KH = HID // 128
EPS = 1e-5
Q_PART = [0, 0, 0, 1, 1, 2]
K_PART = [0, 1, 2, 0, 1, 0]
NTERM = len(Q_PART)
SR = NTERM * DH
R0 = SR + 3
R1 = 2 * SR
KHI, KLO, QLO, QHI = range(4)
GROUP = 4
NG = NHEAD // GROUP
UNROLL = {0: 8, 1: 12}
FIRST = GROUP
SCORE_AHEAD, EXP_AHEAD = 6, 4
CORR_AHEAD, KEY_AHEAD, LOAD_AHEAD = 4, 6, 7
PITCH_A = SPAN + T + SPAN
PITCH_B = 3 * REL
WIN = 2 * REL
VC = DH + 1
VW = 32
BASE = 32

SCALE = {0: (3 * DH) ** -0.5, 1: DH ** -0.5}


def build(nc, t):
    top = ExitStack()
    with top:
        sems, held = {}, ExitStack()

        def sem(name):
            if name not in sems:
                sems[name] = held.enter_context(nc.semaphore(name))
            return sems[name]

        def start_phase():
            with nc.Block() as block:
                @block.sync
                def _(sp):
                    for handle in sems.values():
                        sp.sem_inc(handle, BASE)

        def end_phase():
            with nc.Block() as block:
                @block.sync
                def _(sp):
                    for handle in sems.values():
                        sp.sem_clear(handle)
            held.close()
            sems.clear()

        bank = [top.enter_context(nc.psum_tensor(f"bank{i}", [128, 512], F32)) for i in range(8)]

        def dram(name, shape, dt):
            return nc.dram_tensor(name, shape, dt, kind="Internal").ap()

        stack = {0: dram("stack0", [NHEAD, R0, 4, T], BF16), 1: dram("stack1", [NHEAD, R1, 3, T], BF16)}
        values = dram("values", [NG, 128, GROUP * NT * VC], F32)
        table = dram("table", [H, R0, 2 * REL], BF16)
        heads_out = dram("heads_out", [NHEAD, VW, T], F32)
        resid = dram("resid", [B, T, C], F32)
        shear_a = dram("shear_a", [4, 128, PITCH_A], F32)
        shear_b = dram("shear_b", [4, T, PITCH_B], F32)

        def tables_phase():
            with ExitStack() as ctx:
                def sb(name, shape, dt=F32):
                    return ctx.enter_context(nc.sbuf_tensor(name, shape, dt))

                wpk, wpq, relt = sb("wpk", [C, C]), sb("wpq", [C, C]), sb("relt", [C, REL])
                cols = sb("cols", [C, 4])
                sc = sb("sc", [C, 2])
                negblock = sb("negblock", [C, H])
                pk, pq = sb("pk", [C, REL]), sb("pq", [C, REL])
                d = sb("d", [C, 2, REL])
                e = sb("e", [C, REL + 1])
                e1 = sb("e1", [C, REL + 1])
                kc = sb("kc", [H, REL + T])
                parts = [sb(f"dp{i}", [C, 2, REL], BF16) for i in range(3)]
                kparts = [sb(f"kp{i}", [H, REL + T], BF16) for i in range(3)]
                rest, krest = sb("rest", [C, 2, REL]), sb("krest", [H, REL + T])
                ones, zeros = sb("ones", [SR, T], BF16), sb("zeros", [128, T], BF16)
                zf = sb("zf", [128, 3 * REL])
                bias = sb("bias", [C, 4])
                s_in, s_ps, s_pk, s_col, s_d = (sem(n) for n in ("tab_in", "tab_ps", "tab_pk", "tab_col", "tab_d"))
                s_e, s_kps, s_kc, s_part, s_out = (sem(n) for n in ("tab_e", "tab_kps", "tab_kc", "tab_part", "tab_out"))
                s_fill = sem("tab_fill")

                start_phase()
                with nc.Block() as block:
                    @block.sync
                    def _(sp):
                        for dst, src in ((wpk, t["WpkT"]), (wpq, t["WpqT"]), (relt, t["relT"]), (negblock, t["negblock"])):
                            sp.dma_start(dst[:, :], src).then_inc(s_in, 16)
                        for i, n in enumerate(("bq", "bk", "bpk", "bpq")):
                            sp.dma_start(cols[:, i:i + 1], t[n]).then_inc(s_in, 16)
                        sp.wait_ge(s_fill, BASE + 3)
                        for i in range(4):
                            for at in (0, SPAN + T):
                                sp.dma_start(shear_a[i, :, at:at + SPAN], zf[:, 0:SPAN]).then_inc(s_out, 16)
                            for at in (0, 2 * REL):
                                for n in range(NT):
                                    sp.dma_start(shear_b[i, n * 128:(n + 1) * 128, at:at + REL], zf[:, 0:REL]).then_inc(s_out, 16)
                        sp.wait_ge(s_part, BASE + 1)
                        for j in range(NTERM):
                            rows = slice(DH * j, DH * j + DH)
                            sp.dma_start(table[:, rows, 0:REL], parts[Q_PART[j]][:, 0, :]).then_inc(s_out, 16)
                            sp.dma_start(table[:, rows, REL:2 * REL], parts[K_PART[j]][:, 1, :]).then_inc(s_out, 16)
                        for i in range(3):
                            sp.dma_start(table[:, SR + i, 0:REL], kparts[i][:, 0:REL]).then_inc(s_out, 16)
                            sp.dma_start(table[:, SR + i, REL:2 * REL], zeros[0:H, 0:REL]).then_inc(s_out, 16)
                        for b in range(B):
                            own = slice(b * H, b * H + H)
                            sp.dma_start(stack[0][own, SR:R0, KLO, :], ones[:, :]).then_inc(s_out, 16)
                            sp.dma_start(stack[0][own, SR:R0, KHI, :], ones[:, :]).then_inc(s_out, 16)
                            sp.dma_start(stack[0][own, SR:R0, QLO, :], zeros[0:SR, :]).then_inc(s_out, 16)
                            for i in range(3):
                                sp.dma_start(stack[0][own, SR + i, QHI, :], kparts[i][:, REL:REL + T]).then_inc(s_out, 16)
                        n_out = 4 * (2 + 2 * NT) + 2 * NTERM + 6 + 6 * B
                        sp.wait_ge(s_out, BASE + 16 * n_out)

                    @block.tensor
                    def _(pe):
                        pe.wait_ge(s_in, BASE + 16 * 8)
                        pe.matmul(bank[0][:, 0:REL], wpk[:, :], relt[:, :], start=True, stop=True).then_inc(s_ps, 1)
                        pe.matmul(bank[1][:, 0:REL], wpq[:, :], relt[:, :], start=True, stop=True).then_inc(s_ps, 1)
                        pe.wait_ge(s_e, BASE + 4)
                        pe.matmul(bank[2][0:H, 0:REL + 1], negblock[:, :], e[:, :], start=True, stop=True).then_inc(s_kps, 1)

                    @block.scalar
                    def _(act):
                        act.wait_ge(s_in, BASE + 16 * 8)
                        nc.scalar.activation(sc[:, 0:1], cols[:, 0:1], ACT.Identity, scale=SCALE[0]).then_inc(s_col, 1)
                        nc.scalar.activation(sc[:, 1:2], cols[:, 3:4], ACT.Identity, scale=SCALE[0]).then_inc(s_col, 1)
                        act.wait_ge(s_ps, BASE + 2)
                        nc.scalar.activation(pk[:, :], bank[0][:, 0:REL], ACT.Identity, bias=cols[:, 2:3]).then_inc(s_pk, 1)
                        act.wait_ge(s_col, BASE + 2)
                        nc.scalar.activation(pq[:, :], bank[1][:, 0:REL], ACT.Identity, bias=sc[:, 1:2], scale=SCALE[0]).then_inc(s_pk, 1)

                    @block.vector
                    def _(v):
                        last = REL - 1
                        v.memset(ones[:, :], 1.0).then_inc(s_fill, 1)
                        v.memset(zeros[:, :], 0.0).then_inc(s_fill, 1)
                        v.memset(zf[:, :], 0.0).then_inc(s_fill, 1)
                        v.wait_ge(s_pk, BASE + 2)
                        v.tensor_tensor(bias[:, QLO:QLO + 1], sc[:, 0:1], pq[:, 0:1], ALU.add).then_inc(s_d, 1)
                        v.tensor_tensor(bias[:, QHI:QHI + 1], sc[:, 0:1], pq[:, last:REL], ALU.add).then_inc(s_d, 1)
                        v.tensor_tensor(bias[:, KLO:KLO + 1], cols[:, 1:2], pk[:, 0:1], ALU.add).then_inc(s_d, 1)
                        v.tensor_tensor(bias[:, KHI:KHI + 1], cols[:, 1:2], pk[:, last:REL], ALU.add).then_inc(s_d, 1)
                        v.tensor_scalar(d[:, 0, :], pq[:, :], pq[:, 0:1], None, ALU.subtract).then_inc(s_d, 1)
                        v.tensor_scalar(d[:, 1, :], pk[:, :], pk[:, 0:1], None, ALU.subtract).then_inc(s_d, 1)
                        v.wait_ge(s_d, BASE + 6)
                        v.tensor_scalar(e1[:, 0:REL], d[:, 1, :], pq[:, 0:1], None, ALU.mult).then_inc(s_e, 1)
                        v.tensor_tensor(e1[:, REL:REL + 1], pq[:, 0:1], pk[:, 0:1], ALU.mult).then_inc(s_e, 1)
                        v.wait_ge(s_e, BASE + 2)
                        v.scalar_tensor_tensor(out=e[:, 0:REL], in0=d[:, 0, :], scalar=pk[:, 0:1], in1=e1[:, 0:REL],
                                               op0=ALU.mult, op1=ALU.add).then_inc(s_e, 1)
                        v.scalar_tensor_tensor(out=e[:, REL:REL + 1], in0=pq[:, last:REL], scalar=pk[:, last:REL],
                                               in1=e1[:, REL:REL + 1], op0=ALU.mult, op1=ALU.subtract).then_inc(s_e, 1)
                        v.wait_ge(s_kps, BASE + 1)
                        v.tensor_copy(kc[:, 0:REL], bank[2][0:H, 0:REL]).then_inc(s_kc, 1)
                        v.tensor_scalar(kc[:, REL:REL + T], zeros[0:H, :], bank[2][0:H, REL:REL + 1], None, ALU.add).then_inc(s_kc, 1)
                        v.wait_ge(s_kc, BASE + 2)
                        v.tensor_copy(parts[0][:, :, :], d[:, :, :]).then_inc(s_kc, 1)
                        v.tensor_copy(kparts[0][:, :], kc[:, :]).then_inc(s_kc, 1)
                        v.wait_ge(s_kc, BASE + 4)
                        v.tensor_tensor(rest[:, :, :], d[:, :, :], parts[0][:, :, :], ALU.subtract).then_inc(s_kc, 1)
                        v.tensor_tensor(krest[:, :], kc[:, :], kparts[0][:, :], ALU.subtract).then_inc(s_kc, 1)
                        v.wait_ge(s_kc, BASE + 6)
                        v.tensor_copy(parts[1][:, :, :], rest[:, :, :]).then_inc(s_kc, 1)
                        v.tensor_copy(kparts[1][:, :], krest[:, :]).then_inc(s_kc, 1)
                        v.wait_ge(s_kc, BASE + 8)
                        v.tensor_tensor(parts[2][:, :, :], rest[:, :, :], parts[1][:, :, :], ALU.subtract)
                        v.tensor_tensor(kparts[2][:, :], krest[:, :], kparts[1][:, :], ALU.subtract).then_inc(s_part, 1)

                wq, wk, wv = sb("wq", [C, C]), sb("wk", [C, C]), sb("wv", [C, C])
                bv = sb("bv", [128, C])
                xt = sb("xt", [C, T])
                full = sb("full", [C, 4, T])
                part = [sb(f"part{i}", [C, 4, T], BF16) for i in range(3)]
                left = sb("left", [C, 4, T])
                vt = sb("vt", [128, H, NT, VC])
                n_out = 2 * NTERM + 1
                end_phase()
                w_in, x_in, p_ps, v_ps = sem("p0_w"), sem("p0_x"), sem("p0_ps"), sem("p0_vps")
                p_full, p_hi, p_rest, p_mid, p_lo = (sem(n) for n in ("p0_full", "p0_hi", "p0_rest", "p0_mid", "p0_lo"))
                p_v, p_vone, p_out, held_off = sem("p0_v"), sem("p0_vone"), sem("p0_out"), sem("held_off")
                start_phase()
                with nc.Block() as block:
                    @block.sync
                    def _(sp):
                        for dst, src in ((wq, t["WqT"]), (wk, t["WkT"]), (wv, t["WvT"])):
                            sp.dma_start(dst[:, :], src).then_inc(w_in, 16)
                        sp.dma_start(bv[:, :], t["bv"].partition_broadcast(128)).then_inc(w_in, 16)
                        with sp.Fori(0, B) as b:
                            sp.wait_ge(p_ps, BASE + 2 * b)
                            sp.sem_inc(held_off, 1)
                            sp.wait_ge(v_ps, BASE + b)
                            sp.sem_inc(held_off, 1)
                            sp.dma_start(xt[:, :], t["xT"][b]).then_inc(x_in, 16)
                            sp.wait_ge(p_lo, BASE + b + 1)
                            sp.sem_inc(held_off, 1)
                            own = bass.ts(b, H)
                            for j in range(NTERM):
                                rows = slice(DH * j, DH * j + DH)
                                sp.dma_start(stack[0][own, rows, KHI:KLO + 1, :], part[K_PART[j]][:, KHI:KLO + 1, :]).then_inc(p_out, 16)
                                sp.dma_start(stack[0][own, rows, QLO:QHI + 1, :], part[Q_PART[j]][:, QLO:QHI + 1, :]).then_inc(p_out, 16)
                            sp.wait_ge(p_v, BASE + b + 1)
                            sp.sem_inc(held_off, 1)
                            sp.dma_start(values[bass.ts(b, H // GROUP)].rearrange("g p c -> p g c"),
                                         vt[:, :, :, :].rearrange("p (g h) n c -> p g (h n c)", h=GROUP)).then_inc(p_out, 16)
                        sp.wait_ge(p_out, BASE + 16 * n_out * B)

                    @block.tensor
                    def _(pe):
                        pe.wait_ge(w_in, BASE + 16 * 4)
                        with pe.Fori(0, B) as b:
                            pe.wait_ge(x_in, BASE + 16 * b + 16)
                            pe.wait_ge(p_full, BASE + b)
                            pe.wait_ge(p_v, BASE + b)
                            pe.matmul(bank[0][:, :], wq[:, :], xt[:, :], start=True, stop=True).then_inc(p_ps, 1)
                            pe.matmul(bank[1][:, :], wk[:, :], xt[:, :], start=True, stop=True).then_inc(p_ps, 1)
                            for n in range(NT):
                                last = pe.matmul(bank[2][:, n * 128:(n + 1) * 128], xt[:, n * 128:(n + 1) * 128], wv[:, :],
                                                 start=True, stop=True)
                            last.then_inc(v_ps, 1)

                    @block.scalar
                    def _(act):
                        with act.Fori(0, B) as b:
                            act.wait_ge(p_ps, BASE + 2 * b + 2)
                            act.wait_ge(p_lo, BASE + b)
                            for arr, src, scale in ((QLO, 0, SCALE[0]), (QHI, 0, SCALE[0]), (KLO, 1, 1.0), (KHI, 1, 1.0)):
                                last = nc.scalar.activation(full[:, arr, :], bank[src][:, :], ACT.Identity,
                                                            bias=bias[:, arr:arr + 1], scale=scale)
                            last.then_inc(p_full, 1)
                            act.wait_ge(p_full, BASE + b + 1)
                            act.wait_ge(p_out, BASE + 16 * n_out * b)
                            nc.scalar.copy(part[0][:, :, :], full[:, :, :]).then_inc(p_hi, 1)

                    @block.vector
                    def _(v):
                        v.memset(vt[:, :, :, DH:VC], 1.0).then_inc(p_vone, 1)
                        v.wait_ge(p_vone, BASE + 1)
                        v.wait_ge(w_in, BASE + 16 * 4)
                        with v.Fori(0, B) as b:
                            v.wait_ge(v_ps, BASE + b + 1)
                            v.wait_ge(p_out, BASE + 16 * n_out * b)
                            for n in range(NT):
                                last = v.tensor_tensor(vt[:, :, n, 0:DH],
                                                       bank[2][:, n * 128:(n + 1) * 128].rearrange("p (h d) -> p h d", d=DH),
                                                       bv[:, :].rearrange("p (h d) -> p h d", d=DH), ALU.add)
                            last.then_inc(p_v, 1)
                            v.wait_ge(p_hi, BASE + b + 1)
                            v.tensor_tensor(left[:, :, :], full[:, :, :], part[0][:, :, :], ALU.subtract).then_inc(p_rest, 1)
                            v.wait_ge(p_rest, BASE + b + 1)
                            v.tensor_copy(part[1][:, :, :], left[:, :, :]).then_inc(p_mid, 1)
                            v.wait_ge(p_mid, BASE + b + 1)
                            v.tensor_tensor(part[2][:, :, :], left[:, :, :], part[1][:, :, :], ALU.subtract).then_inc(p_lo, 1)

        def attention_phase(layer):
            rel = layer == 0
            unroll = UNROLL[layer]
            loops = (NHEAD - FIRST - LOAD_AHEAD) // unroll
            last = NHEAD - FIRST - unroll * loops
            vslots = unroll // GROUP
            with ExitStack() as ctx:
                def sb(name, shape, dt=F32):
                    return ctx.enter_context(nc.sbuf_tensor(f"a{layer}_{name}", shape, dt))

                def s(name):
                    return sem(f"a{layer}_{name}")

                rows = R0 if rel else R1
                stk = [sb(f"stk{i}", [rows, 4, T], BF16) for i in range(unroll)]
                vs = [sb(f"vs{i}", [128, GROUP * NT * VC + VW - VC]) for i in range(vslots)]
                prob = [sb(f"prob{i}", [128, NT, T]) for i in range(2)]
                probt = [sb(f"probt{i}", [128, NT, T]) for i in range(unroll)]
                negmax = [sb(f"negmax{i}", [128, NT]) for i in range(2)]
                ident = sb("ident", [128, 128])
                mask = sb("mask", [128, 128], U32)
                outs = sb("outs", [128, T])
                if rel:
                    tab = [sb(f"tab{i}", [R0, 2 * REL], BF16) for i in range(unroll)]
                    keyside = [sb(f"keyside{i}", [128, T]) for i in range(2)]
                    sheared = [sb(f"sheared{i}", [128, T]) for i in range(4)]
                    corr = [sb(f"corr{i}", [128, NT, REL]) for i in range(2)]
                    band = [sb(f"band{i}", [128, NT, WIN]) for i in range(2)]
                score_banks = bank[0:4] if rel else bank[0:3]
                others = bank[4:5] if rel else bank[3:5]
                cbank = bank[7]
                turned_bank = [bank[5], bank[6], bank[6], bank[5]] if rel else [bank[5], bank[6]] * 2
                key_bank, corr_bank = bank[5], bank[6]

                s_const, s_pad, held_off = s("const"), s("pad"), s("held_off")
                stk_in = [s(f"stk_in{i}") for i in range(unroll)]
                v_in = [s(f"v_in{i}") for i in range(vslots)]
                score_mm, fixed, mid_fixed, added, maxed, exped = (s(n) for n in ("score_mm", "fixed", "mid_fixed", "added", "maxed", "exped"))
                turned, copied, pv_mm, out_copied, out_written = (s(n) for n in ("turned", "copied", "pv_mm", "out_copied", "out_written"))
                if rel:
                    key_mm, key_copied, a_written, corr_mm, corr_copied, b_written = (
                        s(n) for n in ("key_mm", "key_copied", "a_written", "corr_mm", "corr_copied", "b_written"))
                    sheared_in = [s(f"sheared_in{i}") for i in range(4)]
                    band_in = [s(f"band_in{i}") for i in range(2)]

                poskey_in = s("poskey_in")

                class Head:
                    def __init__(self, i, at):
                        self.i, self.slot = i + at // unroll, at % unroll
                        self.n = unroll * i + at

                    def use(self, ring):
                        return (unroll // ring) * self.i + self.slot // ring

                def tile_banks(h, n):
                    at = NT * h.slot + n
                    return score_banks[at % len(score_banks)], others[at % len(others)]

                def made(n):
                    return min(n, NHEAD) if isinstance(n, int) else n

                def cut(n):
                    return min(T, 128 * n + (REL + SPAN if rel else 128))

                def fix_cols(n):
                    a = 128 * n + (SPAN if rel else 0)
                    return a, min(T, a + 128)

                def mid_cols(n):
                    return 128 * n + 1, min(T, 128 * n + 129)

                def win_cols(n):
                    a, e = 128 * n - SPAN, 128 * n - SPAN + WIN
                    return max(a, 0), min(e, T), max(a, 0) - a

                def hold(q, event, value):
                    q.wait_ge(event, BASE + value)
                    q.sem_inc(held_off, 1)

                per_stk = 32

                def head_load(sp, h):
                    j = h.slot
                    if rel:
                        sp.dma_start(stk[j][:, :, :], stack[0][h.n]).then_inc(stk_in[j], 16)
                        sp.dma_start(tab[j][:, :], table[h.n % H]).then_inc(stk_in[j], 16)
                    else:
                        sp.dma_start(stk[j][0:SR, KLO:QHI + 1, :], stack[1][h.n, 0:SR]).then_inc(stk_in[j], 16)
                        sp.dma_start(stk[j][SR:R1, QLO:QHI + 1, :], stack[1][h.n, SR:R1, 1:3, :]).then_inc(stk_in[j], 16)

                def shear_a_write(sp, h):
                    hold(sp, key_copied, h.n + 1)
                    sp.dma_start(shear_a[h.slot % 4, :, SPAN:SPAN + T], keyside[h.slot % 2][:, :]).then_inc(a_written, 16)

                def shear_a_read(sp, h):
                    hold(sp, a_written, 16 * (h.n + 1))
                    skew = bass.AP(shear_a.tensor, (h.slot % 4) * 128 * PITCH_A, [[PITCH_A + 1, 128], [1, T]])
                    sp.dma_start(sheared[h.slot % 4][:, :], skew).then_inc(sheared_in[h.slot % 4], 16)

                def shear_b_write(sp, h):
                    hold(sp, corr_copied, h.n + 1)
                    dst = shear_b[h.slot % 4].rearrange("(n p) c -> p n c", p=128)[:, :, REL:2 * REL]
                    sp.dma_start(dst, corr[h.slot % 2][:, :, :]).then_inc(b_written, 16)

                def shear_b_read(sp, h):
                    hold(sp, b_written, 16 * (h.n + 1))
                    skew = bass.AP(shear_b.tensor, (h.slot % 4) * T * PITCH_B + REL,
                                   [[PITCH_B - 1, 128], [128 * PITCH_B, NT], [1, WIN]])
                    sp.dma_start(band[h.slot % 2][:, :, :], skew).then_inc(band_in[h.slot % 2], 16)

                def sync_step(sp, i, j, left):
                    n = unroll * i + j
                    if rel and left > CORR_AHEAD:
                        shear_a_write(sp, Head(i, j + CORR_AHEAD + 1))
                    if rel and left > 1:
                        hold(sp, added, 4 * (n + 1))
                        shear_b_read(sp, Head(i, j + 2))
                    if rel and left > 2:
                        shear_b_write(sp, Head(i, j + 3))
                    if left > LOAD_AHEAD - 1:
                        hold(sp, maxed, 4 * n)
                        head_load(sp, Head(i, j + LOAD_AHEAD))
                    if rel and left > CORR_AHEAD:
                        shear_a_read(sp, Head(i, j + CORR_AHEAD + 1))

                start_phase()
                with nc.Block() as block:
                    @block.sync
                    def _(sp):
                        if rel:
                            head_load(sp, Head(0, 0))
                        for g in range(vslots):
                            sp.dma_start(vs[g][:, 0:GROUP * NT * VC], values[g]).then_inc(v_in[g], 16)
                        sp.dma_start(ident[:, :], t["ident"]).then_inc(s_const, 16)
                        sp.dma_start(mask[:, :], t[f"mask{layer}"]).then_inc(s_const, 16)
                        if not rel:
                            for i in range(unroll):
                                for j in range(NTERM):
                                    sp.dma_start(stk[i][SR + DH * j:SR + DH * j + DH, KLO, :],
                                                 t["poskey"][K_PART[j]]).then_inc(poskey_in, 16)
                        for j in range(1 if rel else 0, LOAD_AHEAD):
                            head_load(sp, Head(0, j))
                        if rel:
                            for j in range(4):
                                shear_a_write(sp, Head(0, j))
                                shear_a_read(sp, Head(0, j))
                            shear_b_write(sp, Head(0, 0))
                            shear_a_write(sp, Head(0, 4))
                            shear_a_read(sp, Head(0, 4))
                            shear_b_read(sp, Head(0, 0))
                            shear_b_write(sp, Head(0, 1))
                            shear_b_read(sp, Head(0, 1))
                            shear_b_write(sp, Head(0, 2))
                        for j in range(FIRST):
                            sync_step(sp, 0, j, NHEAD)
                        with sp.Fori(0, loops) as i:
                            for j in range(unroll):
                                sync_step(sp, i, FIRST + j, NHEAD)
                        for j in range(last):
                            sync_step(sp, loops, FIRST + j, last - 1 - j)
                        sp.wait_ge(out_written, BASE + 16 * NG)

                    def score_tile(pe, h, n):
                        tile, k = 4 * h.n + n, stk[h.slot]
                        score, other = tile_banks(h, n)
                        q = slice(128 * n, 128 * n + 128)
                        c = cut(n)
                        if n == 0:
                            pe.wait_ge(stk_in[h.slot], BASE + per_stk * (h.i + 1))
                        pe.wait_ge(exped, BASE + tile - len(score_banks) + 1)
                        lo = SR if rel else R1
                        pe.matmul(score[:, 0:c], k[0:lo, QLO, q], k[0:lo, KLO, 0:c], start=True, stop=True)
                        khi = KHI if rel else KLO
                        if c < T:
                            pe.matmul(score[:, c:T], k[:, QHI, q], k[:, khi, c:T], start=True, stop=True)
                        pe.wait_ge(fixed if rel else mid_fixed, BASE + tile - len(others) + 1)
                        a, e = fix_cols(n)
                        last = pe.matmul(other[:, 0:e - a], k[:, QHI, q], k[:, khi, a:e], start=True, stop=True)
                        if not rel:
                            a, e = mid_cols(n)
                            last = pe.matmul(other[:, 128:128 + e - a], k[0:SR, QLO, q], k[0:SR, KLO, a:e],
                                             start=True, stop=True)
                        last.then_inc(score_mm, 1)

                    def turn(pe, h, k):
                        if k == 0:
                            pe.wait_ge(exped, BASE + 4 * h.n + 4)
                        if rel and k == 1:
                            pe.wait_ge(corr_copied, BASE + made(h.n + CORR_AHEAD))
                        elif rel and k == 3:
                            pe.wait_ge(key_copied, BASE + made(h.n + KEY_AHEAD + 1))
                        else:
                            pe.wait_ge(copied, BASE + 4 * h.n + (k if rel else k - 1))
                        for n in range(NT):
                            last = pe.transpose(turned_bank[k][:, n * 128:(n + 1) * 128],
                                                prob[h.slot % 2][:, n, k * 128:(k + 1) * 128], ident[:, :])
                        last.then_inc(turned, 1)

                    def weigh(pe, h, k):
                        g = h.slot // GROUP
                        if k == 0:
                            pe.wait_ge(v_in[g], BASE + 16 * (h.i + 1))
                            pe.wait_ge(out_copied, BASE + h.use(GROUP))
                            pe.wait_ge(copied, BASE + 4 * (h.n + GROUP))
                        for j in range(GROUP):
                            at = VC * (NT * j + k)
                            pe.matmul(cbank[32 * j:32 * j + VW, :], vs[g][:, at:at + VW], probt[h.slot + j][:, k, :],
                                      start=(k == 0), stop=(k == NT - 1)).then_inc(pv_mm, 1)

                    def key_side(pe, h):
                        pe.wait_ge(stk_in[h.slot], BASE + per_stk * (h.i + 1))
                        pe.matmul(key_bank[:, :], tab[h.slot][:, 0:REL], stk[h.slot][:, KLO, :], start=True, stop=True).then_inc(key_mm, 1)

                    def correction(pe, h):
                        pe.wait_ge(sheared_in[h.slot % 4], BASE + 16 * (h.use(4) + 1))
                        for n in range(NT):
                            q = slice(128 * n, 128 * n + 128)
                            pe.matmul(corr_bank[:, q], sheared[h.slot % 4][:, q], ident[:, :], start=True, stop=False)
                            last = pe.matmul(corr_bank[:, q], stk[h.slot][0:SR, QLO, q], tab[h.slot][0:SR, REL:2 * REL], start=False, stop=True)
                        last.then_inc(corr_mm, 1)

                    def ahead(i, j, k, tiles):
                        return Head(i, j + (k + tiles) // NT), (k + tiles) % NT

                    def tensor_step(pe, i, j, left, weighed=True):
                        own = Head(i, j)
                        for k in range(NT):
                            if left >= (k + SCORE_AHEAD) // NT:
                                score_tile(pe, *ahead(i, j, k, SCORE_AHEAD))
                            turn(pe, own, k)
                            if k == 0 and weighed:
                                weigh(pe, Head(i, j - j % GROUP - GROUP), j % GROUP)
                            if rel and k == 1 and left >= KEY_AHEAD:
                                pe.wait_ge(copied, BASE + 4 * own.n + 1)
                                key_side(pe, Head(i, j + KEY_AHEAD))
                        if rel and left >= CORR_AHEAD:
                            pe.wait_ge(copied, BASE + 4 * own.n + 3)
                            correction(pe, Head(i, j + CORR_AHEAD))

                    @block.tensor
                    def _(pe):
                        pe.wait_ge(s_const, BASE + 32)
                        if not rel:
                            pe.wait_ge(poskey_in, BASE + 16 * unroll * NTERM)
                        if rel:
                            for j in range(KEY_AHEAD):
                                pe.wait_ge(key_copied, BASE + j)
                                key_side(pe, Head(0, j))
                            for j in range(CORR_AHEAD):
                                pe.wait_ge(corr_copied, BASE + j)
                                correction(pe, Head(0, j))
                            pe.wait_ge(key_copied, BASE + KEY_AHEAD)
                        for n in range(SCORE_AHEAD):
                            score_tile(pe, *ahead(0, 0, 0, n))
                        pe.wait_ge(s_pad, BASE + vslots)
                        for j in range(FIRST):
                            tensor_step(pe, 0, j, NHEAD, weighed=False)
                        with pe.Fori(0, loops) as i:
                            for j in range(unroll):
                                tensor_step(pe, i, FIRST + j, NHEAD)
                        for j in range(last):
                            tensor_step(pe, loops, FIRST + j, last - 1 - j)
                        for k in range(NT):
                            weigh(pe, Head(loops, FIRST + last - GROUP), k)

                    def mix(v, h, n):
                        score, other = tile_banks(h, n)
                        v.wait_ge(score_mm, BASE + 4 * h.n + n + 1)
                        a, e = fix_cols(n)
                        v.sem_inc(held_off, 1)
                        v.copy_predicated(score[:, a:e], mask[:, 0:e - a], other[:, 0:e - a]).then_inc(fixed, 1)

                    def finish(v, h, n):
                        score, other = tile_banks(h, n)
                        v.wait_ge(fixed, BASE + 4 * h.n + n + 1)
                        if rel:
                            if n == 0:
                                v.wait_ge(band_in[h.slot % 2], BASE + 16 * (h.use(2) + 1))
                            a, e, w = win_cols(n)
                            v.tensor_tensor(score[:, a:e], score[:, a:e], band[h.slot % 2][:, n, w:w + e - a], ALU.add).then_inc(added, 1)
                        else:
                            a, e = mid_cols(n)
                            v.sem_inc(held_off, 1)
                            v.copy_predicated(score[:, a:e], ident[:, 0:e - a].bitcast(U32),
                                              other[:, 128:128 + e - a]).then_inc(mid_fixed, 1)

                    def row_max(v, h, n):
                        score, other = tile_banks(h, n)
                        v.wait_ge(added if rel else mid_fixed, BASE + 4 * h.n + n + 1)
                        if n == 0:
                            v.wait_ge(exped, BASE + 4 * (h.n - 1))
                        v.tensor_reduce(negmax[h.slot % 2][:, n:n + 1], score[:, :], AX.X, ALU.max, negate=True).then_inc(maxed, 1)

                    def key_out(v, h):
                        v.wait_ge(key_mm, BASE + h.n + 1)
                        v.wait_ge(a_written, BASE + 16 * (h.n - 1))
                        v.tensor_copy(keyside[h.slot % 2][:, :], key_bank[:, :]).then_inc(key_copied, 1)

                    @block.vector
                    def _(v):
                        for g in range(vslots):
                            v.memset(vs[g][:, GROUP * NT * VC:], 0.0).then_inc(s_pad, 1)
                        v.wait_ge(s_const, BASE + 32)
                        if rel:
                            for j in range(KEY_AHEAD):
                                key_out(v, Head(0, j))
                        for n in range(SCORE_AHEAD):
                            mix(v, *ahead(0, 0, 0, n))
                            if n:
                                row_max(v, *ahead(0, 0, 0, n - 1))
                            finish(v, *ahead(0, 0, 0, n))

                        def vector_step(i, j, left):
                            for k in range(NT):
                                if left >= (k + SCORE_AHEAD) // NT:
                                    mix(v, *ahead(i, j, k, SCORE_AHEAD))
                                if left >= (k + SCORE_AHEAD - 1) // NT:
                                    row_max(v, *ahead(i, j, k, SCORE_AHEAD - 1))
                                if left >= (k + SCORE_AHEAD) // NT:
                                    finish(v, *ahead(i, j, k, SCORE_AHEAD))
                                if rel and k == 1 and left >= KEY_AHEAD:
                                    key_out(v, Head(i, j + KEY_AHEAD))

                        for j in range(FIRST):
                            vector_step(0, j, NHEAD)
                        with v.Fori(0, loops) as i:
                            for j in range(unroll):
                                vector_step(i, FIRST + j, NHEAD)
                        for j in range(last):
                            vector_step(loops, FIRST + j, last - 1 - j)

                    def exp_tile(act, h, n):
                        act.wait_ge(maxed, BASE + 4 * h.n + n + 1)
                        if n == 0:
                            act.wait_ge(turned, BASE + 4 * (h.n - 1))
                        score, _ = tile_banks(h, n)
                        nc.scalar.activation(prob[h.slot % 2][:, n, :], score[:, :], ACT.Exp,
                                             bias=negmax[h.slot % 2][:, n:n + 1]).then_inc(exped, 1)

                    def copy_turned(act, h, k):
                        act.wait_ge(turned, BASE + 4 * h.n + k + 1)
                        if k == 0:
                            act.wait_ge(pv_mm, BASE + 16 * (h.use(GROUP) - vslots + 1))
                        nc.scalar.copy(probt[h.slot][:, k, :], turned_bank[k][:, :]).then_inc(copied, 1)

                    def group_out(act, h, more):
                        g = h.use(GROUP)
                        hold(act, pv_mm, 16 * (g + 1))
                        if more:
                            act.dma_start(vs[h.slot // GROUP][:, 0:GROUP * NT * VC], values[g + vslots]).then_inc(v_in[h.slot // GROUP], 16)
                        act.wait_ge(out_written, BASE + 16 * g)
                        nc.scalar.copy(outs[:, :], cbank[:, :]).then_inc(out_copied, 1)
                        hold(act, out_copied, g + 1)
                        act.dma_start(heads_out[bass.ts(g, GROUP)], outs[:, :]).then_inc(out_written, 16)

                    def corr_out(act, h):
                        act.wait_ge(corr_mm, BASE + h.n + 1)
                        act.wait_ge(b_written, BASE + 16 * (h.n - 1))
                        nc.scalar.copy(corr[h.slot % 2][:, :, :], corr_bank[:, :].rearrange("p (n r) -> p n r", n=NT)).then_inc(corr_copied, 1)

                    @block.scalar
                    def _(act):
                        if rel:
                            for j in range(CORR_AHEAD):
                                corr_out(act, Head(0, j))
                        for n in range(EXP_AHEAD):
                            exp_tile(act, *ahead(0, 0, 0, n))

                        def scalar_step(i, j, left, weighed=True):
                            own = Head(i, j)
                            for k in range(NT):
                                if left >= (k + EXP_AHEAD) // NT:
                                    exp_tile(act, *ahead(i, j, k, EXP_AHEAD))
                                copy_turned(act, own, k)
                                if k == 1 and weighed and j % GROUP == GROUP - 1:
                                    group_out(act, Head(i, j - j % GROUP - GROUP), left >= GROUP * (vslots - 1))
                            if rel and left >= CORR_AHEAD:
                                corr_out(act, Head(i, j + CORR_AHEAD))

                        for j in range(FIRST):
                            scalar_step(0, j, NHEAD, weighed=False)
                        with act.Fori(0, loops) as i:
                            for j in range(unroll):
                                scalar_step(i, FIRST + j, NHEAD)
                        for j in range(last):
                            scalar_step(loops, FIRST + j, last - 1 - j)
                        group_out(act, Head(loops, FIRST + last - GROUP), False)

        def dense_phase(layer):
            first = layer == 0
            with ExitStack() as ctx:
                def sb(name, shape, dt=F32):
                    return ctx.enter_context(nc.sbuf_tensor(f"d{layer}_{name}", shape, dt))

                def s(name):
                    return sem(f"d{layer}_{name}")

                loads = []

                def const(name, shape, src, dt=F32):
                    tile = sb(name, shape, dt)
                    loads.append((tile, src))
                    return tile

                ident = const("ident", [128, 128], t["ident"])
                wo = const("wo", [C, C], t["WoT"] if first else t["Wo"])
                bo = const("bo", [128, C], (t["bo"] if first else t["bo1"]).partition_broadcast(128))
                if first:
                    w_r, w_k, w_v = (const(n, [C, C], t[n]) for n in ("W_rT", "W_kT", "W_vT"))
                    mu = const("mu", [C, 2], t["mu"])
                    wq, wqs, wk, wv = (const(n, [C, C], t[n]) for n in ("Wq", "Wq_swap", "Wk", "Wv"))
                    uv = const("uv", [C, 3], t["uv"])
                    trig = const("trig", [C, 4, T], t["trig"])
                    uvs = sb("uvs", [C, 3])
                    xt1 = sb("xt1", [C, 1 + T])
                    delta, xr, xk = sb("delta", [C, T]), sb("xr", [C, T]), sb("xk", [C, T])
                    kr, kact, gate = sb("kr", [C, T]), sb("kact", [C, T]), sb("gate", [128, NT, C])
                    x2 = sb("x2", [128, NT, C])
                    xt2 = sb("xt2", [C, T])
                    full = sb("full", [C, 4, T])
                    qv = sb("qv", [C, 2, T])
                    rot = sb("rot", [C, 4, T])
                    left = sb("left", [C, 4, T])
                    part = [sb(f"part{i}", [C, 4 * T + 2], BF16) for i in range(3)]
                    vt = sb("vt", [128, H, NT, VC])
                else:
                    w1, w2 = (const(n, [C, HID], t[n]) for n in ("w1T", "w2T"))
                    h1, h2 = (const(n, [128, KH, HID], t[n].rearrange("(k p) o -> p k o", p=128)) for n in ("h1T", "h2T"))
                    w3 = const("w3", [128, KH, C], t["w3T"].rearrange("(k p) o -> p k o", p=128))
                    fs = const("fs", [128, 4, KH], t["hid_s"])
                    s3 = const("s3", [128, C], t["w3_s"].partition_broadcast(128))
                    xt1 = sb("xt1", [C, 1 + T])
                    silu, ha, hb, hc = (sb(n, [128, KH, T]) for n in ("silu", "ha", "hb", "hc"))
                    x2 = sb("x2", [128, NT, C])
                head_t, sums, head_n = sb("head_t", [C, T]), sb("sums", [C, T]), sb("head_n", [C, T])
                xin, xb, pre, x1 = (sb(n, [128, NT, C]) for n in ("xin", "xb", "pre", "x1"))
                stats, mv = sb("stats", [128, NT, 6]), sb("mv", [128, NT, 2])
                veps, rstd, half = sb("veps", [128, NT]), sb("rstd", [128, NT]), sb("half", [128, NT])
                drop = sb("drop", [128, NT, C])

                c_in, ready, held_off = s("c_in"), s("ready"), s("held_off")
                e = {n: s(n) for n in (
                    "x_in", "head_in", "recip", "normed", "out_mm", "biased", "summed",
                    "st1", "mv1", "ve1", "rs1", "x1", "tr1", "xt1", "f_stored",
                    "st2", "mv2", "ve2", "rs2", "x2", "gated", "added")}
                if first:
                    e |= {n: s(n) for n in ("delta", "mixed", "k_mm", "r_mm", "kr", "kact", "sig", "kv_mm", "tr2", "xt2",
                                            "qk_mm", "v_mm", "qk", "r1", "r2", "rot", "hi", "left", "mid", "lo", "vt", "written")}
                else:
                    e |= {n: s(n) for n in ("w1_mm", "w2_mm", "silu", "ha", "h1_mm", "hb", "h2_mm", "hc", "o_mm")}

                def norm_vector(v, b, src, dst, i):
                    for n in range(NT):
                        last = v.bn_stats(stats[:, n, :], src[:, n, :])
                    last.then_inc(e[f"st{i}"], 1)
                    v.wait_ge(e[f"st{i}"], BASE + b + 1)
                    v.sem_inc(held_off, 1)
                    for n in range(NT):
                        last = v.bn_aggr(mv[:, n, :], stats[:, n, :])
                    last.then_inc(e[f"mv{i}"], 1)
                    v.wait_ge(e[f"rs{i}"], BASE + b + 1)
                    for n in range(NT):
                        last = v.tensor_scalar(dst[:, n, :], src[:, n, :], mv[:, n, 0:1], rstd[:, n:n + 1], ALU.subtract, ALU.mult)
                    last.then_inc(e[f"x{i}"], 1)

                def norm_pool(p, b, i):
                    p.wait_ge(e[f"mv{i}"], BASE + b + 1)
                    p.sem_inc(held_off, 1)
                    p.tensor_scalar(veps[:, :], mv[:, :, 1], EPS, None, ALU.add).then_inc(e[f"ve{i}"], 1)
                    p.wait_ge(e[f"ve{i}"], BASE + b + 1)
                    p.tensor_tensor(rstd[:, :], veps[:, :], half[:, :], ALU.pow).then_inc(e[f"rs{i}"], 1)

                def flip(pe, dst, src, event):
                    for n in range(NT):
                        last = pe.transpose(dst[:, n * 128:(n + 1) * 128], src[:, n, :], ident[:, :])
                    last.then_inc(event, 1)

                def by_token(pe, dst, src, w, event):
                    for n in range(NT):
                        last = pe.matmul(dst[:, n * 128:(n + 1) * 128], src[:, n * 128:(n + 1) * 128], w, start=True, stop=True)
                    last.then_inc(event, 1)

                n_written = 5 * NTERM + 1
                uvs_in, fill = s("uvs_in"), s("fill")

                start_phase()
                with nc.Block() as block:
                    @block.sync
                    def _(sp):
                        for tile, src in loads:
                            dst = tile[:, :] if len(tile.shape) == 2 else tile[:, :, :]
                            sp.dma_start(dst, src).then_inc(c_in, 16)
                        with sp.Fori(0, B) as b:
                            sp.wait_ge(e["normed"], BASE + b)
                            sp.sem_inc(held_off, 1)
                            sp.wait_ge(e["biased"], BASE + b)
                            sp.sem_inc(held_off, 1)
                            own = bass.ts(b, H)
                            sp.dma_start(head_t[:, :], heads_out[own, 0:DH, :]).then_inc(e["head_in"], 16)
                            rep = bass.AP(heads_out.tensor, (b * H) * (VW * T) + DH * T, [[VW * T, H], [0, DH], [1, T]])
                            sp.dma_start(sums[:, :], rep).then_inc(e["head_in"], 16)
                            old = t["x"][b] if first else resid[b]
                            sp.dma_start(xin[:, :, :], old.rearrange("(n p) c -> p n c", p=128)).then_inc(e["x_in"], 16)
                            sp.wait_ge(e["x2"], BASE + b + 1)
                            sp.sem_inc(held_off, 1)
                            new = resid[b] if first else t["out"][b]
                            sp.dma_start(new.rearrange("(n p) c -> p n c", p=128), x2[:, :, :]).then_inc(e["f_stored"], 16)
                            if first:
                                sp.wait_ge(e["lo"], BASE + b + 1)
                                sp.sem_inc(held_off, 1)
                                for j in range(NTERM):
                                    content, pos = slice(DH * j, DH * j + DH), slice(SR + DH * j, SR + DH * j + DH)
                                    st, q = stack[1], part[Q_PART[j]]
                                    sp.dma_start(st[own, content, 0, :], part[K_PART[j]][:, 0:T]).then_inc(e["written"], 16)
                                    sp.dma_start(st[own, content, 1, :], q[:, T:2 * T]).then_inc(e["written"], 16)
                                    sp.dma_start(st[own, content, 2, :], q[:, T:2 * T]).then_inc(e["written"], 16)
                                    sp.dma_start(st[own, pos, 1, :], q[:, 2 * T:3 * T]).then_inc(e["written"], 16)
                                    sp.dma_start(st[own, pos, 2, :], q[:, 3 * T + 1:4 * T + 1]).then_inc(e["written"], 16)
                                sp.wait_ge(e["vt"], BASE + b + 1)
                                sp.sem_inc(held_off, 1)
                                sp.dma_start(values[bass.ts(b, H // GROUP)].rearrange("g p c -> p g c"),
                                         vt[:, :, :, :].rearrange("p (g h) n c -> p g (h n c)", h=GROUP)).then_inc(e["written"], 16)
                        sp.wait_ge(e["f_stored"], BASE + 16 * B)
                        if first:
                            sp.wait_ge(e["written"], BASE + 16 * n_written * B)

                    @block.tensor
                    def _(pe):
                        pe.wait_ge(c_in, BASE + 16 * len(loads))
                        with pe.Fori(0, B) as b:
                            pe.wait_ge(e["normed"], BASE + b + 1)
                            if first:
                                pe.wait_ge(e["qk"], BASE + b)
                            else:
                                pe.wait_ge(e["gated"], BASE + b)
                            by_token(pe, bank[0], head_n, wo[:, :], e["out_mm"])
                            pe.wait_ge(e["x1"], BASE + b + 1)
                            if first:
                                flip(pe, bank[1], x1, e["tr1"])
                                pe.wait_ge(e["mixed"], BASE + b + 1)
                                pe.matmul(bank[2][:, :], w_k[:, :], xk[:, :], start=True, stop=True).then_inc(e["k_mm"], 1)
                                pe.wait_ge(e["vt"], BASE + b)
                                by_token(pe, bank[3], xr, w_r[:, :], e["r_mm"])
                                pe.wait_ge(e["kact"], BASE + b + 1)
                                by_token(pe, bank[4], kact, w_v[:, :], e["kv_mm"])
                                pe.wait_ge(e["x2"], BASE + b + 1)
                                flip(pe, bank[5], x2, e["tr2"])
                                pe.wait_ge(e["xt2"], BASE + b + 1)
                                pe.matmul(bank[2][:, :], wk[:, :], xt2[:, :], start=True, stop=True)
                                pe.matmul(bank[0][:, :], wq[:, :], xt2[:, :], start=True, stop=True)
                                pe.matmul(bank[1][:, :], wqs[:, :], xt2[:, :], start=True, stop=True).then_inc(e["qk_mm"], 1)
                                by_token(pe, bank[3], xt2, wv[:, :], e["v_mm"])
                            else:
                                flip(pe, bank[7], x1, e["tr1"])
                                pe.wait_ge(e["xt1"], BASE + b + 1)
                                for m in range(KH):
                                    col = slice(128 * m, 128 * m + 128)
                                    pe.matmul(bank[m][:, :], w1[:, col], xt1[:, 1:1 + T], start=True, stop=True).then_inc(e["w1_mm"], 1)
                                    pe.matmul(bank[4 + m][:, :], w2[:, col], xt1[:, 1:1 + T], start=True, stop=True).then_inc(e["w2_mm"], 1)
                                pe.wait_ge(e["ha"], BASE + KH * b + KH)
                                for m in range(KH):
                                    for k in range(KH):
                                        last = pe.matmul(bank[m][:, :], h1[:, k, 128 * m:128 * m + 128], ha[:, k, :],
                                                         start=(k == 0), stop=(k == KH - 1))
                                    last.then_inc(e["h1_mm"], 1)
                                pe.wait_ge(e["hb"], BASE + KH * b + KH)
                                for m in range(KH):
                                    for k in range(KH):
                                        last = pe.matmul(bank[4 + m][:, :], h2[:, k, 128 * m:128 * m + 128], hb[:, k, :],
                                                         start=(k == 0), stop=(k == KH - 1))
                                    last.then_inc(e["h2_mm"], 1)
                                pe.wait_ge(e["hc"], BASE + KH * b + KH)
                                for n in range(NT):
                                    for k in range(KH):
                                        last = pe.matmul(bank[0][:, n * 128:(n + 1) * 128], hc[:, k, n * 128:(n + 1) * 128], w3[:, k, :],
                                                         start=(k == 0), stop=(k == KH - 1))
                                last.then_inc(e["o_mm"], 1)

                    @block.gpsimd
                    def _(p):
                        p.memset(half[:, :], -0.5).then_inc(ready, 1)
                        p.wait_ge(ready, BASE + 1)
                        with p.Fori(0, B) as b:
                            norm_pool(p, b, 1)
                            norm_pool(p, b, 2)
                            if first:
                                p.wait_ge(e["qk"], BASE + b + 1)
                                p.tensor_tensor(rot[:, 1, :], qv[:, 1, :], trig[:, 1, :], ALU.mult)
                                p.tensor_tensor(rot[:, 3, :], qv[:, 1, :], trig[:, 3, :], ALU.mult).then_inc(e["r1"], 1)

                    @block.scalar
                    def _(act):
                        act.wait_ge(c_in, BASE + 16 * len(loads))
                        if first:
                            nc.scalar.activation(uvs[:, :], uv[:, :], ACT.Identity, scale=SCALE[1]).then_inc(uvs_in, 1)
                            act.wait_ge(uvs_in, BASE + 1)
                        with act.Fori(0, B) as b:
                            act.wait_ge(e["tr1"], BASE + b + 1)
                            nc.scalar.copy(xt1[:, 1:1 + T], bank[1 if first else 7][:, :]).then_inc(e["xt1"], 1)
                            if first:
                                act.wait_ge(e["r_mm"], BASE + b + 1)
                                nc.scalar.activation(gate[:, :, :], bank[3][:, :].rearrange("p (n c) -> p n c", n=NT),
                                                     ACT.Sigmoid).then_inc(e["sig"], 1)
                                act.wait_ge(e["kr"], BASE + b + 1)
                                nc.scalar.activation(kact[:, :], kr[:, :], ACT.Square).then_inc(e["kact"], 1)
                                act.wait_ge(e["tr2"], BASE + b + 1)
                                nc.scalar.copy(xt2[:, :], bank[5][:, :]).then_inc(e["xt2"], 1)
                                act.wait_ge(e["qk_mm"], BASE + b + 1)
                                nc.scalar.copy(full[:, 0, :], bank[2][:, :])
                                nc.scalar.activation(full[:, 1, :], bank[0][:, :], ACT.Identity, bias=uvs[:, 0:1], scale=SCALE[1])
                                nc.scalar.activation(qv[:, 0, :], bank[0][:, :], ACT.Identity, bias=uvs[:, 1:2], scale=SCALE[1])
                                nc.scalar.activation(qv[:, 1, :], bank[1][:, :], ACT.Identity, bias=uvs[:, 2:3],
                                                     scale=SCALE[1]).then_inc(e["qk"], 1)
                                act.wait_ge(e["qk"], BASE + b + 1)
                                act.wait_ge(e["rot"], BASE + b + 1)
                                act.wait_ge(e["written"], BASE + 16 * n_written * b)
                                nc.scalar.copy(part[0][:, 0:4 * T], full[:, :, :].rearrange("p a t -> p (a t)")).then_inc(e["hi"], 1)
                            else:
                                for m in range(KH):
                                    act.wait_ge(e["w1_mm"], BASE + KH * b + m + 1)
                                    nc.scalar.activation(silu[:, m, :], bank[m][:, :], ACT.Silu, scale=fs[:, 0, m:m + 1]).then_inc(e["silu"], 1)
                                for m in range(KH):
                                    act.wait_ge(e["h1_mm"], BASE + KH * b + m + 1)
                                    nc.scalar.activation(hb[:, m, :], bank[m][:, :], ACT.Gelu, scale=fs[:, 2, m:m + 1]).then_inc(e["hb"], 1)
                                for m in range(KH):
                                    act.wait_ge(e["h2_mm"], BASE + KH * b + m + 1)
                                    nc.scalar.activation(hc[:, m, :], bank[4 + m][:, :], ACT.Gelu, scale=fs[:, 3, m:m + 1]).then_inc(e["hc"], 1)

                    @block.vector
                    def _(v):
                        if first:
                            v.memset(xt1[:, 0:1], 0.0).then_inc(fill, 1)
                            v.memset(vt[:, :, :, DH:VC], 1.0).then_inc(fill, 1)
                            for i in range(3):
                                v.memset(part[i][:, 4 * T:4 * T + 2], 0.0).then_inc(fill, 1)
                            v.wait_ge(fill, BASE + 5)
                        v.wait_ge(c_in, BASE + 16 * len(loads))
                        with v.Fori(0, B) as b:
                            v.wait_ge(e["head_in"], BASE + 32 * b + 32)
                            v.reciprocal(sums[:, :], sums[:, :]).then_inc(e["recip"], 1)
                            v.wait_ge(e["recip"], BASE + b + 1)
                            v.tensor_tensor(head_n[:, :], head_t[:, :], sums[:, :], ALU.mult).then_inc(e["normed"], 1)
                            v.wait_ge(e["x_in"], BASE + 16 * b + 16)
                            for n in range(NT):
                                last = v.tensor_tensor(xb[:, n, :], xin[:, n, :], bo[:, :], ALU.add)
                            last.then_inc(e["biased"], 1)
                            v.wait_ge(e["biased"], BASE + b + 1)
                            v.wait_ge(e["out_mm"], BASE + b + 1)
                            v.tensor_tensor(pre[:, :, :], bank[0][:, :].rearrange("p (n c) -> p n c", n=NT), xb[:, :, :],
                                            ALU.add).then_inc(e["summed"], 1)
                            v.wait_ge(e["summed"], BASE + b + 1)
                            norm_vector(v, b, pre, x1, 1)
                            if first:
                                v.wait_ge(e["xt1"], BASE + b + 1)
                                v.tensor_tensor(delta[:, :], xt1[:, 1:1 + T], xt1[:, 0:T], ALU.subtract).then_inc(e["delta"], 1)
                                v.wait_ge(e["delta"], BASE + b + 1)
                                v.scalar_tensor_tensor(out=xk[:, :], in0=delta[:, :], scalar=mu[:, 1:2], in1=xt1[:, 0:T],
                                                       op0=ALU.mult, op1=ALU.add)
                                v.scalar_tensor_tensor(out=xr[:, :], in0=delta[:, :], scalar=mu[:, 0:1], in1=xt1[:, 0:T],
                                                       op0=ALU.mult, op1=ALU.add).then_inc(e["mixed"], 1)
                                v.wait_ge(e["k_mm"], BASE + b + 1)
                                v.tensor_scalar(kr[:, :], bank[2][:, :], 0.0, None, ALU.max).then_inc(e["kr"], 1)
                                v.wait_ge(e["sig"], BASE + b + 1)
                                v.wait_ge(e["kv_mm"], BASE + b + 1)
                                v.tensor_tensor(drop[:, :, :], bank[4][:, :].rearrange("p (n c) -> p n c", n=NT), gate[:, :, :],
                                                ALU.mult).then_inc(e["gated"], 1)
                            else:
                                for m in range(KH):
                                    v.wait_ge(e["w2_mm"], BASE + KH * b + m + 1)
                                    v.wait_ge(e["silu"], BASE + KH * b + m + 1)
                                    v.scalar_tensor_tensor(out=ha[:, m, :], in0=bank[4 + m][:, :], scalar=fs[:, 1, m:m + 1],
                                                           in1=silu[:, m, :], op0=ALU.mult, op1=ALU.mult).then_inc(e["ha"], 1)
                                v.wait_ge(e["o_mm"], BASE + b + 1)
                                for n in range(NT):
                                    last = v.tensor_tensor(drop[:, n, :], bank[0][:, n * 128:(n + 1) * 128], s3[:, :], ALU.mult)
                                last.then_inc(e["gated"], 1)
                            v.wait_ge(e["gated"], BASE + b + 1)
                            v.tensor_tensor(pre[:, :, :], drop[:, :, :], x1[:, :, :], ALU.add).then_inc(e["added"], 1)
                            v.wait_ge(e["added"], BASE + b + 1)
                            v.wait_ge(e["f_stored"], BASE + 16 * b)
                            norm_vector(v, b, pre, x2, 2)
                            if first:
                                v.wait_ge(e["v_mm"], BASE + b + 1)
                                v.wait_ge(e["written"], BASE + 16 * n_written * b)
                                for n in range(NT):
                                    last = v.tensor_copy(vt[:, :, n, 0:DH],
                                                         bank[3][:, n * 128:(n + 1) * 128].rearrange("p (h d) -> p h d", d=DH))
                                last.then_inc(e["vt"], 1)
                                v.wait_ge(e["qk"], BASE + b + 1)
                                v.tensor_tensor(rot[:, 0, :], qv[:, 0, :], trig[:, 0, :], ALU.mult)
                                v.tensor_tensor(rot[:, 2, :], qv[:, 0, :], trig[:, 2, :], ALU.mult).then_inc(e["r2"], 1)
                                v.wait_ge(e["r2"], BASE + b + 1)
                                v.wait_ge(e["r1"], BASE + b + 1)
                                v.tensor_tensor(full[:, 2, :], rot[:, 0, :], rot[:, 1, :], ALU.add)
                                v.tensor_tensor(full[:, 3, :], rot[:, 2, :], rot[:, 3, :], ALU.add).then_inc(e["rot"], 1)
                                v.wait_ge(e["hi"], BASE + b + 1)
                                flat = full[:, :, :].rearrange("p a t -> p (a t)")
                                lf = left[:, :, :].rearrange("p a t -> p (a t)")
                                v.tensor_tensor(lf, flat, part[0][:, 0:4 * T], ALU.subtract).then_inc(e["left"], 1)
                                v.wait_ge(e["left"], BASE + b + 1)
                                v.tensor_copy(part[1][:, 0:4 * T], lf).then_inc(e["mid"], 1)
                                v.wait_ge(e["mid"], BASE + b + 1)
                                v.tensor_tensor(part[2][:, 0:4 * T], lf, part[1][:, 0:4 * T], ALU.subtract).then_inc(e["lo"], 1)

        tables_phase()
        end_phase()
        attention_phase(0)
        end_phase()
        dense_phase(0)
        end_phase()
        attention_phase(1)
        end_phase()
        dense_phase(1)


def _tables(np):
    k = np.arange(T, dtype=np.float64)
    freq = (1.0 / np.float32(10000.0) ** (np.arange(0, DH, 2, dtype=np.float32) / np.float32(DH))).astype(np.float64)
    sin, cos = (lambda p: np.sin(p[None, :] * freq[:, None])), (lambda p: np.cos(p[None, :] * freq[:, None]))
    own = [np.concatenate([sin(p), sin(p)]) for p in (k, k + T)]
    swap = [np.concatenate([cos(p), -cos(p)]) for p in (k, k + T)]
    trig = np.stack([own[0], swap[0], own[1], swap[1]], 1)
    key = np.concatenate([cos(k), sin(k)]).astype(np.float32)
    bits = []
    left = key.copy()
    for _ in range(3):
        u = left.view(np.uint32)
        r = ((u + np.uint32(0x7FFF) + ((u >> 16) & 1)) >> 16).astype(np.uint32)
        bits.append(r.astype(np.uint16))
        left = left - (r << 16).astype(np.uint32).view(np.float32)
    p, c = np.arange(128)[:, None], np.arange(128)[None, :]
    block = -(np.arange(C)[:, None] // DH == np.arange(H)[None, :]).astype(np.float32)
    return {
        "ident": np.eye(128, dtype=np.float32), "mask0": (c >= p).astype(np.uint32), "mask1": (c >= p + 2).astype(np.uint32),
        "negblock": block, "trig": np.ascontiguousarray(np.tile(trig, (H, 1, 1)).astype(np.float32)),
        "poskey": np.stack(bits),
    }


def kernel(**inputs):
    import numpy as np
    import concourse.bacc as bacc
    from concourse.bass_utils import run_bass_kernel_spmd

    a = {n: np.asarray(v) for n, v in inputs.items()}
    L0, F0, L1, F1 = "L0_attn_", "L0_ffn_", "L1_attn_", "L1_ffn_"
    swap = (np.arange(C) // DH) * DH + (np.arange(C) + DH // 2) % DH

    def tr(x):
        return np.ascontiguousarray(x.T)

    def col(x):
        return np.ascontiguousarray(x.reshape(C, 1))

    arrays = {
        "x": a[L0 + "x"], "xT": np.ascontiguousarray(a[L0 + "x"].transpose(0, 2, 1)),
        "WqT": tr(a[L0 + "Wq"]), "WkT": tr(a[L0 + "Wk"]), "WvT": tr(a[L0 + "Wv"]), "WoT": tr(a[L0 + "Wo"]),
        "WpkT": tr(a[L0 + "Wpk"]), "WpqT": tr(a[L0 + "Wpq"]), "relT": tr(a[L0 + "rel_emb"]),
        "bq": col(a[L0 + "bq"]), "bk": col(a[L0 + "bk"]), "bpk": col(a[L0 + "bpk"]), "bpq": col(a[L0 + "bpq"]),
        "bv": a[L0 + "bv"], "bo": a[L0 + "bo"],
        "W_rT": tr(a[F0 + "W_r"]), "W_kT": tr(a[F0 + "W_k"]), "W_vT": tr(a[F0 + "W_v"]),
        "mu": np.ascontiguousarray(np.stack([a[F0 + "mu_r"], a[F0 + "mu_k"]], 1)),
        "Wq": a[L1 + "Wq"], "Wq_swap": np.ascontiguousarray(a[L1 + "Wq"][:, swap]), "Wk": a[L1 + "Wk"], "Wv": a[L1 + "Wv"],
        "Wo": a[L1 + "Wo"], "bo1": a[L1 + "bo"],
        "uv": np.ascontiguousarray(np.stack([a[L1 + "u"].reshape(C), a[L1 + "v"].reshape(C), a[L1 + "v"].reshape(C)[swap]], 1)),
        "w1T": tr(a[F1 + "w1_w"]), "w2T": tr(a[F1 + "w2_w"]), "h1T": tr(a[F1 + "h1_w"]), "h2T": tr(a[F1 + "h2_w"]),
        "w3T": tr(a[F1 + "w3_w"]), "w3_s": a[F1 + "w3_s"],
        "hid_s": np.ascontiguousarray(np.stack([a[F1 + n].reshape(KH, 128) for n in ("w1_s", "w2_s", "h1_s", "h2_s")], 0)
                                      .transpose(2, 0, 1)),
    }
    arrays.update(_tables(np))
    nc = bacc.Bacc("TRN2", target_bir_lowering=False, num_devices=1)
    t = {}
    for n, v in arrays.items():
        dt = BF16 if n == "poskey" else mybir.dt.from_np(v.dtype)
        if n == "poskey":
            t[n] = nc.dram_tensor("in_" + n, v.shape, mybir.dt.uint16, kind="ExternalInput").ap().bitcast(BF16)
        else:
            t[n] = nc.dram_tensor("in_" + n, v.shape, dt, kind="ExternalInput").ap()
    t["out"] = nc.dram_tensor("out_0", (B, T, C), F32, kind="ExternalOutput").ap()
    build(nc, t)
    r = run_bass_kernel_spmd(nc, [{"in_" + n: v for n, v in arrays.items()}], core_ids=[0])
    return r.results[0]["out_0"]
```

```python
from contextlib import ExitStack

import concourse.bass as bass
from concourse import mybir

F32 = mybir.dt.float32
BF16 = mybir.dt.bfloat16
U32 = mybir.dt.uint32
ALU = mybir.AluOpType
ACT = mybir.ActivationFunctionType
AX = mybir.AxisListType

B, T, C = 8, 512, 128
H = 16
DH = C // H
NT = T // 128
NHEAD = B * H
SPAN = 64
REL = 2 * SPAN
HID = 512
KH = HID // 128
EPS = 1e-5
Q_PART = [0, 0, 0, 1, 1, 2]
K_PART = [0, 1, 2, 0, 1, 0]
NTERM = len(Q_PART)
TERM_RUNS = [(0, 3, 0), (3, 2, 1), (5, 1, 2)]
SR = NTERM * DH
R0 = SR + 3
R1 = 2 * SR
KHI, KLO, QLO, QHI = range(4)
GROUP = 4
NG = NHEAD // GROUP
UNROLL = {0: 8, 1: 12}
FIRST = GROUP
SCORE_AHEAD, EXP_AHEAD = 6, 4
CORR_AHEAD, KEY_AHEAD, LOAD_AHEAD = 4, 6, 7
PITCH_A = SPAN + T + SPAN
PITCH_B = 3 * REL
WIN = 2 * REL
VC = DH + 1
VW = 32
BASE = 32

SCALE = {0: (3 * DH) ** -0.5, 1: DH ** -0.5}


def build(nc, t):
    top = ExitStack()
    with top:
        sems, held = {}, ExitStack()

        def sem(name):
            if name not in sems:
                sems[name] = held.enter_context(nc.semaphore(name))
            return sems[name]

        def start_phase():
            with nc.Block() as block:
                @block.sync
                def _(sp):
                    for handle in sems.values():
                        sp.sem_inc(handle, BASE)

        def end_phase():
            with nc.Block() as block:
                @block.sync
                def _(sp):
                    for handle in sems.values():
                        sp.sem_clear(handle)
            held.close()
            sems.clear()

        bank = [top.enter_context(nc.psum_tensor(f"bank{i}", [128, 512], F32)) for i in range(8)]

        def dram(name, shape, dt):
            return nc.dram_tensor(name, shape, dt, kind="Internal").ap()

        stack = {0: dram("stack0", [B, NTERM, C, 4, T], BF16), 1: dram("stack1", [B, NTERM, C, 4, T], BF16)}
        consts = dram("consts", [H, R0 - SR, 4, T], BF16)
        values = dram("values", [NG, 128, GROUP * NT * VC], F32)
        table = dram("table", [H, R0, 2 * REL], BF16)
        heads_out = dram("heads_out", [NHEAD, VW, T], F32)
        resid = dram("resid", [B, T, C], F32)
        shear_a = dram("shear_a", [4, 128, PITCH_A], F32)
        shear_b = dram("shear_b", [4, T, PITCH_B], F32)

        def tables_phase():
            with ExitStack() as ctx:
                def sb(name, shape, dt=F32):
                    return ctx.enter_context(nc.sbuf_tensor(name, shape, dt))

                wpk, wpq, relt = sb("wpk", [C, C]), sb("wpq", [C, C]), sb("relt", [C, REL])
                cols = sb("cols", [C, 4])
                sc = sb("sc", [C, 2])
                negblock = sb("negblock", [C, H])
                pk, pq = sb("pk", [C, REL]), sb("pq", [C, REL])
                d = sb("d", [C, 2, REL])
                e = sb("e", [C, REL + 1])
                e1 = sb("e1", [C, REL + 1])
                kc = sb("kc", [H, REL + T])
                parts = [sb(f"dp{i}", [C, 2, REL], BF16) for i in range(3)]
                kparts = [sb(f"kp{i}", [H, REL + T], BF16) for i in range(3)]
                rest, krest = sb("rest", [C, 2, REL]), sb("krest", [H, REL + T])
                ones, zeros = sb("ones", [SR, T], BF16), sb("zeros", [128, T], BF16)
                zf = sb("zf", [128, REL])
                bias = sb("bias", [C, 4])
                s_in, s_ps, s_pk, s_col, s_d = (sem(n) for n in ("tab_in", "tab_ps", "tab_pk", "tab_col", "tab_d"))
                s_e, s_kps, s_kc, s_part, s_out = (sem(n) for n in ("tab_e", "tab_kps", "tab_kc", "tab_part", "tab_out"))
                s_fill = sem("tab_fill")

                start_phase()
                with nc.Block() as block:
                    @block.sync
                    def _(sp):
                        for dst, src in ((wpk, t["WpkT"]), (wpq, t["WpqT"]), (relt, t["relT"]), (negblock, t["negblock"])):
                            sp.dma_start(dst[:, :], src).then_inc(s_in, 16)
                        for i, n in enumerate(("bq", "bk", "bpk", "bpq")):
                            sp.dma_start(cols[:, i:i + 1], t[n]).then_inc(s_in, 16)
                        sp.wait_ge(s_fill, BASE + 3)
                        zeros_of = lambda many, width: bass.AP(zf[:, :].tensor, 0, [[REL, 128], [0, many], [1, width]])
                        for at in (0, SPAN + T):
                            sp.dma_start(shear_a[:, :, at:at + SPAN].rearrange("s p c -> p s c"), zeros_of(4, SPAN)).then_inc(s_out, 16)
                        rows_b = shear_b.rearrange("s (n p) c -> p (s n) c", p=128)
                        for at in (0, 2 * REL):
                            sp.dma_start(rows_b[:, :, at:at + REL], zeros_of(4 * NT, REL)).then_inc(s_out, 16)
                        sp.wait_ge(s_part, BASE + 1)
                        for j in range(NTERM):
                            rows = slice(DH * j, DH * j + DH)
                            sp.dma_start(table[:, rows, 0:REL], parts[Q_PART[j]][:, 0, :]).then_inc(s_out, 16)
                            sp.dma_start(table[:, rows, REL:2 * REL], parts[K_PART[j]][:, 1, :]).then_inc(s_out, 16)
                        for i in range(3):
                            sp.dma_start(table[:, SR + i, 0:REL], kparts[i][:, 0:REL]).then_inc(s_out, 16)
                            sp.dma_start(table[:, SR + i, REL:2 * REL], zeros[0:H, 0:REL]).then_inc(s_out, 16)
                        sp.dma_start(consts[:, :, KLO, :], ones[:, :]).then_inc(s_out, 16)
                        sp.dma_start(consts[:, :, KHI, :], ones[:, :]).then_inc(s_out, 16)
                        sp.dma_start(consts[:, :, QLO, :], zeros[0:SR, :]).then_inc(s_out, 16)
                        for i in range(3):
                            sp.dma_start(consts[:, i, QHI, :], kparts[i][:, REL:REL + T]).then_inc(s_out, 16)
                        n_out = 4 + 2 * NTERM + 6 + 6
                        sp.wait_ge(s_out, BASE + 16 * n_out)

                    @block.tensor
                    def _(pe):
                        pe.wait_ge(s_in, BASE + 16 * 8)
                        pe.matmul(bank[0][:, 0:REL], wpk[:, :], relt[:, :], start=True, stop=True).then_inc(s_ps, 1)
                        pe.matmul(bank[1][:, 0:REL], wpq[:, :], relt[:, :], start=True, stop=True).then_inc(s_ps, 1)
                        pe.wait_ge(s_e, BASE + 4)
                        pe.matmul(bank[2][0:H, 0:REL + 1], negblock[:, :], e[:, :], start=True, stop=True).then_inc(s_kps, 1)

                    @block.scalar
                    def _(act):
                        act.wait_ge(s_in, BASE + 16 * 8)
                        nc.scalar.activation(sc[:, 0:1], cols[:, 0:1], ACT.Identity, scale=SCALE[0]).then_inc(s_col, 1)
                        nc.scalar.activation(sc[:, 1:2], cols[:, 3:4], ACT.Identity, scale=SCALE[0]).then_inc(s_col, 1)
                        act.wait_ge(s_ps, BASE + 2)
                        nc.scalar.activation(pk[:, :], bank[0][:, 0:REL], ACT.Identity, bias=cols[:, 2:3]).then_inc(s_pk, 1)
                        act.wait_ge(s_col, BASE + 2)
                        nc.scalar.activation(pq[:, :], bank[1][:, 0:REL], ACT.Identity, bias=sc[:, 1:2], scale=SCALE[0]).then_inc(s_pk, 1)

                    @block.vector
                    def _(v):
                        last = REL - 1
                        v.memset(ones[:, :], 1.0).then_inc(s_fill, 1)
                        v.memset(zeros[:, :], 0.0).then_inc(s_fill, 1)
                        v.memset(zf[:, :], 0.0).then_inc(s_fill, 1)
                        v.wait_ge(s_pk, BASE + 2)
                        v.tensor_tensor(bias[:, QLO:QLO + 1], sc[:, 0:1], pq[:, 0:1], ALU.add).then_inc(s_d, 1)
                        v.tensor_tensor(bias[:, QHI:QHI + 1], sc[:, 0:1], pq[:, last:REL], ALU.add).then_inc(s_d, 1)
                        v.tensor_tensor(bias[:, KLO:KLO + 1], cols[:, 1:2], pk[:, 0:1], ALU.add).then_inc(s_d, 1)
                        v.tensor_tensor(bias[:, KHI:KHI + 1], cols[:, 1:2], pk[:, last:REL], ALU.add).then_inc(s_d, 1)
                        v.tensor_scalar(d[:, 0, :], pq[:, :], pq[:, 0:1], None, ALU.subtract).then_inc(s_d, 1)
                        v.tensor_scalar(d[:, 1, :], pk[:, :], pk[:, 0:1], None, ALU.subtract).then_inc(s_d, 1)
                        v.wait_ge(s_d, BASE + 6)
                        v.tensor_scalar(e1[:, 0:REL], d[:, 1, :], pq[:, 0:1], None, ALU.mult).then_inc(s_e, 1)
                        v.tensor_tensor(e1[:, REL:REL + 1], pq[:, 0:1], pk[:, 0:1], ALU.mult).then_inc(s_e, 1)
                        v.wait_ge(s_e, BASE + 2)
                        v.scalar_tensor_tensor(out=e[:, 0:REL], in0=d[:, 0, :], scalar=pk[:, 0:1], in1=e1[:, 0:REL],
                                               op0=ALU.mult, op1=ALU.add).then_inc(s_e, 1)
                        v.scalar_tensor_tensor(out=e[:, REL:REL + 1], in0=pq[:, last:REL], scalar=pk[:, last:REL],
                                               in1=e1[:, REL:REL + 1], op0=ALU.mult, op1=ALU.subtract).then_inc(s_e, 1)
                        v.wait_ge(s_kps, BASE + 1)
                        v.tensor_copy(kc[:, 0:REL], bank[2][0:H, 0:REL]).then_inc(s_kc, 1)
                        v.tensor_scalar(kc[:, REL:REL + T], zeros[0:H, :], bank[2][0:H, REL:REL + 1], None, ALU.add).then_inc(s_kc, 1)
                        v.wait_ge(s_kc, BASE + 2)
                        v.tensor_copy(parts[0][:, :, :], d[:, :, :]).then_inc(s_kc, 1)
                        v.tensor_copy(kparts[0][:, :], kc[:, :]).then_inc(s_kc, 1)
                        v.wait_ge(s_kc, BASE + 4)
                        v.tensor_tensor(rest[:, :, :], d[:, :, :], parts[0][:, :, :], ALU.subtract).then_inc(s_kc, 1)
                        v.tensor_tensor(krest[:, :], kc[:, :], kparts[0][:, :], ALU.subtract).then_inc(s_kc, 1)
                        v.wait_ge(s_kc, BASE + 6)
                        v.tensor_copy(parts[1][:, :, :], rest[:, :, :]).then_inc(s_kc, 1)
                        v.tensor_copy(kparts[1][:, :], krest[:, :]).then_inc(s_kc, 1)
                        v.wait_ge(s_kc, BASE + 8)
                        v.tensor_tensor(parts[2][:, :, :], rest[:, :, :], parts[1][:, :, :], ALU.subtract)
                        v.tensor_tensor(kparts[2][:, :], krest[:, :], kparts[1][:, :], ALU.subtract).then_inc(s_part, 1)

                wq, wk, wv = sb("wq", [C, C]), sb("wk", [C, C]), sb("wv", [C, C])
                bv = sb("bv", [128, C])
                xt = [sb(f"xt{i}", [C, T]) for i in range(2)]
                full = [sb(f"full{i}", [C, 4, T]) for i in range(2)]
                part = [sb(f"part{i}", [C, 3, 4, T], BF16) for i in range(2)]
                left = [sb(f"left{i}", [C, 4, T]) for i in range(2)]
                vt = [sb(f"vt{i}", [128, H, NT, VC]) for i in range(2)]
                n_out = 2 * len(TERM_RUNS) + 1
                end_phase()
                w_in, p_ps, v_ps = sem("p0_w"), sem("p0_ps"), sem("p0_vps")
                p_full, p_hi, p_rest, p_mid, p_lo = (sem(n) for n in ("p0_full", "p0_hi", "p0_rest", "p0_mid", "p0_lo"))
                p_v, p_vone, held_off = sem("p0_v"), sem("p0_vone"), sem("held_off")
                x_in, p_out = ([sem(f"p0_{n}{i}") for i in range(2)] for n in ("x", "out"))
                start_phase()
                with nc.Block() as block:
                    @block.sync
                    def _(sp):
                        def load(b, p):
                            sp.dma_start(xt[p][:, :], t["xT"][b]).then_inc(x_in[p], 16)

                        def step(i, p, more):
                            b = 2 * i + p
                            sp.wait_ge(p_v, BASE + b + 1)
                            sp.sem_inc(held_off, 1)
                            sp.dma_start(values[bass.ts(b, H // GROUP)].rearrange("g p c -> p g c"),
                                         vt[p][:, :, :, :].rearrange("p (g h) n c -> p g (h n c)", h=GROUP)).then_inc(p_out[p], 16)
                            if more:
                                sp.wait_ge(p_ps, BASE + 2 * b + 2)
                                sp.sem_inc(held_off, 1)
                                load(b + 2, p)
                            sp.wait_ge(p_lo, BASE + b + 1)
                            sp.sem_inc(held_off, 1)
                            for first, n, q in TERM_RUNS:
                                dst = stack[0][b, first:first + n].rearrange("j c a t -> c j a t")
                                sp.dma_start(dst[:, :, KHI:KLO + 1, :].rearrange("c j a t -> c j (a t)"),
                                             part[p][:, 0:n, KHI:KLO + 1, :].rearrange("c j a t -> c j (a t)")).then_inc(p_out[p], 16)
                                same = bass.AP(part[p][:, :, :, :].tensor, (4 * q + QLO) * T, [[3 * 4 * T, C], [0, n], [1, 2 * T]])
                                sp.dma_start(dst[:, :, QLO:QHI + 1, :].rearrange("c j a t -> c j (a t)"), same).then_inc(p_out[p], 16)

                        load(0, 0)
                        for dst, src in ((wv, t["WvT"]), (wq, t["WqT"]), (wk, t["WkT"])):
                            sp.dma_start(dst[:, :], src).then_inc(w_in, 16)
                        sp.dma_start(bv[:, :], t["bv"].partition_broadcast(128)).then_inc(w_in, 16)
                        load(1, 1)
                        with sp.Fori(0, B // 2 - 1) as i:
                            for p in range(2):
                                step(i, p, True)
                        for p in range(2):
                            step(B // 2 - 1, p, False)
                        for p in range(2):
                            sp.wait_ge(p_out[p], BASE + 16 * n_out * (B // 2))

                    @block.tensor
                    def _(pe):
                        pe.wait_ge(w_in, BASE + 16 * 4)
                        with pe.Fori(0, B // 2) as i:
                            for p in range(2):
                                b = 2 * i + p
                                pe.wait_ge(x_in[p], BASE + 16 * i + 16)
                                pe.wait_ge(p_full, BASE + b - 1)
                                pe.wait_ge(p_v, BASE + b - 1)
                                for n in range(NT):
                                    last = pe.matmul(bank[3 * p + 2][:, n * 128:(n + 1) * 128], xt[p][:, n * 128:(n + 1) * 128], wv[:, :],
                                                     start=True, stop=True)
                                last.then_inc(v_ps, 1)
                                pe.matmul(bank[3 * p][:, :], wq[:, :], xt[p][:, :], start=True, stop=True).then_inc(p_ps, 1)
                                pe.matmul(bank[3 * p + 1][:, :], wk[:, :], xt[p][:, :], start=True, stop=True).then_inc(p_ps, 1)

                    @block.scalar
                    def _(act):
                        with act.Fori(0, B // 2) as i:
                            for p in range(2):
                                b = 2 * i + p
                                act.wait_ge(p_ps, BASE + 2 * b + 2)
                                act.wait_ge(p_rest, BASE + b - 1)
                                for arr, src, scale in ((QLO, 0, SCALE[0]), (QHI, 0, SCALE[0]), (KLO, 1, 1.0), (KHI, 1, 1.0)):
                                    last = nc.scalar.activation(full[p][:, arr, :], bank[3 * p + src][:, :], ACT.Identity,
                                                                bias=bias[:, arr:arr + 1], scale=scale)
                                last.then_inc(p_full, 1)
                                act.wait_ge(p_full, BASE + b + 1)
                                act.wait_ge(p_out[p], BASE + 16 * n_out * i)
                                nc.scalar.copy(part[p][:, 0, :, :], full[p][:, :, :]).then_inc(p_hi, 1)

                    @block.vector
                    def _(v):
                        for p in range(2):
                            v.memset(vt[p][:, :, :, DH:VC], 1.0).then_inc(p_vone, 1)
                        v.wait_ge(p_vone, BASE + 2)
                        v.wait_ge(w_in, BASE + 16 * 4)
                        with v.Fori(0, B // 2) as i:
                            for p in range(2):
                                b = 2 * i + p
                                v.wait_ge(v_ps, BASE + b + 1)
                                v.wait_ge(p_out[p], BASE + 16 * n_out * i)
                                for n in range(NT):
                                    last = v.tensor_tensor(vt[p][:, :, n, 0:DH],
                                                           bank[3 * p + 2][:, n * 128:(n + 1) * 128].rearrange("p (h d) -> p h d", d=DH),
                                                           bv[:, :].rearrange("p (h d) -> p h d", d=DH), ALU.add)
                                last.then_inc(p_v, 1)
                                v.wait_ge(p_hi, BASE + b + 1)
                                v.tensor_tensor(left[p][:, :, :], full[p][:, :, :], part[p][:, 0, :, :], ALU.subtract).then_inc(p_rest, 1)
                                v.wait_ge(p_rest, BASE + b + 1)
                                v.tensor_copy(part[p][:, 1, :, :], left[p][:, :, :]).then_inc(p_mid, 1)
                                v.wait_ge(p_mid, BASE + b + 1)
                                v.tensor_tensor(part[p][:, 2, :, :], left[p][:, :, :], part[p][:, 1, :, :], ALU.subtract).then_inc(p_lo, 1)

        def attention_phase(layer):
            rel = layer == 0
            unroll = UNROLL[layer]
            loops = (NHEAD - FIRST - LOAD_AHEAD) // unroll
            last = NHEAD - FIRST - unroll * loops
            vslots = unroll // GROUP
            with ExitStack() as ctx:
                def sb(name, shape, dt=F32):
                    return ctx.enter_context(nc.sbuf_tensor(f"a{layer}_{name}", shape, dt))

                def s(name):
                    return sem(f"a{layer}_{name}")

                rows = R0 if rel else R1
                stks = sb("stks", [rows, unroll, 4, T], BF16)
                stk = [stks[:, i] for i in range(unroll)]
                vs = [sb(f"vs{i}", [128, GROUP * NT * VC + VW - VC]) for i in range(vslots)]
                prob = [sb(f"prob{i}", [128, NT, T]) for i in range(2)]
                probt = [sb(f"probt{i}", [128, NT, T]) for i in range(unroll)]
                negmax = [sb(f"negmax{i}", [128, NT]) for i in range(2)]
                ident = sb("ident", [128, 128])
                mask = sb("mask", [128, 128], U32)
                outs = sb("outs", [128, T])
                if rel:
                    tabs = sb("tabs", [R0, unroll, 2 * REL], BF16)
                    tab = [tabs[:, i] for i in range(unroll)]
                    keyside = [sb(f"keyside{i}", [128, T]) for i in range(2)]
                    sheared = [sb(f"sheared{i}", [128, T]) for i in range(4)]
                    corr = [sb(f"corr{i}", [128, NT, REL]) for i in range(2)]
                    band = [sb(f"band{i}", [128, NT, WIN]) for i in range(2)]
                score_banks = bank[0:4] if rel else bank[0:3]
                others = bank[4:5] if rel else bank[3:5]
                cbank = bank[7]
                turned_bank = [bank[5], bank[6], bank[6], bank[5]] if rel else [bank[5], bank[6]] * 2
                key_bank, corr_bank = bank[5], bank[6]

                s_const, s_pad, held_off = s("const"), s("pad"), s("held_off")
                stk_in = [s(f"stk_in{i}") for i in range(unroll)]
                v_in = [s(f"v_in{i}") for i in range(vslots)]
                score_mm, fixed, mid_fixed, added, maxed, exped = (s(n) for n in ("score_mm", "fixed", "mid_fixed", "added", "maxed", "exped"))
                turned, copied, pv_mm, out_copied, out_written = (s(n) for n in ("turned", "copied", "pv_mm", "out_copied", "out_written"))
                if rel:
                    key_mm, key_copied, a_written, corr_mm, corr_copied, b_written = (
                        s(n) for n in ("key_mm", "key_copied", "a_written", "corr_mm", "corr_copied", "b_written"))
                    sheared_in = [s(f"sheared_in{i}") for i in range(4)]
                    band_in = [s(f"band_in{i}") for i in range(2)]
                    tab_in, consts_in = ([s(f"{n}_in{i}") for i in range(unroll // GROUP)] for n in ("tab", "consts"))

                poskey_in = s("poskey_in")

                class Head:
                    def __init__(self, i, at):
                        self.i, self.slot = i + at // unroll, at % unroll
                        self.n = unroll * i + at

                    def use(self, ring):
                        return (unroll // ring) * self.i + self.slot // ring

                def tile_banks(h, n):
                    at = NT * h.slot + n
                    return score_banks[at % len(score_banks)], others[at % len(others)]

                def made(n):
                    return min(n, NHEAD) if isinstance(n, int) else n

                def cut(n):
                    return min(T, 128 * n + (REL + SPAN if rel else 128))

                def fix_cols(n):
                    a = 128 * n + (SPAN if rel else 0)
                    return a, min(T, a + 128)

                def mid_cols(n):
                    return 128 * n + 1, min(T, 128 * n + 129)

                def win_cols(n):
                    a, e = 128 * n - SPAN, 128 * n - SPAN + WIN
                    return max(a, 0), min(e, T), max(a, 0) - a

                def hold(q, event, value):
                    q.wait_ge(event, BASE + value)
                    q.sem_inc(held_off, 1)

                per_stk = 16 if rel else 48

                def head_load(sp, h):
                    j, b = h.slot, h.n // H
                    own = bass.ts(h.n % H, DH)
                    if rel:
                        sp.dma_start(stk[j][0:SR, :, :], stack[0][b, :, own, :, :]).then_inc(stk_in[j], 16)
                    else:
                        sp.dma_start(stk[j][0:SR, KLO:QLO + 1, :], stack[1][b, :, own, 0:2, :]).then_inc(stk_in[j], 16)
                        sp.dma_start(stk[j][0:SR, QHI, :], stack[1][b, :, own, 1, :]).then_inc(stk_in[j], 16)
                        sp.dma_start(stk[j][SR:R1, QLO:QHI + 1, :], stack[1][b, :, own, 2:4, :]).then_inc(stk_in[j], 16)

                def tab_load(sp, h):
                    src = table[bass.ds(h.n % H, GROUP)].rearrange("h r c -> r h c")
                    sp.dma_start(tabs[:, h.slot:h.slot + GROUP, :], src).then_inc(tab_in[h.slot // GROUP], 16)

                def consts_load(sp, h):
                    src = consts[bass.ds(h.n % H, GROUP), :, QHI, :].rearrange("h r t -> r h t")
                    sp.dma_start(stks[SR:R0, h.slot:h.slot + GROUP, QHI, :], src).then_inc(consts_in[h.slot // GROUP], 16)

                def shear_a_write(sp, h):
                    hold(sp, key_copied, h.n + 1)
                    sp.dma_start(shear_a[h.slot % 4, :, SPAN:SPAN + T], keyside[h.slot % 2][:, :]).then_inc(a_written, 16)

                def shear_a_read(sp, h):
                    hold(sp, a_written, 16 * (h.n + 1))
                    skew = bass.AP(shear_a.tensor, (h.slot % 4) * 128 * PITCH_A, [[PITCH_A + 1, 128], [1, T]])
                    sp.dma_start(sheared[h.slot % 4][:, :], skew).then_inc(sheared_in[h.slot % 4], 16)

                def shear_b_write(sp, h):
                    hold(sp, corr_copied, h.n + 1)
                    dst = shear_b[h.slot % 4].rearrange("(n p) c -> p n c", p=128)[:, :, REL:2 * REL]
                    sp.dma_start(dst, corr[h.slot % 2][:, :, :]).then_inc(b_written, 16)

                def shear_b_read(sp, h):
                    hold(sp, b_written, 16 * (h.n + 1))
                    skew = bass.AP(shear_b.tensor, (h.slot % 4) * T * PITCH_B + REL,
                                   [[PITCH_B - 1, 128], [128 * PITCH_B, NT], [1, WIN]])
                    sp.dma_start(band[h.slot % 2][:, :, :], skew).then_inc(band_in[h.slot % 2], 16)

                def group_store(sp, h, more):
                    g = h.use(GROUP)
                    hold(sp, out_copied, g + 1)
                    sp.dma_start(heads_out[bass.ts(g, GROUP)], outs[:, :]).then_inc(out_written, 16)
                    if more:
                        sp.dma_start(vs[h.slot // GROUP][:, 0:GROUP * NT * VC], values[g + vslots]).then_inc(v_in[h.slot // GROUP], 16)

                def sync_step(sp, i, j, left, weighed=True):
                    n = unroll * i + j
                    if rel and left > CORR_AHEAD:
                        shear_a_write(sp, Head(i, j + CORR_AHEAD + 1))
                    if rel and left > 1:
                        hold(sp, added, 4 * (n + 1))
                        shear_b_read(sp, Head(i, j + 2))
                    if rel and left > 2:
                        shear_b_write(sp, Head(i, j + 3))
                    if left > LOAD_AHEAD - 1:
                        hold(sp, maxed, 4 * n)
                        head_load(sp, Head(i, j + LOAD_AHEAD))
                    if rel and j % GROUP == 1 and left >= 10:
                        tab_load(sp, Head(i, j + 7))
                    if rel and j % GROUP == GROUP - 1 and left >= 8:
                        hold(sp, maxed, 4 * (n + 1))
                        consts_load(sp, Head(i, j + 5))
                    if rel and left > CORR_AHEAD:
                        shear_a_read(sp, Head(i, j + CORR_AHEAD + 1))
                    if weighed and j % GROUP == GROUP - 1:
                        group_store(sp, Head(i, j + 1 - 2 * GROUP), left >= GROUP * (vslots - 1))

                start_phase()
                with nc.Block() as block:
                    @block.sync
                    def _(sp):
                        if rel:
                            head_load(sp, Head(0, 0))
                            for g in range(unroll // GROUP):
                                tab_load(sp, Head(0, GROUP * g))
                            for g in range(unroll // GROUP):
                                own = slice(GROUP * g, GROUP * g + GROUP)
                                sp.dma_start(stks[SR:R0, own, :, :].rearrange("r h a t -> r h (a t)"),
                                             consts[own].rearrange("h r a t -> r h (a t)")).then_inc(consts_in[g], 16)
                        for g in range(vslots):
                            sp.dma_start(vs[g][:, 0:GROUP * NT * VC], values[g]).then_inc(v_in[g], 16)
                        sp.dma_start(ident[:, :], t["ident"]).then_inc(s_const, 16)
                        sp.dma_start(mask[:, :], t[f"mask{layer}"]).then_inc(s_const, 16)
                        if not rel:
                            every = bass.AP(t["poskey"].tensor, 0, [[T, SR], [0, unroll], [1, T]])
                            sp.dma_start(stks[SR:R1, :, KLO, :], every).then_inc(poskey_in, 16)
                        for j in range(1 if rel else 0, LOAD_AHEAD):
                            head_load(sp, Head(0, j))
                        if rel:
                            for j in range(2):
                                shear_a_write(sp, Head(0, j))
                                shear_a_read(sp, Head(0, j))
                            for j in range(2):
                                shear_b_write(sp, Head(0, j))
                                shear_a_write(sp, Head(0, j + 2))
                                shear_b_read(sp, Head(0, j))
                                shear_a_read(sp, Head(0, j + 2))
                            shear_b_write(sp, Head(0, 2))
                            shear_a_write(sp, Head(0, 4))
                            shear_a_read(sp, Head(0, 4))
                        for j in range(FIRST):
                            sync_step(sp, 0, j, NHEAD, weighed=False)
                        with sp.Fori(0, loops) as i:
                            for j in range(unroll):
                                sync_step(sp, i, FIRST + j, NHEAD)
                        for j in range(last):
                            sync_step(sp, loops, FIRST + j, last - 1 - j)
                        group_store(sp, Head(loops, FIRST + last - GROUP), False)
                        sp.wait_ge(out_written, BASE + 16 * NG)

                    def score_tile(pe, h, n):
                        tile, k = 4 * h.n + n, stk[h.slot]
                        score, other = tile_banks(h, n)
                        q = slice(128 * n, 128 * n + 128)
                        c = cut(n)
                        if n == 0:
                            pe.wait_ge(stk_in[h.slot], BASE + per_stk * (h.i + 1))
                            if rel:
                                pe.wait_ge(consts_in[h.slot // GROUP], BASE + 16 * (h.i + 1))
                        pe.wait_ge(exped, BASE + tile - len(score_banks) + 1)
                        lo = SR if rel else R1
                        pe.matmul(score[:, 0:c], k[0:lo, QLO, q], k[0:lo, KLO, 0:c], start=True, stop=True)
                        khi = KHI if rel else KLO
                        if c < T:
                            pe.matmul(score[:, c:T], k[:, QHI, q], k[:, khi, c:T], start=True, stop=True)
                        pe.wait_ge(fixed if rel else mid_fixed, BASE + tile - len(others) + 1)
                        a, e = fix_cols(n)
                        last = pe.matmul(other[:, 0:e - a], k[:, QHI, q], k[:, khi, a:e], start=True, stop=True)
                        if not rel:
                            a, e = mid_cols(n)
                            last = pe.matmul(other[:, 128:128 + e - a], k[0:SR, QLO, q], k[0:SR, KLO, a:e],
                                             start=True, stop=True)
                        last.then_inc(score_mm, 1)

                    def turn(pe, h, k):
                        if k == 0:
                            pe.wait_ge(exped, BASE + 4 * h.n + 4)
                        if rel and k == 1:
                            pe.wait_ge(corr_copied, BASE + made(h.n + CORR_AHEAD))
                        elif rel and k == 3:
                            pe.wait_ge(key_copied, BASE + made(h.n + KEY_AHEAD + 1))
                        else:
                            pe.wait_ge(copied, BASE + 4 * h.n + (k if rel else k - 1))
                        for n in range(NT):
                            last = pe.transpose(turned_bank[k][:, n * 128:(n + 1) * 128],
                                                prob[h.slot % 2][:, n, k * 128:(k + 1) * 128], ident[:, :])
                        last.then_inc(turned, 1)

                    def weigh(pe, h, k):
                        g = h.slot // GROUP
                        if k == 0:
                            pe.wait_ge(v_in[g], BASE + 16 * (h.i + 1))
                            pe.wait_ge(out_copied, BASE + h.use(GROUP))
                            pe.wait_ge(copied, BASE + 4 * (h.n + GROUP))
                        for j in range(GROUP):
                            at = VC * (NT * j + k)
                            pe.matmul(cbank[32 * j:32 * j + VW, :], vs[g][:, at:at + VW], probt[h.slot + j][:, k, :],
                                      start=(k == 0), stop=(k == NT - 1)).then_inc(pv_mm, 1)

                    def key_side(pe, h):
                        pe.wait_ge(stk_in[h.slot], BASE + per_stk * (h.i + 1))
                        pe.wait_ge(tab_in[h.slot // GROUP], BASE + 16 * (h.i + 1))
                        pe.matmul(key_bank[:, :], tab[h.slot][:, 0:REL], stk[h.slot][:, KLO, :], start=True, stop=True).then_inc(key_mm, 1)

                    def correction(pe, h):
                        pe.wait_ge(sheared_in[h.slot % 4], BASE + 16 * (h.use(4) + 1))
                        for n in range(NT):
                            q = slice(128 * n, 128 * n + 128)
                            pe.matmul(corr_bank[:, q], sheared[h.slot % 4][:, q], ident[:, :], is_transpose=True, start=True, stop=False)
                            last = pe.matmul(corr_bank[:, q], stk[h.slot][0:SR, QLO, q], tab[h.slot][0:SR, REL:2 * REL], start=False, stop=True)
                        last.then_inc(corr_mm, 1)

                    def ahead(i, j, k, tiles):
                        return Head(i, j + (k + tiles) // NT), (k + tiles) % NT

                    def tensor_step(pe, i, j, left, weighed=True):
                        own = Head(i, j)
                        for k in range(NT):
                            if left >= (k + SCORE_AHEAD) // NT:
                                score_tile(pe, *ahead(i, j, k, SCORE_AHEAD))
                            turn(pe, own, k)
                            if k == 0 and weighed:
                                weigh(pe, Head(i, j - j % GROUP - GROUP), j % GROUP)
                            if rel and k == 1 and left >= KEY_AHEAD:
                                pe.wait_ge(copied, BASE + 4 * own.n + 1)
                                key_side(pe, Head(i, j + KEY_AHEAD))
                        if rel and left >= CORR_AHEAD:
                            pe.wait_ge(copied, BASE + 4 * own.n + 3)
                            correction(pe, Head(i, j + CORR_AHEAD))

                    @block.tensor
                    def _(pe):
                        pe.wait_ge(s_const, BASE + 32)
                        if not rel:
                            pe.wait_ge(poskey_in, BASE + 16)
                        if rel:
                            for g in range(unroll // GROUP):
                                pe.wait_ge(consts_in[g], BASE + 16)
                            for j in range(KEY_AHEAD):
                                pe.wait_ge(key_copied, BASE + j)
                                key_side(pe, Head(0, j))
                                if j >= 2:
                                    pe.wait_ge(corr_copied, BASE + j - 2)
                                    correction(pe, Head(0, j - 2))
                            pe.wait_ge(key_copied, BASE + KEY_AHEAD)
                        for n in range(SCORE_AHEAD):
                            score_tile(pe, *ahead(0, 0, 0, n))
                        pe.wait_ge(s_pad, BASE + vslots)
                        for j in range(FIRST):
                            tensor_step(pe, 0, j, NHEAD, weighed=False)
                        with pe.Fori(0, loops) as i:
                            for j in range(unroll):
                                tensor_step(pe, i, FIRST + j, NHEAD)
                        for j in range(last):
                            tensor_step(pe, loops, FIRST + j, last - 1 - j)
                        for k in range(NT):
                            weigh(pe, Head(loops, FIRST + last - GROUP), k)

                    def mix(v, h, n):
                        score, other = tile_banks(h, n)
                        v.wait_ge(score_mm, BASE + 4 * h.n + n + 1)
                        a, e = fix_cols(n)
                        v.sem_inc(held_off, 1)
                        v.copy_predicated(score[:, a:e], mask[:, 0:e - a], other[:, 0:e - a]).then_inc(fixed, 1)

                    def finish(v, h, n):
                        score, other = tile_banks(h, n)
                        v.wait_ge(fixed, BASE + 4 * h.n + n + 1)
                        if rel:
                            if n == 0:
                                v.wait_ge(band_in[h.slot % 2], BASE + 16 * (h.use(2) + 1))
                            a, e, w = win_cols(n)
                            v.tensor_tensor(score[:, a:e], score[:, a:e], band[h.slot % 2][:, n, w:w + e - a], ALU.add).then_inc(added, 1)
                        else:
                            a, e = mid_cols(n)
                            v.sem_inc(held_off, 1)
                            v.copy_predicated(score[:, a:e], ident[:, 0:e - a].bitcast(U32),
                                              other[:, 128:128 + e - a]).then_inc(mid_fixed, 1)

                    def row_max(v, h, n):
                        score, other = tile_banks(h, n)
                        v.wait_ge(added if rel else mid_fixed, BASE + 4 * h.n + n + 1)
                        if n == 0:
                            v.wait_ge(exped, BASE + 4 * (h.n - 1))
                        v.tensor_reduce(negmax[h.slot % 2][:, n:n + 1], score[:, :], AX.X, ALU.max, negate=True).then_inc(maxed, 1)

                    def key_out(v, h):
                        v.wait_ge(key_mm, BASE + h.n + 1)
                        v.wait_ge(a_written, BASE + 16 * (h.n - 1))
                        v.tensor_copy(keyside[h.slot % 2][:, :], key_bank[:, :]).then_inc(key_copied, 1)

                    @block.vector
                    def _(v):
                        for g in range(vslots):
                            v.memset(vs[g][:, GROUP * NT * VC:], 0.0).then_inc(s_pad, 1)
                        v.wait_ge(s_const, BASE + 32)
                        if rel:
                            for j in range(KEY_AHEAD):
                                key_out(v, Head(0, j))
                        for n in range(SCORE_AHEAD):
                            mix(v, *ahead(0, 0, 0, n))
                            if n:
                                row_max(v, *ahead(0, 0, 0, n - 1))
                            finish(v, *ahead(0, 0, 0, n))

                        def vector_step(i, j, left):
                            for k in range(NT):
                                if left >= (k + SCORE_AHEAD) // NT:
                                    mix(v, *ahead(i, j, k, SCORE_AHEAD))
                                if left >= (k + SCORE_AHEAD - 1) // NT:
                                    row_max(v, *ahead(i, j, k, SCORE_AHEAD - 1))
                                if left >= (k + SCORE_AHEAD) // NT:
                                    finish(v, *ahead(i, j, k, SCORE_AHEAD))
                                if rel and k == 1 and left >= KEY_AHEAD:
                                    key_out(v, Head(i, j + KEY_AHEAD))

                        for j in range(FIRST):
                            vector_step(0, j, NHEAD)
                        with v.Fori(0, loops) as i:
                            for j in range(unroll):
                                vector_step(i, FIRST + j, NHEAD)
                        for j in range(last):
                            vector_step(loops, FIRST + j, last - 1 - j)

                    def exp_tile(act, h, n):
                        act.wait_ge(maxed, BASE + 4 * h.n + n + 1)
                        if n == 0:
                            act.wait_ge(turned, BASE + 4 * (h.n - 1))
                        score, _ = tile_banks(h, n)
                        nc.scalar.activation(prob[h.slot % 2][:, n, :], score[:, :], ACT.Exp,
                                             bias=negmax[h.slot % 2][:, n:n + 1]).then_inc(exped, 1)

                    def copy_turned(act, h, k):
                        act.wait_ge(turned, BASE + 4 * h.n + k + 1)
                        if k == 0:
                            act.wait_ge(pv_mm, BASE + 16 * (h.use(GROUP) - vslots + 1))
                        nc.scalar.copy(probt[h.slot][:, k, :], turned_bank[k][:, :]).then_inc(copied, 1)

                    def group_out(act, h):
                        act.wait_ge(pv_mm, BASE + 16 * (h.use(GROUP) + 1))
                        act.wait_ge(out_written, BASE + 16 * h.use(GROUP))
                        nc.scalar.copy(outs[:, :], cbank[:, :]).then_inc(out_copied, 1)

                    def corr_out(act, h):
                        act.wait_ge(corr_mm, BASE + h.n + 1)
                        act.wait_ge(b_written, BASE + 16 * (h.n - 1))
                        nc.scalar.copy(corr[h.slot % 2][:, :, :], corr_bank[:, :].rearrange("p (n r) -> p n r", n=NT)).then_inc(corr_copied, 1)

                    @block.scalar
                    def _(act):
                        if rel:
                            for j in range(CORR_AHEAD):
                                corr_out(act, Head(0, j))
                        for n in range(EXP_AHEAD):
                            exp_tile(act, *ahead(0, 0, 0, n))

                        def scalar_step(i, j, left, weighed=True):
                            own = Head(i, j)
                            for k in range(NT):
                                if left >= (k + EXP_AHEAD) // NT:
                                    exp_tile(act, *ahead(i, j, k, EXP_AHEAD))
                                copy_turned(act, own, k)
                                if k == 1 and weighed and j % GROUP == GROUP - 1:
                                    group_out(act, Head(i, j - j % GROUP - GROUP))
                            if rel and left >= CORR_AHEAD:
                                corr_out(act, Head(i, j + CORR_AHEAD))

                        for j in range(FIRST):
                            scalar_step(0, j, NHEAD, weighed=False)
                        with act.Fori(0, loops) as i:
                            for j in range(unroll):
                                scalar_step(i, FIRST + j, NHEAD)
                        for j in range(last):
                            scalar_step(loops, FIRST + j, last - 1 - j)
                        group_out(act, Head(loops, FIRST + last - GROUP))

        def dense_phase(layer):
            first = layer == 0
            with ExitStack() as ctx:
                def sb(name, shape, dt=F32):
                    return ctx.enter_context(nc.sbuf_tensor(f"d{layer}_{name}", shape, dt))

                def s(name):
                    return sem(f"d{layer}_{name}")

                loads = []
                N_FIRST = 3

                def const(name, shape, src, dt=F32):
                    tile = sb(name, shape, dt)
                    loads.append((tile, src))
                    return tile

                ident = const("ident", [128, 128], t["ident"])
                wo = const("wo", [C, C], t["WoT"] if first else t["Wo"])
                bo = const("bo", [128, C], (t["bo"] if first else t["bo1"]).partition_broadcast(128))
                if first:
                    w_r, w_k, w_v = (const(n, [C, C], t[n]) for n in ("W_rT", "W_kT", "W_vT"))
                    mu = const("mu", [C, 2], t["mu"])
                    wq, wqs, wk, wv = (const(n, [C, C], t[n]) for n in ("Wq", "Wq_swap", "Wk", "Wv"))
                    uv = const("uv", [C, 3], t["uv"])
                    trig = const("trig", [C, 4, T], t["trig"])
                    uvs = sb("uvs", [C, 3])
                    xt1 = sb("xt1", [C, 1 + T])
                    delta, xr, xk = sb("delta", [C, T]), sb("xr", [C, T]), sb("xk", [C, T])
                    kr, kact, gate = sb("kr", [C, T]), sb("kact", [C, T]), sb("gate", [128, NT, C])
                    x2 = sb("x2", [128, NT, C])
                    xt2 = sb("xt2", [C, T])
                    full = sb("full", [C, 4, T])
                    qv = sb("qv", [C, 2, T])
                    rot = sb("rot", [C, 4, T])
                    left = sb("left", [C, 4, T])
                    part = sb("part", [C, 3, 4 * T + 2], BF16)
                    vt = sb("vt", [128, H, NT, VC])
                else:
                    w1, w2 = (const(n, [C, HID], t[n]) for n in ("w1T", "w2T"))
                    h1, h2 = (const(n, [128, KH, HID], t[n].rearrange("(k p) o -> p k o", p=128)) for n in ("h1T", "h2T"))
                    w3 = const("w3", [128, KH, C], t["w3T"].rearrange("(k p) o -> p k o", p=128))
                    fs = const("fs", [128, 4, KH], t["hid_s"])
                    s3 = const("s3", [128, C], t["w3_s"].partition_broadcast(128))
                    xt1 = sb("xt1", [C, 1 + T])
                    silu, ha, hb, hc = (sb(n, [128, KH, T]) for n in ("silu", "ha", "hb", "hc"))
                    x2 = sb("x2", [128, NT, C])
                head_t, sums, head_n = sb("head_t", [C, T]), sb("sums", [C, T]), sb("head_n", [C, T])
                xin, xb, pre1, pre2, x1 = (sb(n, [128, NT, C]) for n in ("xin", "xb", "pre1", "pre2", "x1"))
                x1n = x1 if first else sb("x1n", [128, NT, C])
                stats, mv = sb("stats", [128, NT, 6]), sb("mv", [128, 2, NT, 2])
                veps, rstd, half = sb("veps", [128, NT]), sb("rstd", [128, 2, NT]), sb("half", [128, NT])
                drop = sb("drop", [128, NT, C])

                c_in, late_in, ready, held_off = s("c_in"), s("late_in"), s("ready"), s("held_off")
                e = {n: s(n) for n in (
                    "x_in", "head_in", "kept", "recip", "normed", "out_mm", "biased", "summed",
                    "st1", "mv1", "ve1", "rs1", "x1", "tr1", "xt1", "f_stored",
                    "st2", "mv2", "ve2", "rs2", "x2", "gated", "added")}
                if first:
                    e |= {n: s(n) for n in ("delta", "mixed", "k_mm", "r_mm", "kr", "kact", "sig", "kv_mm", "tr2", "xt2",
                                            "qk_mm", "v_mm", "qk", "r1", "r2", "rot", "hi", "left", "mid", "lo", "vt", "written", "vt_written")}
                else:
                    e |= {n: s(n) for n in ("w1_mm", "w2_mm", "silu", "ha", "h1_mm", "hb", "h2_mm", "hc", "o_mm")}

                def statistics(v, b, src, i):
                    for n in range(NT):
                        last = v.bn_stats(stats[:, n, :], src[:, n, :])
                    last.then_inc(e[f"st{i}"], 1)
                    v.wait_ge(e[f"st{i}"], BASE + b + 1)
                    v.sem_inc(held_off, 1)
                    for n in range(NT):
                        last = v.bn_aggr(mv[:, i - 1, n, :], stats[:, n, :])
                    last.then_inc(e[f"mv{i}"], 1)

                def rows(v, b, src, dst, i):
                    v.wait_ge(e[f"rs{i}"], BASE + b + 1)
                    for n in range(NT):
                        last = v.tensor_scalar(dst[:, n, :], src[:, n, :], mv[:, i - 1, n, 0:1], rstd[:, i - 1, n:n + 1], ALU.subtract, ALU.mult)
                    last.then_inc(e[f"x{i}"], 1)

                def norm_pool(p, b, i):
                    p.wait_ge(e[f"mv{i}"], BASE + b + 1)
                    p.sem_inc(held_off, 1)
                    p.tensor_scalar(veps[:, :], mv[:, i - 1, :, 1], EPS, None, ALU.add).then_inc(e[f"ve{i}"], 1)
                    p.wait_ge(e[f"ve{i}"], BASE + b + 1)
                    p.tensor_tensor(rstd[:, i - 1, :], veps[:, :], half[:, :], ALU.pow).then_inc(e[f"rs{i}"], 1)

                def flip(pe, dst, src, event):
                    for n in range(NT):
                        last = pe.transpose(dst[:, n * 128:(n + 1) * 128], src[:, n, :], ident[:, :])
                    last.then_inc(event, 1)

                def by_token(pe, dst, src, w, event):
                    for n in range(NT):
                        last = pe.matmul(dst[:, n * 128:(n + 1) * 128], src[:, n * 128:(n + 1) * 128], w, start=True, stop=True)
                    last.then_inc(event, 1)


                def steps(eng, step):
                    with eng.Fori(0, B - 2) as b:
                        step(b, True, True)
                    step(B - 2, True, False)
                    step(B - 1, False, False)

                n_written = 4 * len(TERM_RUNS)
                uvs_in, fill = s("uvs_in"), s("fill")
                if first:
                    q_bank, qs_bank, k_bank, v_bank, ffn_k_bank, flip2_bank, out_bank, flip1_bank = bank
                    gate_bank, kv_bank = out_bank, flip1_bank
                else:
                    out_bank, flip1_bank, o_bank = bank[4], bank[5], bank[3]
                    h2_banks = [bank[6], bank[7], bank[4], bank[5]]

                start_phase()
                with nc.Block() as block:
                    @block.sync
                    def _(sp):
                        def load_constants(which, event):
                            for tile, src in which:
                                dst = tile[:, :] if len(tile.shape) == 2 else tile[:, :, :]
                                sp.dma_start(dst, src).then_inc(event, 16)

                        def hold(event, value):
                            sp.wait_ge(event, BASE + value)
                            sp.sem_inc(held_off, 1)

                        def load_batch(b):
                            hold(e["normed"], b)
                            sp.dma_start(head_t[:, :], heads_out[bass.ts(b, H), 0:DH, :]).then_inc(e["head_in"], 16)
                            rep = bass.AP(heads_out.tensor, (b * H) * (VW * T) + DH * T, [[VW * T, H], [0, DH], [1, T]])
                            sp.dma_start(sums[:, :], rep).then_inc(e["head_in"], 16)
                            hold(e["biased"], b)
                            old = t["x"][b] if first else resid[b]
                            sp.dma_start(xin[:, :, :], old.rearrange("(n p) c -> p n c", p=128)).then_inc(e["x_in"], 16)

                        def store(b):
                            hold(e["x2"], b + 1)
                            new = resid[b] if first else t["out"][b]
                            sp.dma_start(new.rearrange("(n p) c -> p n c", p=128), x2[:, :, :]).then_inc(e["f_stored"], 16)

                        def write_stacks(b):
                            own = bass.ts(b, H)
                            hold(e["vt"], b + 1)
                            sp.dma_start(values[bass.ts(b, H // GROUP)].rearrange("g p c -> p g c"),
                                         vt[:, :, :, :].rearrange("p (g h) n c -> p g (h n c)", h=GROUP)).then_inc(e["vt_written"], 16)
                            hold(e["lo"], b + 1)
                            for first_term, n, q in TERM_RUNS:
                                dst = stack[1][b, first_term:first_term + n].rearrange("j c a t -> c j a t")
                                sp.dma_start(dst[:, :, 0, :], part[:, 0:n, 0:T]).then_inc(e["written"], 16)
                                for a, at in ((1, T), (2, 2 * T), (3, 3 * T + 1)):
                                    same = bass.AP(part[:, :, :].tensor, q * (4 * T + 2) + at, [[3 * (4 * T + 2), C], [0, n], [1, T]])
                                    sp.dma_start(dst[:, :, a, :], same).then_inc(e["written"], 16)

                        load_constants(loads[:N_FIRST], c_in)
                        load_batch(0)
                        load_constants(loads[N_FIRST:], late_in)
                        load_batch(1)

                        def step(b, more, load):
                            if first:
                                store(b)
                            if load:
                                load_batch(b + 2)
                            if first:
                                write_stacks(b)
                            else:
                                store(b)

                        steps(sp, step)
                        sp.wait_ge(e["f_stored"], BASE + 16 * B)
                        if first:
                            sp.wait_ge(e["written"], BASE + 16 * n_written * B)
                            sp.wait_ge(e["vt_written"], BASE + 16 * B)

                    @block.tensor
                    def _(pe):
                        def out_product(b):
                            pe.wait_ge(e["normed"], BASE + b + 1)
                            if first:
                                pe.wait_ge(e["sig"], BASE + b)
                            by_token(pe, out_bank, head_n, wo[:, :], e["out_mm"])

                        def flip1(b):
                            pe.wait_ge(e["x1"], BASE + b + 1)
                            if first:
                                pe.wait_ge(e["gated"], BASE + b)
                            flip(pe, flip1_bank, x1n, e["tr1"])

                        def mix_products(b):
                            pe.wait_ge(e["mixed"], BASE + b + 1)
                            pe.wait_ge(e["kr"], BASE + b)
                            pe.matmul(ffn_k_bank[:, :], w_k[:, :], xk[:, :], start=True, stop=True).then_inc(e["k_mm"], 1)
                            by_token(pe, gate_bank, xr, w_r[:, :], e["r_mm"])
                            pe.wait_ge(e["kact"], BASE + b + 1)
                            by_token(pe, kv_bank, kact, w_v[:, :], e["kv_mm"])

                        def projections(b, more):
                            pe.wait_ge(e["xt2"], BASE + b + 1)
                            pe.wait_ge(e["qk"], BASE + b)
                            pe.matmul(k_bank[:, :], wk[:, :], xt2[:, :], start=True, stop=True)
                            pe.matmul(q_bank[:, :], wq[:, :], xt2[:, :], start=True, stop=True)
                            if more:
                                out_product(b + 1)
                            pe.matmul(qs_bank[:, :], wqs[:, :], xt2[:, :], start=True, stop=True).then_inc(e["qk_mm"], 1)
                            pe.wait_ge(e["vt"], BASE + b)
                            by_token(pe, v_bank, xt2, wv[:, :], e["v_mm"])

                        def gated_products(b):
                            pe.wait_ge(e["xt1"], BASE + b + 1)
                            for m in range(KH):
                                col = slice(128 * m, 128 * m + 128)
                                if m == 3:
                                    pe.wait_ge(e["gated"], BASE + b)
                                pe.matmul(bank[m][:, :], w1[:, col], xt1[:, 1:1 + T], start=True, stop=True).then_inc(e["w1_mm"], 1)
                                pe.matmul(bank[4 + m][:, :], w2[:, col], xt1[:, 1:1 + T], start=True, stop=True).then_inc(e["w2_mm"], 1)

                        def hidden(b, m, dst, w, src, ready, event):
                            for k in range(KH):
                                if m == 0:
                                    pe.wait_ge(ready, BASE + KH * b + k + 1)
                                last = pe.matmul(dst[:, :], w[:, k, 128 * m:128 * m + 128], src[:, k, :], start=(k == 0), stop=(k == KH - 1))
                            last.then_inc(event, 1)

                        def step(b, more, load):
                            if first:
                                pe.wait_ge(e["x2"], BASE + b + 1)
                                pe.wait_ge(e["xt2"], BASE + b)
                                flip(pe, flip2_bank, x2, e["tr2"])
                                projections(b, more)
                                if more:
                                    flip1(b + 1)
                                    mix_products(b + 1)
                                return
                            gated_products(b)
                            for m in range(KH):
                                hidden(b, m, bank[m], h1, ha, e["ha"], e["h1_mm"])
                                if more and m == 1:
                                    out_product(b + 1)
                            if more:
                                flip1(b + 1)
                            for m in range(KH):
                                if more and m == 2:
                                    pe.wait_ge(e["summed"], BASE + b + 2)
                                if more and m == 3:
                                    pe.wait_ge(e["xt1"], BASE + b + 2)
                                hidden(b, m, h2_banks[m], h2, hb, e["hb"], e["h2_mm"])
                            for n in range(NT):
                                for k in range(KH):
                                    if n == 0:
                                        pe.wait_ge(e["hc"], BASE + KH * b + k + 1)
                                    last = pe.matmul(o_bank[:, n * 128:(n + 1) * 128], hc[:, k, n * 128:(n + 1) * 128], w3[:, k, :],
                                                     start=(k == 0), stop=(k == KH - 1))
                            last.then_inc(e["o_mm"], 1)

                        pe.wait_ge(c_in, BASE + 16 * N_FIRST)
                        out_product(0)
                        flip1(0)
                        pe.wait_ge(late_in, BASE + 16 * (len(loads) - N_FIRST))
                        if first:
                            mix_products(0)
                        steps(pe, step)

                    @block.gpsimd
                    def _(p):
                        p.memset(half[:, :], -0.5).then_inc(ready, 1)
                        p.wait_ge(ready, BASE + 1)

                        def step(b, more, load):
                            if more:
                                norm_pool(p, b + 1, 1)
                            if not first:
                                norm_pool(p, b, 2)
                            else:
                                p.wait_ge(e["qk"], BASE + b + 1)
                                p.tensor_tensor(rot[:, 1, :], qv[:, 1, :], trig[:, 1, :], ALU.mult)
                                p.tensor_tensor(rot[:, 3, :], qv[:, 1, :], trig[:, 3, :], ALU.mult).then_inc(e["r1"], 1)
                                if more:
                                    norm_pool(p, b + 1, 2)

                        norm_pool(p, 0, 1)
                        if first:
                            norm_pool(p, 0, 2)
                        steps(p, step)

                    @block.scalar
                    def _(act):
                        def turn1(b):
                            act.wait_ge(e["tr1"], BASE + b + 1)
                            nc.scalar.copy(xt1[:, 1:1 + T], flip1_bank[:, :]).then_inc(e["xt1"], 1)

                        def mixing(b):
                            act.wait_ge(e["r_mm"], BASE + b + 1)
                            nc.scalar.activation(gate[:, :, :], gate_bank[:, :].rearrange("p (n c) -> p n c", n=NT),
                                                 ACT.Sigmoid).then_inc(e["sig"], 1)
                            act.wait_ge(e["kr"], BASE + b + 1)
                            nc.scalar.activation(kact[:, :], kr[:, :], ACT.Square).then_inc(e["kact"], 1)

                        def step(b, more, load):
                            if first:
                                act.wait_ge(e["tr2"], BASE + b + 1)
                                nc.scalar.copy(xt2[:, :], flip2_bank[:, :]).then_inc(e["xt2"], 1)
                                act.wait_ge(e["qk_mm"], BASE + b + 1)
                                act.wait_ge(e["left"], BASE + b)
                                nc.scalar.copy(full[:, 0, :], k_bank[:, :])
                                nc.scalar.activation(full[:, 1, :], q_bank[:, :], ACT.Identity, bias=uvs[:, 0:1], scale=SCALE[1])
                                nc.scalar.activation(qv[:, 0, :], q_bank[:, :], ACT.Identity, bias=uvs[:, 1:2], scale=SCALE[1])
                                nc.scalar.activation(qv[:, 1, :], qs_bank[:, :], ACT.Identity, bias=uvs[:, 2:3],
                                                     scale=SCALE[1]).then_inc(e["qk"], 1)
                                if more:
                                    turn1(b + 1)
                                act.wait_ge(e["qk"], BASE + b + 1)
                                act.wait_ge(e["rot"], BASE + b + 1)
                                act.wait_ge(e["written"], BASE + 16 * n_written * b)
                                nc.scalar.copy(part[:, 0, 0:4 * T], full[:, :, :].rearrange("p a t -> p (a t)")).then_inc(e["hi"], 1)
                                if more:
                                    mixing(b + 1)
                                return
                            for m in range(KH):
                                act.wait_ge(e["w1_mm"], BASE + KH * b + m + 1)
                                nc.scalar.activation(silu[:, m, :], bank[m][:, :], ACT.Silu, scale=fs[:, 0, m:m + 1]).then_inc(e["silu"], 1)
                            for m in range(KH):
                                act.wait_ge(e["h1_mm"], BASE + KH * b + m + 1)
                                nc.scalar.activation(hb[:, m, :], bank[m][:, :], ACT.Gelu, scale=fs[:, 2, m:m + 1]).then_inc(e["hb"], 1)
                            if more:
                                turn1(b + 1)
                            for m in range(KH):
                                act.wait_ge(e["h2_mm"], BASE + KH * b + m + 1)
                                nc.scalar.activation(hc[:, m, :], h2_banks[m][:, :], ACT.Gelu, scale=fs[:, 3, m:m + 1]).then_inc(e["hc"], 1)

                        act.wait_ge(late_in, BASE + 16 * (len(loads) - N_FIRST))
                        if first:
                            nc.scalar.activation(uvs[:, :], uv[:, :], ACT.Identity, scale=SCALE[1]).then_inc(uvs_in, 1)
                            act.wait_ge(uvs_in, BASE + 1)
                        turn1(0)
                        if first:
                            mixing(0)
                        steps(act, step)

                    @block.vector
                    def _(v):
                        def normalise(b):
                            v.wait_ge(e["head_in"], BASE + 32 * b + 32)
                            v.reciprocal(sums[:, :], sums[:, :]).then_inc(e["recip"], 1)
                            v.wait_ge(e["recip"], BASE + b + 1)
                            v.tensor_tensor(head_n[:, :], head_t[:, :], sums[:, :], ALU.mult).then_inc(e["normed"], 1)
                            v.wait_ge(e["x_in"], BASE + 16 * b + 16)
                            for n in range(NT):
                                last = v.tensor_tensor(xb[:, n, :], xin[:, n, :], bo[:, :], ALU.add)
                            last.then_inc(e["biased"], 1)

                        def residual1(b):
                            v.wait_ge(e["biased"], BASE + b + 1)
                            v.wait_ge(e["out_mm"], BASE + b + 1)
                            v.tensor_tensor(pre1[:, :, :], out_bank[:, :].rearrange("p (n c) -> p n c", n=NT), xb[:, :, :],
                                            ALU.add).then_inc(e["summed"], 1)
                            v.wait_ge(e["summed"], BASE + b + 1)
                            statistics(v, b, pre1, 1)

                        def token_mix(b):
                            v.wait_ge(e["xt1"], BASE + b + 1)
                            v.tensor_tensor(delta[:, :], xt1[:, 1:1 + T], xt1[:, 0:T], ALU.subtract).then_inc(e["delta"], 1)
                            v.wait_ge(e["delta"], BASE + b + 1)
                            v.scalar_tensor_tensor(out=xk[:, :], in0=delta[:, :], scalar=mu[:, 1:2], in1=xt1[:, 0:T],
                                                   op0=ALU.mult, op1=ALU.add)
                            v.scalar_tensor_tensor(out=xr[:, :], in0=delta[:, :], scalar=mu[:, 0:1], in1=xt1[:, 0:T],
                                                   op0=ALU.mult, op1=ALU.add).then_inc(e["mixed"], 1)

                        def relu(b):
                            v.wait_ge(e["k_mm"], BASE + b + 1)
                            v.tensor_scalar(kr[:, :], ffn_k_bank[:, :], 0.0, None, ALU.max).then_inc(e["kr"], 1)

                        def residual2(b):
                            if first:
                                v.wait_ge(e["sig"], BASE + b + 1)
                                v.wait_ge(e["kv_mm"], BASE + b + 1)
                                v.tensor_tensor(drop[:, :, :], kv_bank[:, :].rearrange("p (n c) -> p n c", n=NT), gate[:, :, :],
                                                ALU.mult).then_inc(e["gated"], 1)
                            else:
                                v.wait_ge(e["o_mm"], BASE + b + 1)
                                for n in range(NT):
                                    last = v.tensor_tensor(drop[:, n, :], o_bank[:, n * 128:(n + 1) * 128], s3[:, :], ALU.mult)
                                last.then_inc(e["gated"], 1)
                            v.wait_ge(e["gated"], BASE + b + 1)
                            v.tensor_tensor(pre2[:, :, :], drop[:, :, :], x1[:, :, :], ALU.add).then_inc(e["added"], 1)
                            v.wait_ge(e["added"], BASE + b + 1)
                            statistics(v, b, pre2, 2)

                        def rows2(b):
                            v.wait_ge(e["f_stored"], BASE + 16 * b)
                            rows(v, b, pre2, x2, 2)

                        def keep_rows1(b):
                            if not first:
                                v.wait_ge(e["x1"], BASE + b + 1)
                                v.tensor_copy(x1[:, :, :], x1n[:, :, :]).then_inc(e["kept"], 1)
                                v.wait_ge(e["kept"], BASE + b + 1)

                        def step0(b, more, load):
                            if more:
                                normalise(b + 1)
                                residual1(b + 1)
                            v.wait_ge(e["v_mm"], BASE + b + 1)
                            v.wait_ge(e["vt_written"], BASE + 16 * b)
                            for n in range(NT):
                                last = v.tensor_copy(vt[:, :, n, 0:DH],
                                                     v_bank[:, n * 128:(n + 1) * 128].rearrange("p (h d) -> p h d", d=DH))
                            last.then_inc(e["vt"], 1)
                            v.wait_ge(e["qk"], BASE + b + 1)
                            v.tensor_tensor(rot[:, 0, :], qv[:, 0, :], trig[:, 0, :], ALU.mult)
                            v.tensor_tensor(rot[:, 2, :], qv[:, 0, :], trig[:, 2, :], ALU.mult).then_inc(e["r2"], 1)
                            if more:
                                rows(v, b + 1, pre1, x1n, 1)
                            v.wait_ge(e["r2"], BASE + b + 1)
                            v.wait_ge(e["r1"], BASE + b + 1)
                            v.tensor_tensor(full[:, 2, :], rot[:, 0, :], rot[:, 1, :], ALU.add)
                            v.tensor_tensor(full[:, 3, :], rot[:, 2, :], rot[:, 3, :], ALU.add).then_inc(e["rot"], 1)
                            if more:
                                token_mix(b + 1)
                            v.wait_ge(e["hi"], BASE + b + 1)
                            flat = full[:, :, :].rearrange("p a t -> p (a t)")
                            lf = left[:, :, :].rearrange("p a t -> p (a t)")
                            v.tensor_tensor(lf, flat, part[:, 0, 0:4 * T], ALU.subtract).then_inc(e["left"], 1)
                            if more:
                                relu(b + 1)
                            v.wait_ge(e["left"], BASE + b + 1)
                            v.tensor_copy(part[:, 1, 0:4 * T], lf).then_inc(e["mid"], 1)
                            v.wait_ge(e["mid"], BASE + b + 1)
                            v.tensor_tensor(part[:, 2, 0:4 * T], lf, part[:, 1, 0:4 * T], ALU.subtract).then_inc(e["lo"], 1)
                            if more:
                                residual2(b + 1)
                                rows2(b + 1)

                        def step1(b, more, load):
                            for m in range(KH):
                                v.wait_ge(e["w2_mm"], BASE + KH * b + m + 1)
                                v.wait_ge(e["silu"], BASE + KH * b + m + 1)
                                v.scalar_tensor_tensor(out=ha[:, m, :], in0=bank[4 + m][:, :], scalar=fs[:, 1, m:m + 1],
                                                       in1=silu[:, m, :], op0=ALU.mult, op1=ALU.mult).then_inc(e["ha"], 1)
                            if more:
                                normalise(b + 1)
                                residual1(b + 1)
                                rows(v, b + 1, pre1, x1n, 1)
                            residual2(b)
                            if more:
                                keep_rows1(b + 1)
                            rows2(b)

                        if first:
                            v.memset(xt1[:, 0:1], 0.0).then_inc(fill, 1)
                            v.memset(vt[:, :, :, DH:VC], 1.0).then_inc(fill, 1)
                            for i in range(3):
                                v.memset(part[:, i, 4 * T:4 * T + 2], 0.0).then_inc(fill, 1)
                            v.wait_ge(fill, BASE + 5)
                        v.wait_ge(c_in, BASE + 16 * N_FIRST)
                        normalise(0)
                        residual1(0)
                        rows(v, 0, pre1, x1n, 1)
                        v.wait_ge(late_in, BASE + 16 * (len(loads) - N_FIRST))
                        keep_rows1(0)
                        if first:
                            token_mix(0)
                            relu(0)
                            residual2(0)
                            rows2(0)
                        steps(v, step0 if first else step1)

        tables_phase()
        end_phase()
        attention_phase(0)
        end_phase()
        dense_phase(0)
        end_phase()
        attention_phase(1)
        end_phase()
        dense_phase(1)


def _tables(np):
    k = np.arange(T, dtype=np.float64)
    freq = (1.0 / np.float32(10000.0) ** (np.arange(0, DH, 2, dtype=np.float32) / np.float32(DH))).astype(np.float64)
    sin, cos = (lambda p: np.sin(p[None, :] * freq[:, None])), (lambda p: np.cos(p[None, :] * freq[:, None]))
    own = [np.concatenate([sin(p), sin(p)]) for p in (k, k + T)]
    swap = [np.concatenate([cos(p), -cos(p)]) for p in (k, k + T)]
    trig = np.stack([own[0], swap[0], own[1], swap[1]], 1)
    key = np.concatenate([cos(k), sin(k)]).astype(np.float32)
    bits = []
    left = key.copy()
    for _ in range(3):
        u = left.view(np.uint32)
        r = ((u + np.uint32(0x7FFF) + ((u >> 16) & 1)) >> 16).astype(np.uint32)
        bits.append(r.astype(np.uint16))
        left = left - (r << 16).astype(np.uint32).view(np.float32)
    p, c = np.arange(128)[:, None], np.arange(128)[None, :]
    block = -(np.arange(C)[:, None] // DH == np.arange(H)[None, :]).astype(np.float32)
    return {
        "ident": np.eye(128, dtype=np.float32), "mask0": (c >= p).astype(np.uint32), "mask1": (c >= p + 2).astype(np.uint32),
        "negblock": block, "trig": np.ascontiguousarray(np.tile(trig, (H, 1, 1)).astype(np.float32)),
        "poskey": np.concatenate([bits[i] for i in K_PART]),
    }


def kernel(**inputs):
    import numpy as np
    import concourse.bacc as bacc
    from concourse.bass_utils import run_bass_kernel_spmd

    a = {n: np.asarray(v) for n, v in inputs.items()}
    L0, F0, L1, F1 = "L0_attn_", "L0_ffn_", "L1_attn_", "L1_ffn_"
    swap = (np.arange(C) // DH) * DH + (np.arange(C) + DH // 2) % DH

    def tr(x):
        return np.ascontiguousarray(x.T)

    def col(x):
        return np.ascontiguousarray(x.reshape(C, 1))

    arrays = {
        "x": a[L0 + "x"], "xT": np.ascontiguousarray(a[L0 + "x"].transpose(0, 2, 1)),
        "WqT": tr(a[L0 + "Wq"]), "WkT": tr(a[L0 + "Wk"]), "WvT": tr(a[L0 + "Wv"]), "WoT": tr(a[L0 + "Wo"]),
        "WpkT": tr(a[L0 + "Wpk"]), "WpqT": tr(a[L0 + "Wpq"]), "relT": tr(a[L0 + "rel_emb"]),
        "bq": col(a[L0 + "bq"]), "bk": col(a[L0 + "bk"]), "bpk": col(a[L0 + "bpk"]), "bpq": col(a[L0 + "bpq"]),
        "bv": a[L0 + "bv"], "bo": a[L0 + "bo"],
        "W_rT": tr(a[F0 + "W_r"]), "W_kT": tr(a[F0 + "W_k"]), "W_vT": tr(a[F0 + "W_v"]),
        "mu": np.ascontiguousarray(np.stack([a[F0 + "mu_r"], a[F0 + "mu_k"]], 1)),
        "Wq": a[L1 + "Wq"], "Wq_swap": np.ascontiguousarray(a[L1 + "Wq"][:, swap]), "Wk": a[L1 + "Wk"], "Wv": a[L1 + "Wv"],
        "Wo": a[L1 + "Wo"], "bo1": a[L1 + "bo"],
        "uv": np.ascontiguousarray(np.stack([a[L1 + "u"].reshape(C), a[L1 + "v"].reshape(C), a[L1 + "v"].reshape(C)[swap]], 1)),
        "w1T": tr(a[F1 + "w1_w"]), "w2T": tr(a[F1 + "w2_w"]), "h1T": tr(a[F1 + "h1_w"]), "h2T": tr(a[F1 + "h2_w"]),
        "w3T": tr(a[F1 + "w3_w"]), "w3_s": a[F1 + "w3_s"],
        "hid_s": np.ascontiguousarray(np.stack([a[F1 + n].reshape(KH, 128) for n in ("w1_s", "w2_s", "h1_s", "h2_s")], 0)
                                      .transpose(2, 0, 1)),
    }
    arrays.update(_tables(np))
    nc = bacc.Bacc("TRN2", target_bir_lowering=False, num_devices=1)
    t = {}
    for n, v in arrays.items():
        dt = BF16 if n == "poskey" else mybir.dt.from_np(v.dtype)
        if n == "poskey":
            t[n] = nc.dram_tensor("in_" + n, v.shape, mybir.dt.uint16, kind="ExternalInput").ap().bitcast(BF16)
        else:
            t[n] = nc.dram_tensor("in_" + n, v.shape, dt, kind="ExternalInput").ap()
    t["out"] = nc.dram_tensor("out_0", (B, T, C), F32, kind="ExternalOutput").ap()
    build(nc, t)
    r = run_bass_kernel_spmd(nc, [{"in_" + n: v for n, v in arrays.items()}], core_ids=[0])
    return r.results[0]["out_0"]
```
